# Optimizing a Trainium2 kernel written in Bass

```python
import numpy as np
import jax
import jax.numpy as jnp

def _softmax(x, axis=-1):
    return jax.nn.softmax(x, axis=axis)

def _gelu(x):
    return jax.nn.gelu(x, approximate=True)

def _silu(x):
    return jax.nn.silu(x)

def _sigmoid(x):
    return jax.nn.sigmoid(x)

def _layernorm(x, axis=-1, eps=1e-05):
    m = jnp.mean(x, axis=axis, keepdims=True)
    v = jnp.var(x, axis=axis, keepdims=True)
    return (x - m) / jnp.sqrt(v + eps)

def _scatter_add(tgt, idx, src, axis=0):
    return tgt.at[idx].add(src)

def _segment_sum(src, seg, n):
    return jax.ops.segment_sum(src, seg, n)
kernel_name = 'mk_vit_tower_cls_d2_tok_img256_r4_fe7856'

def setup_inputs(seed: int=0):
    np.random.seed(seed)
    _w = jnp.asarray

    def _rec_inputs():
        import jax
        import jax.numpy as jnp
        _rk = jax.random.key(seed)
        x = 7.22013e-05 + 1.00017 * jax.random.normal(jax.random.fold_in(_rk, 1), (4, 1, 1024, 64), jnp.float32)
        cls_tok = 0.02 * jax.random.normal(jax.random.fold_in(_rk, 5), (1, 1, 64), jnp.float32)
        return (x, cls_tok)
    x, cls_tok = _rec_inputs()

    def _L0_tok_setup():
        import jax, jax.numpy as jnp
        import numpy as np
        T, D_IN, D_INT, D_OUT, B = (1024, 64, 64, 64, 8)
        key = jax.random.key(seed)
        ks = jax.random.split(key, 12)
        s_in = 1.0 / np.sqrt(D_IN)
        s_int = 1.0 / np.sqrt(D_INT)
        return {'x_batched': jax.random.normal(ks[0], (B, 1, T, D_IN), dtype=jnp.float32), 'd_gamma_batched': jax.random.uniform(ks[1], (T, T), dtype=jnp.float32), 'Wq': jax.random.uniform(ks[2], (D_IN, D_INT), jnp.float32, -s_in, s_in), 'bq': jax.random.uniform(ks[3], (D_INT,), jnp.float32, -s_in, s_in), 'Wk': jax.random.uniform(ks[4], (D_IN, D_INT), jnp.float32, -s_in, s_in), 'bk': jax.random.uniform(ks[5], (D_INT,), jnp.float32, -s_in, s_in), 'Wv': jax.random.uniform(ks[6], (D_IN, D_INT), jnp.float32, -s_in, s_in), 'bv': jax.random.uniform(ks[7], (D_INT,), jnp.float32, -s_in, s_in), 'Wo': jax.random.uniform(ks[8], (D_INT, D_OUT), jnp.float32, -s_int, s_int), 'bo': jax.random.uniform(ks[9], (D_OUT,), jnp.float32, -s_int, s_int), 'prelu_a': jnp.float32(0.25)}
    _L0_tok_all = _L0_tok_setup()
    _L0_tok_in = {k: v for k, v in _L0_tok_all.items() if k in ('d_gamma_batched', 'Wq', 'bq', 'Wk', 'bk', 'Wv', 'bv', 'Wo', 'bo', 'prelu_a')}
    del _L0_tok_all

    def _L0_attn_setup():
        import jax, jax.numpy as jnp
        import numpy as np
        N, T, C = (2, 1024, 64)
        H = 4
        HD = C // H
        WIN = 64
        LEFT = WIN - 1 - WIN // 2
        SCALE = HD ** (-0.5)
        MASK_VAL = -100.0
        key = jax.random.key(seed)
        k0, k1, k2, k3 = jax.random.split(key, 4)
        x = jax.random.normal(k0, (N, T, C), dtype=jnp.float32)
        W_qkv = jax.random.normal(k1, (C, 3 * C), dtype=jnp.float32) * 0.02
        b_qkv = jnp.zeros((3 * C,), dtype=jnp.float32)
        rel_bias = jax.random.normal(k2, (1, H, 1, WIN), dtype=jnp.float32) * 0.02
        W_proj = jax.random.normal(k3, (C, C), dtype=jnp.float32) * 0.02
        b_proj = jnp.zeros((C,), dtype=jnp.float32)
        return {'x': x, 'W_qkv': W_qkv, 'b_qkv': b_qkv, 'rel_bias': rel_bias, 'W_proj': W_proj, 'b_proj': b_proj}
    _L0_attn_all = _L0_attn_setup()
    _L0_attn_in = {k: v for k, v in _L0_attn_all.items() if k in ('W_qkv', 'b_qkv', 'rel_bias', 'W_proj', 'b_proj')}
    del _L0_attn_all

    def _L0_ffn_setup():
        import jax, jax.numpy as jnp
        import numpy as np
        DIM = 64
        HEADS = 8
        NUM_KEYS = 64
        NUM_KV = NUM_KEYS ** 2
        PK_TOPK = 16
        FINAL_TOPK = 16
        DIM_KEY = DIM // 2
        P = 2

        def _pk(x, Wq_pk, pk_keys):
            b, n, _ = x.shape
            q = (x @ Wq_pk).reshape(b, n, P, HEADS, DIM_KEY).transpose(2, 0, 1, 3, 4)
            sim = jnp.einsum('pbnhd,pkhd->pbnhk', q, pk_keys)
            scores, idx = jax.lax.top_k(sim, PK_TOPK)
            idx0 = idx[0]
            idx1 = idx[1] * NUM_KEYS
            index = (idx0[..., :, None] + idx1[..., None, :]).reshape(b, n, HEADS, PK_TOPK * PK_TOPK)
            score = (scores[0][..., :, None] + scores[1][..., None, :]).reshape(b, n, HEADS, PK_TOPK * PK_TOPK)
            final_scores, pk_idx = jax.lax.top_k(score, FINAL_TOPK)
            final_indices = jnp.take_along_axis(index, pk_idx, axis=-1)
            final_scores = jax.nn.softmax(final_scores, axis=-1)
            return (final_scores, final_indices)
        key = jax.random.key(seed)
        ks = jax.random.split(key, 7)
        b, n = (2, 256)
        std = 0.02
        x = jax.random.normal(ks[0], (b, n, DIM), dtype=jnp.float32)
        Wq_pk = jax.random.normal(ks[1], (DIM, P * HEADS * DIM_KEY), dtype=jnp.float32) * std
        pk_keys = jax.random.normal(ks[2], (P, NUM_KEYS, HEADS, DIM_KEY), dtype=jnp.float32) * std
        Wq = jax.random.normal(ks[3], (DIM, HEADS * DIM), dtype=jnp.float32) * std
        keys_table = jax.random.normal(ks[4], (NUM_KV * HEADS, DIM), dtype=jnp.float32) * std
        values_table = jax.random.normal(ks[5], (NUM_KV * HEADS, DIM), dtype=jnp.float32) * std
        Wo = jax.random.normal(ks[6], (DIM * HEADS, DIM), dtype=jnp.float32) * std
        return {'x': x, 'Wq_pk': Wq_pk, 'pk_keys': pk_keys, 'Wq': Wq, 'keys_table': keys_table, 'values_table': values_table, 'Wo': Wo}
    _L0_ffn_all = _L0_ffn_setup()
    _L0_ffn_in = {k: v for k, v in _L0_ffn_all.items() if k in ('Wq_pk', 'pk_keys', 'Wq', 'keys_table', 'values_table', 'Wo')}
    del _L0_ffn_all

    def _L1_attn_setup():
        import jax, jax.numpy as jnp
        import numpy as np
        D_MODEL = 64
        N_HEADS = 8
        HEAD_DIM = D_MODEL // N_HEADS
        SCALE = HEAD_DIM ** (-0.5)
        key = jax.random.key(seed)
        ks = jax.random.split(key, 9)
        B, N = (2, 1024)
        init = 1.0 / np.sqrt(D_MODEL)

        def lin(kw, kb):
            W = jax.random.uniform(kw, (D_MODEL, D_MODEL), jnp.float32, -init, init)
            b = jax.random.uniform(kb, (D_MODEL,), jnp.float32, -init, init)
            return (W, b)
        Wq, bq = lin(ks[0], ks[1])
        Wk, bk = lin(ks[2], ks[3])
        Wv, bv = lin(ks[4], ks[5])
        Wo, bo = lin(ks[6], ks[7])
        x = jax.random.normal(ks[8], (B, N, D_MODEL), jnp.float32)
        return {'x': x, 'Wq': Wq, 'bq': bq, 'Wk': Wk, 'bk': bk, 'Wv': Wv, 'bv': bv, 'Wo': Wo, 'bo': bo}
    _L1_attn_all = _L1_attn_setup()
    _L1_attn_in = {k: v for k, v in _L1_attn_all.items() if k in ('Wq', 'bq', 'Wk', 'bk', 'Wv', 'bv', 'Wo', 'bo')}
    del _L1_attn_all

    def _L1_ffn_setup():
        import jax, jax.numpy as jnp
        import numpy as np
        B, N, D = (16, 1024, 64)
        NUM_EXPERTS, TOP_K, HEADS = (4, 2, 4)
        N_EDGES = 262144
        LN_EPS = 1e-05

        def _layernorm(x, g, b):
            mu = x.mean(-1, keepdims=True)
            var = ((x - mu) ** 2).mean(-1, keepdims=True)
            return (x - mu) * jax.lax.rsqrt(var + LN_EPS) * g + b

        def _forward(x, edge_index, W_gat, att_src, att_dst, b_gat, ln_gamma, ln_beta, W1, b1, W2, b2):
            Bc, Nc, Dc = x.shape
            M = Bc * Nc
            x_flat = x.reshape(M, Dc)
            h = (x_flat @ W_gat).reshape(M, HEADS, NUM_EXPERTS)
            loops = jnp.arange(M, dtype=edge_index.dtype)
            src = jnp.concatenate([edge_index[0], loops])
            dst = jnp.concatenate([edge_index[1], loops])
            a_src = (h * att_src).sum(-1)
            a_dst = (h * att_dst).sum(-1)
            e = jax.nn.leaky_relu(a_src[src] + a_dst[dst], negative_slope=0.2)
            e_max = jax.ops.segment_max(e, dst, num_segments=M)
            ee = jnp.exp(e - e_max[dst])
            denom = jax.ops.segment_sum(ee, dst, num_segments=M)
            alpha = ee / (denom[dst] + 1e-16)
            msg = h[src] * alpha[:, :, None]
            agg = jax.ops.segment_sum(msg, dst, num_segments=M).reshape(M, HEADS * NUM_EXPERTS) + b_gat
            scores = _layernorm(agg, ln_gamma, ln_beta).reshape(M, HEADS, NUM_EXPERTS).mean(1)
            scores = scores.reshape(Bc, Nc, NUM_EXPERTS)
            topk_s, topk_i = jax.lax.top_k(scores, TOP_K)
            w = jax.nn.softmax(topk_s, axis=-1)
            out = jnp.zeros_like(x)
            for ei in range(NUM_EXPERTS):
                g = jnp.where(topk_i == ei, w, 0.0).sum(-1)
                hh = jax.nn.gelu(x @ W1[ei] + b1[ei], approximate=False)
                out = out + g[..., None] * (hh @ W2[ei] + b2[ei])
            return out
        key = jax.random.key(seed)
        ks = jax.random.split(key, 8)
        s = 0.05
        return {'x': jax.random.normal(ks[0], (B, N, D), jnp.float32), 'W_gat': jax.random.normal(ks[1], (D, HEADS * NUM_EXPERTS), jnp.float32) * s, 'att_src': jax.random.normal(ks[2], (HEADS, NUM_EXPERTS), jnp.float32) * s, 'att_dst': jax.random.normal(ks[3], (HEADS, NUM_EXPERTS), jnp.float32) * s, 'b_gat': jnp.zeros((HEADS * NUM_EXPERTS,), jnp.float32), 'ln_gamma': jnp.ones((HEADS * NUM_EXPERTS,), jnp.float32), 'ln_beta': jnp.zeros((HEADS * NUM_EXPERTS,), jnp.float32), 'W1': jax.random.normal(ks[4], (NUM_EXPERTS, D, 2 * D), jnp.float32) * s, 'b1': jnp.zeros((NUM_EXPERTS, 2 * D), jnp.float32), 'W2': jax.random.normal(ks[5], (NUM_EXPERTS, 2 * D, D), jnp.float32) * s, 'b2': jnp.zeros((NUM_EXPERTS, D), jnp.float32), 'edge_index': jax.random.randint(ks[6], (2, N_EDGES), 0, B * N, jnp.int32)}
    _L1_ffn_all = _L1_ffn_setup()
    _L1_ffn_in = {k: v for k, v in _L1_ffn_all.items() if k in ('W_gat', 'att_src', 'att_dst', 'b_gat', 'ln_gamma', 'ln_beta', 'W1', 'b1', 'W2', 'b2', 'edge_index')}
    del _L1_ffn_all
    return {'x': x, 'cls_tok': cls_tok, 'L0_tok_d_gamma_batched': _L0_tok_in['d_gamma_batched'], 'L0_tok_Wq': _L0_tok_in['Wq'], 'L0_tok_bq': _L0_tok_in['bq'], 'L0_tok_Wk': _L0_tok_in['Wk'], 'L0_tok_bk': _L0_tok_in['bk'], 'L0_tok_Wv': _L0_tok_in['Wv'], 'L0_tok_bv': _L0_tok_in['bv'], 'L0_tok_Wo': _L0_tok_in['Wo'], 'L0_tok_bo': _L0_tok_in['bo'], 'L0_tok_prelu_a': _L0_tok_in['prelu_a'], 'L0_attn_W_qkv': _L0_attn_in['W_qkv'], 'L0_attn_b_qkv': _L0_attn_in['b_qkv'], 'L0_attn_rel_bias': _L0_attn_in['rel_bias'], 'L0_attn_W_proj': _L0_attn_in['W_proj'], 'L0_attn_b_proj': _L0_attn_in['b_proj'], 'L0_ffn_Wq_pk': _L0_ffn_in['Wq_pk'], 'L0_ffn_pk_keys': _L0_ffn_in['pk_keys'], 'L0_ffn_Wq': _L0_ffn_in['Wq'], 'L0_ffn_keys_table': _L0_ffn_in['keys_table'], 'L0_ffn_values_table': _L0_ffn_in['values_table'], 'L0_ffn_Wo': _L0_ffn_in['Wo'], 'L1_attn_Wq': _L1_attn_in['Wq'], 'L1_attn_bq': _L1_attn_in['bq'], 'L1_attn_Wk': _L1_attn_in['Wk'], 'L1_attn_bk': _L1_attn_in['bk'], 'L1_attn_Wv': _L1_attn_in['Wv'], 'L1_attn_bv': _L1_attn_in['bv'], 'L1_attn_Wo': _L1_attn_in['Wo'], 'L1_attn_bo': _L1_attn_in['bo'], 'L1_ffn_W_gat': _L1_ffn_in['W_gat'], 'L1_ffn_att_src': _L1_ffn_in['att_src'], 'L1_ffn_att_dst': _L1_ffn_in['att_dst'], 'L1_ffn_b_gat': _L1_ffn_in['b_gat'], 'L1_ffn_ln_gamma': _L1_ffn_in['ln_gamma'], 'L1_ffn_ln_beta': _L1_ffn_in['ln_beta'], 'L1_ffn_W1': _L1_ffn_in['W1'], 'L1_ffn_b1': _L1_ffn_in['b1'], 'L1_ffn_W2': _L1_ffn_in['W2'], 'L1_ffn_b2': _L1_ffn_in['b2'], 'L1_ffn_edge_index': _L1_ffn_in['edge_index']}

def reference(x, cls_tok, L0_tok_d_gamma_batched, L0_tok_Wq, L0_tok_bq, L0_tok_Wk, L0_tok_bk, L0_tok_Wv, L0_tok_bv, L0_tok_Wo, L0_tok_bo, L0_tok_prelu_a, L0_attn_W_qkv, L0_attn_b_qkv, L0_attn_rel_bias, L0_attn_W_proj, L0_attn_b_proj, L0_ffn_Wq_pk, L0_ffn_pk_keys, L0_ffn_Wq, L0_ffn_keys_table, L0_ffn_values_table, L0_ffn_Wo, L1_attn_Wq, L1_attn_bq, L1_attn_Wk, L1_attn_bk, L1_attn_Wv, L1_attn_bv, L1_attn_Wo, L1_attn_bo, L1_ffn_W_gat, L1_ffn_att_src, L1_ffn_att_dst, L1_ffn_b_gat, L1_ffn_ln_gamma, L1_ffn_ln_beta, L1_ffn_W1, L1_ffn_b1, L1_ffn_W2, L1_ffn_b2, L1_ffn_edge_index):
    import jax
    import jax.numpy as jnp

    def _L0_tok_ref(x_batched, d_gamma_batched, Wq, bq, Wk, bk, Wv, bv, Wo, bo, prelu_a):
        import jax, jax.numpy as jnp
        import numpy as np
        T, D_IN, D_INT, D_OUT, B = (1024, 64, 64, 64, 8)
        x = x_batched.reshape(x_batched.shape[0], T, D_IN)
        q = x @ Wq + bq
        k = x @ Wk + bk
        v = x @ Wv + bv
        scores = jnp.einsum('btd,bsd->bts', q, k)
        retained = jnp.einsum('bts,bsd->btd', d_gamma_batched * scores, v)
        y = retained @ Wo + bo
        out = jnp.where(y >= 0, y, prelu_a * y)
        return out

    def _L0_attn_ref(x, W_qkv, b_qkv, rel_bias, W_proj, b_proj):
        import jax, jax.numpy as jnp
        import numpy as np
        N, T, C = (2, 1024, 64)
        H = 4
        HD = C // H
        WIN = 64
        LEFT = WIN - 1 - WIN // 2
        SCALE = HD ** (-0.5)
        MASK_VAL = -100.0
        n, t, c = x.shape
        qkv = (x @ W_qkv + b_qkv).reshape(n, t, 3, H, HD)
        q, k, v = (qkv[:, :, 0], qkv[:, :, 1], qkv[:, :, 2])
        idx = jnp.arange(t)[:, None] + jnp.arange(WIN)[None, :] - LEFT
        valid = (idx >= 0) & (idx < t)
        idx_c = jnp.clip(idx, 0, t - 1)
        kw = k[:, idx_c]
        vw = v[:, idx_c]
        attn = jnp.einsum('nthd,ntwhd->nhtw', q * SCALE, kw)
        attn = attn + rel_bias
        attn = attn + jnp.where(valid, 0.0, MASK_VAL)[None, None]
        attn = jax.nn.softmax(attn, axis=-1)
        out = jnp.einsum('nhtw,ntwhd->nthd', attn, vw).reshape(n, t, c)
        return out @ W_proj + b_proj

    def _L0_ffn_ref(x, Wq_pk, pk_keys, Wq, keys_table, values_table, Wo):
        import jax, jax.numpy as jnp
        import numpy as np
        DIM = 64
        HEADS = 8
        NUM_KEYS = 64
        NUM_KV = NUM_KEYS ** 2
        PK_TOPK = 16
        FINAL_TOPK = 16
        DIM_KEY = DIM // 2
        P = 2

        def _pk(x, Wq_pk, pk_keys):
            b, n, _ = x.shape
            q = (x @ Wq_pk).reshape(b, n, P, HEADS, DIM_KEY).transpose(2, 0, 1, 3, 4)
            sim = jnp.einsum('pbnhd,pkhd->pbnhk', q, pk_keys)
            scores, idx = jax.lax.top_k(sim, PK_TOPK)
            idx0 = idx[0]
            idx1 = idx[1] * NUM_KEYS
            index = (idx0[..., :, None] + idx1[..., None, :]).reshape(b, n, HEADS, PK_TOPK * PK_TOPK)
            score = (scores[0][..., :, None] + scores[1][..., None, :]).reshape(b, n, HEADS, PK_TOPK * PK_TOPK)
            final_scores, pk_idx = jax.lax.top_k(score, FINAL_TOPK)
            final_indices = jnp.take_along_axis(index, pk_idx, axis=-1)
            final_scores = jax.nn.softmax(final_scores, axis=-1)
            return (final_scores, final_indices)
        b, n, d = x.shape
        q = (x @ Wq).reshape(b, n, HEADS, DIM) * DIM ** (-0.5)
        kv_scores, indices = _pk(x, Wq_pk, pk_keys)
        offsets = jnp.arange(HEADS, dtype=indices.dtype) * NUM_KV
        ind = indices + offsets[None, None, :, None]
        k = jnp.einsum('bnhk,bnhkd->bnhd', kv_scores, keys_table[ind])
        v = jnp.einsum('bnhk,bnhkd->bnhd', kv_scores, values_table[ind])
        sim = jnp.einsum('bihd,bjhd->bhij', q, k)
        neg = -jnp.finfo(sim.dtype).max
        causal = jnp.tril(jnp.ones((n, n), dtype=bool))
        sim = jnp.where(causal, sim, neg)
        attn = jax.nn.softmax(sim, axis=-1)
        out = jnp.einsum('bhij,bjhd->bhid', attn, v)
        out = out.transpose(0, 2, 1, 3).reshape(b, n, HEADS * DIM)
        return out @ Wo

    def _L1_attn_ref(x, Wq, bq, Wk, bk, Wv, bv, Wo, bo):
        import jax, jax.numpy as jnp
        import numpy as np
        D_MODEL = 64
        N_HEADS = 8
        HEAD_DIM = D_MODEL // N_HEADS
        SCALE = HEAD_DIM ** (-0.5)
        B, N, C = x.shape
        q = x @ Wq.T + bq
        k = x @ Wk.T + bk
        v = x @ Wv.T + bv
        q = q.reshape(B, N, N_HEADS, HEAD_DIM).transpose(0, 2, 1, 3)
        k = k.reshape(B, N, N_HEADS, HEAD_DIM).transpose(0, 2, 1, 3)
        v = v.reshape(B, N, N_HEADS, HEAD_DIM).transpose(0, 2, 1, 3)
        scores = jnp.einsum('bhnd,bhmd->bhnm', q, k) * SCALE
        attn = jax.nn.softmax(scores, axis=-1)
        out = jnp.einsum('bhnm,bhmd->bhnd', attn, v)
        out = out.transpose(0, 2, 1, 3).reshape(B, N, C)
        return out @ Wo.T + bo

    def _L1_ffn_ref(x, W_gat, att_src, att_dst, b_gat, ln_gamma, ln_beta, W1, b1, W2, b2, edge_index):
        import jax, jax.numpy as jnp
        import numpy as np
        B, N, D = (16, 1024, 64)
        NUM_EXPERTS, TOP_K, HEADS = (4, 2, 4)
        N_EDGES = 262144
        LN_EPS = 1e-05

        def _layernorm(x, g, b):
            mu = x.mean(-1, keepdims=True)
            var = ((x - mu) ** 2).mean(-1, keepdims=True)
            return (x - mu) * jax.lax.rsqrt(var + LN_EPS) * g + b

        def _forward(x, edge_index, W_gat, att_src, att_dst, b_gat, ln_gamma, ln_beta, W1, b1, W2, b2):
            Bc, Nc, Dc = x.shape
            M = Bc * Nc
            x_flat = x.reshape(M, Dc)
            h = (x_flat @ W_gat).reshape(M, HEADS, NUM_EXPERTS)
            loops = jnp.arange(M, dtype=edge_index.dtype)
            src = jnp.concatenate([edge_index[0], loops])
            dst = jnp.concatenate([edge_index[1], loops])
            a_src = (h * att_src).sum(-1)
            a_dst = (h * att_dst).sum(-1)
            e = jax.nn.leaky_relu(a_src[src] + a_dst[dst], negative_slope=0.2)
            e_max = jax.ops.segment_max(e, dst, num_segments=M)
            ee = jnp.exp(e - e_max[dst])
            denom = jax.ops.segment_sum(ee, dst, num_segments=M)
            alpha = ee / (denom[dst] + 1e-16)
            msg = h[src] * alpha[:, :, None]
            agg = jax.ops.segment_sum(msg, dst, num_segments=M).reshape(M, HEADS * NUM_EXPERTS) + b_gat
            scores = _layernorm(agg, ln_gamma, ln_beta).reshape(M, HEADS, NUM_EXPERTS).mean(1)
            scores = scores.reshape(Bc, Nc, NUM_EXPERTS)
            topk_s, topk_i = jax.lax.top_k(scores, TOP_K)
            w = jax.nn.softmax(topk_s, axis=-1)
            out = jnp.zeros_like(x)
            for ei in range(NUM_EXPERTS):
                g = jnp.where(topk_i == ei, w, 0.0).sum(-1)
                hh = jax.nn.gelu(x @ W1[ei] + b1[ei], approximate=False)
                out = out + g[..., None] * (hh @ W2[ei] + b2[ei])
            return out
        return _forward(x, edge_index, W_gat, att_src, att_dst, b_gat, ln_gamma, ln_beta, W1, b1, W2, b2)
    h = _L0_tok_ref(x, L0_tok_d_gamma_batched, L0_tok_Wq, L0_tok_bq, L0_tok_Wk, L0_tok_bk, L0_tok_Wv, L0_tok_bv, L0_tok_Wo, L0_tok_bo, L0_tok_prelu_a)
    h = jnp.concatenate([jnp.broadcast_to(cls_tok, (h.shape[0], 1, h.shape[2])), h], axis=1)
    h = h + _L0_attn_ref(_layernorm(h, axis=-1), L0_attn_W_qkv, L0_attn_b_qkv, L0_attn_rel_bias, L0_attn_W_proj, L0_attn_b_proj)
    h = h + _L0_ffn_ref(_layernorm(h, axis=-1), L0_ffn_Wq_pk, L0_ffn_pk_keys, L0_ffn_Wq, L0_ffn_keys_table, L0_ffn_values_table, L0_ffn_Wo)
    h = h + _L1_attn_ref(_layernorm(h, axis=-1), L1_attn_Wq, L1_attn_bq, L1_attn_Wk, L1_attn_bk, L1_attn_Wv, L1_attn_bv, L1_attn_Wo, L1_attn_bo)
    h = h + _L1_ffn_ref(_layernorm(h, axis=-1), L1_ffn_W_gat, L1_ffn_att_src, L1_ffn_att_dst, L1_ffn_b_gat, L1_ffn_ln_gamma, L1_ffn_ln_beta, L1_ffn_W1, L1_ffn_b1, L1_ffn_W2, L1_ffn_b2, L1_ffn_edge_index)
    return h

_drawn_inputs = setup_inputs


def setup_inputs(seed=0):
    import zlib

    import numpy as np

    out = dict(_drawn_inputs(seed))
    spreads = {'L0_attn_b_qkv': (0.0, 0.8),
     'L0_attn_b_proj': (0.0, 0.8),
     'L1_ffn_b_gat': (0.0, 0.8),
     'L1_ffn_ln_gamma': (1.0, 0.6),
     'L1_ffn_ln_beta': (0.0, 0.8),
     'L1_ffn_b1': (0.0, 0.8),
     'L1_ffn_b2': (0.0, 2.0)}
    factors = {'cls_tok': 43.93,
     'L0_tok_bo': 8.0,
     'L0_attn_W_qkv': 8.0,
     'L0_attn_rel_bias': 64.0,
     'L0_attn_W_proj': 8.0,
     'L0_ffn_Wq_pk': 64.0,
     'L0_ffn_pk_keys': 64.0,
     'L0_ffn_Wq': 64.0,
     'L0_ffn_keys_table': 64.0,
     'L0_ffn_values_table': 64.0,
     'L0_ffn_Wo': 64.0,
     'L1_attn_Wq': 8.0,
     'L1_attn_bq': 8.0,
     'L1_attn_Wk': 8.0,
     'L1_attn_bk': 64.0,
     'L1_attn_Wv': 8.0,
     'L1_attn_bv': 8.0,
     'L1_attn_Wo': 8.0,
     'L1_attn_bo': 29.55,
     'L1_ffn_W_gat': 8.0,
     'L1_ffn_att_src': 8.0,
     'L1_ffn_att_dst': 8.0,
     'L1_ffn_W1': 8.0,
     'L1_ffn_W2': 8.0}
    for name, (base, spread) in spreads.items():
        noise = np.random.default_rng([zlib.crc32(name.encode()), seed]).standard_normal(out[name].shape)
        drawn = base * np.exp(spread * noise) if base else spread * noise
        out[name] = jnp.asarray(drawn.astype(out[name].dtype))
    for name, factor in factors.items():
        out[name] = (out[name] * factor).astype(out[name].dtype)
    return out
```

```python
import concourse.bass as bass
from concourse import mybir
from contextlib import ExitStack
import numpy as np

F32 = mybir.dt.float32
BF16 = mybir.dt.bfloat16
I32 = mybir.dt.int32
ALU = mybir.AluOpType
ACT = mybir.ActivationFunctionType
AX = mybir.AxisListType

BATCH, TOK, DIM = 4, 1024, 64
SEQ = TOK + 1
TP = 114
TILES = 9
PAD = TP * TILES
UNITS = BATCH * TILES
NODES = BATCH * PAD
AUG = DIM + 1
HALF = 3 * TP
EPS = 1e-5


class Steps:

    def __init__(self, eng, sem, base=0):
        self.eng, self.sem, self.base, self.n = eng, sem, base, 0

    def mark(self, ins):
        self.n += 1
        ins.then_inc(self.sem, 1)

    def settle(self):
        self.eng.wait_ge(self.sem, self.base + self.n)

    def link(self, ins):
        self.mark(ins)
        self.settle()


class Space:

    def __init__(self, nc, ctx, stage):
        self.nc, self.ctx, self.stage = nc, ctx, stage
        self.sems = []
        ctx.callback(self.close)

    def close(self):
        if self.sems:
            self.nc.clear_and_free_semaphores(self.sems)
            self.nc.all_engine_barrier()

    def sb(self, name, shape, dtype=F32):
        return self.ctx.enter_context(self.nc.sbuf_tensor(f"{self.stage}_{name}", shape, dtype))

    def ps(self, name, shape=(128, 1024)):
        return self.ctx.enter_context(self.nc.psum_tensor(f"{self.stage}_{name}", list(shape), F32))

    def sem(self, name):
        handle = self.nc.alloc_semaphore(name=f"{self.stage}_{name}")
        self.sems.append(handle)
        return handle


def bc_free(ap, parts, inner):
    return ap.unsqueeze(2).to_broadcast([parts, ap.shape[1], inner])


def turn(nc, out, in_, identity, after_wait=False):
    if after_wait:
        return nc.tensor.matmul(out, in_, identity, start=True, stop=True)
    return nc.tensor.transpose(out, in_, identity)


def constants_stage(nc, ident, ones):
    with ExitStack() as ctx:
        s = Space(nc, ctx, "const")
        done = s.sem("done")
        block = ctx.enter_context(nc.Block())

        @block.gpsimd
        def _(pool):
            nc.gpsimd.memset(ident[:, :], 0.0).then_inc(done, 1)
            nc.gpsimd.memset(ones[:, :], 1.0).then_inc(done, 1)
            pool.wait_ge(done, 2)
            nc.gpsimd.affine_select(out=ident[:, :], in_=ident[:, :], compare_op=ALU.not_equal,
                                    fill=1.0, base=0, pattern=[[-1, 128]],
                                    channel_multiplier=1).then_inc(done, 1)
            pool.wait_ge(done, 3)


def tok_stage(nc, io, H, ident):
    ST = TOK // 128
    with ExitStack() as ctx:
        s = Space(nc, ctx, "tok")
        gT = s.sb("gammaT", [128, ST, TOK])
        xb = s.sb("x", [128, ST, DIM])
        xT = s.sb("xT", [AUG, TOK])
        qT = s.sb("qT", [DIM, TOK])
        kT = s.sb("kT", [DIM, TOK])
        v = s.sb("v", [128, ST * DIM])
        pT = s.sb("weightedT", [128, 2, TOK])
        retT = s.sb("retainedT", [AUG, PAD])
        neg = s.sb("negative", [TP, TILES * DIM])
        wq, wk, wv, wo = (s.sb(n, [AUG, DIM]) for n in ("wq", "wk", "wv", "wo"))
        slope = s.sb("slope", [TP, 1])
        psA, psB, psC, psD = (s.ps(n) for n in ("psA", "psB", "psC", "psD"))
        w_in, g_in, x_in, init = s.sem("w_in"), s.sem("g_in"), s.sem("x_in"), s.sem("init")
        x_tr, xT_done, qkv_mm, q_done, k_done, v_done = (
            s.sem(n) for n in ("x_tr", "xT_done", "qkv_mm", "q_done", "k_done", "v_done"))
        sc_mm, weighted, ret_mm, ret_done, y_mm = (
            s.sem(n) for n in ("sc_mm", "weighted", "ret_mm", "ret_done", "y_mm"))
        neg_done, h_done, cls_in = s.sem("neg_done"), s.sem("h_done"), s.sem("cls_in")
        block = ctx.enter_context(nc.Block())
        x_dram = io["x"].rearrange("b c (s p) d -> (b c) p s d", p=128)

        @block.sync
        def _(sp):
            sp.dma_start(xb[:, :, :], x_dram[0]).then_inc(x_in, 16)
            for w, n in ((wq, "q"), (wk, "k"), (wv, "v"), (wo, "o")):
                sp.dma_start(w[0:DIM, :], io[f"L0_tok_W{n}"]).then_inc(w_in, 16)
                sp.dma_start(w[DIM:AUG, :], io[f"L0_tok_b{n}"].unsqueeze(0)).then_inc(w_in, 16)
            sp.dma_start(slope[:, :], io["L0_tok_prelu_a"].to_broadcast([TP, 1])).then_inc(w_in, 16)
            sp.dma_start(gT[:, :, :], io["L0_tok_gammaT"].rearrange("(s p) t -> p s t", p=128)).then_inc(g_in, 16)
            with sp.Fori(1, BATCH) as b:
                sp.wait_ge(x_tr, b)
                sp.dma_start(xb[:, :, :], x_dram[bass.ds(b, 1)].rearrange("a p s d -> (a p) s d")).then_inc(x_in, 16)
            sp.wait_ge(h_done, BATCH)
            sp.dma_start(H[0:1, 0:UNITS:TILES, :], io["cls_tok"].to_broadcast([1, BATCH, DIM])).then_inc(cls_in, 16)
            sp.wait_ge(cls_in, 16)

        @block.tensor
        def _(pe):
            pe.wait_ge(w_in, 16 * 9)
            pe.wait_ge(init, 2)
            with pe.Fori(0, BATCH) as b:
                pe.wait_ge(x_in, b * 16 + 16)
                pe.wait_ge(weighted, b * ST)
                for t in range(ST):
                    last = turn(nc, psA[0:DIM, t * 128:(t + 1) * 128], xb[:, t, :], ident[:, :], after_wait=t == 0)
                last.then_inc(x_tr, 1)
                pe.wait_ge(xT_done, b + 1)
                pe.wait_ge(ret_done, b)
                pe.wait_ge(h_done, b)
                for c in range(2):
                    cols = slice(c * 512, (c + 1) * 512)
                    nc.tensor.matmul(psB[0:DIM, cols], wq[:, :], xT[:, cols], start=True, stop=True)
                    nc.tensor.matmul(psC[0:DIM, cols], wk[:, :], xT[:, cols], start=True, stop=True)
                for t in range(ST):
                    last = nc.tensor.matmul(psD[:, t * DIM:(t + 1) * DIM], xT[:, t * 128:(t + 1) * 128], wv[:, :],
                                            start=True, stop=True)
                last.then_inc(qkv_mm, 1)
                pe.wait_ge(q_done, b + 1)
                pe.wait_ge(k_done, b + 1)
                for t in range(ST + 1):
                    if t < ST:
                        if t >= 2:
                            pe.wait_ge(weighted, b * ST + t - 1)
                        for c in range(2):
                            cols = slice(c * 512, (c + 1) * 512)
                            last = nc.tensor.matmul((psA, psB)[t % 2][:, cols], kT[:, t * 128:(t + 1) * 128],
                                                    qT[:, cols], start=True, stop=True)
                        last.then_inc(sc_mm, 1)
                    if t == 0:
                        pe.wait_ge(v_done, b + 1)
                    else:
                        u = t - 1
                        pe.wait_ge(weighted, b * ST + u + 1)
                        for c in range(2):
                            cols = slice(c * 512, (c + 1) * 512)
                            last = nc.tensor.matmul(psC[0:DIM, cols], v[:, u * DIM:(u + 1) * DIM], pT[:, u % 2, cols],
                                                    start=(u == 0), stop=(u == ST - 1))
                        last.then_inc(ret_mm, 1)
                pe.wait_ge(ret_done, b + 1)
                for j in range(TILES):
                    last = nc.tensor.matmul(psD[0:TP, j * DIM:(j + 1) * DIM], retT[:, j * TP:(j + 1) * TP], wo[:, :],
                                            start=True, stop=True)
                last.then_inc(y_mm, 1)

        @block.scalar
        def _(act):
            with act.Fori(0, BATCH) as b:
                act.wait_ge(x_tr, b + 1)
                act.wait_ge(qkv_mm, b)
                nc.scalar.activation(xT[0:DIM, :], psA[0:DIM, :], ACT.Copy).then_inc(xT_done, 1)
                act.wait_ge(qkv_mm, b + 1)
                act.wait_ge(ret_mm, b * ST)
                nc.scalar.activation(v[:, :], psD[:, 0:ST * DIM], ACT.Copy).then_inc(v_done, 1)
                act.wait_ge(ret_mm, b * ST + ST)
                act.wait_ge(y_mm, b)
                nc.scalar.activation(retT[0:DIM, 1:1 + TOK], psC[0:DIM, :], ACT.Copy).then_inc(ret_done, 1)

        @block.vector
        def _(dve):
            nc.vector.memset(xT[DIM:AUG, :], 1.0).then_inc(init, 1)
            nc.vector.memset(retT[DIM:AUG, :], 1.0).then_inc(init, 1)
            nc.vector.memset(retT[0:DIM, 0:1], 0.0).then_inc(init, 1)
            nc.vector.memset(retT[0:DIM, PAD - 1:PAD], 0.0).then_inc(init, 1)
            dve.wait_ge(g_in, 16)
            dve.wait_ge(w_in, 16 * 9)
            with dve.Fori(0, BATCH) as b:
                dve.wait_ge(qkv_mm, b + 1)
                dve.wait_ge(sc_mm, b * ST)
                nc.vector.tensor_copy(qT[:, :], psB[0:DIM, :]).then_inc(q_done, 1)
                nc.vector.tensor_copy(kT[:, :], psC[0:DIM, :]).then_inc(k_done, 1)
                for t in range(ST):
                    dve.wait_ge(sc_mm, b * ST + t + 1)
                    if t >= 2:
                        dve.wait_ge(ret_mm, b * ST + t - 1)
                    nc.vector.tensor_tensor(pT[:, t % 2, :], (psA, psB)[t % 2][:, :], gT[:, t, :],
                                            ALU.mult).then_inc(weighted, 1)
                dve.wait_ge(y_mm, b + 1)
                dve.wait_ge(h_done, b)
                nc.vector.tensor_scalar(neg[:, :], psD[0:TP, 0:TILES * DIM], 0.0, slope[:, 0:1],
                                        ALU.min, ALU.mult).then_inc(neg_done, 1)
                dve.wait_ge(neg_done, b + 1)
                nc.vector.scalar_tensor_tensor(
                    H[:, bass.ds(b * TILES, TILES), :].rearrange("p t d -> p (t d)"), psD[0:TP, 0:TILES * DIM], 0.0,
                    neg[:, :], ALU.max, ALU.add).then_inc(h_done, 1)


def norm_stage(nc, name, H, xT, ident):
    with ExitStack() as ctx:
        s = Space(nc, ctx, name)
        stat = s.sb("stat", [TP, UNITS])
        rstd = s.sb("rstd", [TP, UNITS])
        root = s.sb("root", [TP, UNITS])
        xc = s.sb("centred", [TP, UNITS, DIM])
        sq = s.sb("square", [TP, UNITS, DIM])
        xn = s.sb("normed", [TP, 2, TILES, DIM])
        ps = [s.ps(f"ps{k}", (128, 3, 512)) for k in range(2)]
        step, var_done, root_done = s.sem("step"), s.sem("var_done"), s.sem("root_done")
        normed, turned, copied = s.sem("normed"), s.sem("turned"), s.sem("copied")
        block = ctx.enter_context(nc.Block())

        @block.vector
        def _(dve):
            st = Steps(dve, step)
            st.mark(nc.vector.memset(xT[DIM:AUG, :, :], 1.0))
            st.link(nc.vector.tensor_reduce(stat[:, :], H[:, :, :], op=ALU.add, axis=AX.X))
            st.link(nc.vector.tensor_scalar(stat[:, :], stat[:, :], 1.0 / DIM, None, ALU.mult))
            st.link(nc.vector.tensor_tensor(xc[:, :, :], H[:, :, :], bc_free(stat[:, :], TP, DIM), ALU.subtract))
            st.link(nc.vector.tensor_tensor(sq[:, :, :], xc[:, :, :], xc[:, :, :], ALU.mult))
            st.link(nc.vector.tensor_reduce(stat[:, :], sq[:, :, :], op=ALU.add, axis=AX.X))
            nc.vector.tensor_scalar(rstd[:, :], stat[:, :], 1.0 / DIM, EPS, ALU.mult, ALU.add).then_inc(var_done, 1)
            dve.wait_ge(root_done, 1)
            st.link(nc.vector.reciprocal(rstd[:, :], root[:, :]))
            with dve.Fori(0, BATCH // 2) as i:
                for k in range(2):
                    dve.wait_ge(turned, i * 2)
                    nc.vector.tensor_tensor(
                        xn[:, k, :, :], xc[:, bass.ds(i * 2 * TILES + k * TILES, TILES), :],
                        rstd[:, bass.ds(i * 2 * TILES + k * TILES, TILES)].unsqueeze(2).to_broadcast([TP, TILES, DIM]),
                        ALU.mult).then_inc(normed, 1)

        @block.tensor
        def _(pe):
            with pe.Fori(0, BATCH // 2) as i:
                for k in range(2):
                    pe.wait_ge(normed, i * 2 + k + 1)
                    pe.wait_ge(copied, i * 2)
                    for t in range(TILES):
                        last = turn(nc, ps[k][0:DIM, t // 3, t % 3 * TP:(t % 3 + 1) * TP],
                                    xn[:, k, t, :], ident[0:TP, 0:TP], after_wait=t == 0)
                    last.then_inc(turned, 1)

        @block.scalar
        def _(act):
            act.wait_ge(var_done, 1)
            nc.scalar.activation(root[:, :], rstd[:, :], ACT.Sqrt).then_inc(root_done, 1)
            with act.Fori(0, BATCH // 2) as i:
                for k in range(2):
                    act.wait_ge(turned, i * 2 + k + 1)
                    nc.scalar.activation(
                        xT[0:DIM, bass.ds(i * 2 + k, 1), :].rearrange("p b (c n) -> p (b c) n", c=3),
                        ps[k][0:DIM, :, 0:HALF], ACT.Copy).then_inc(copied, 1)
            act.wait_ge(copied, BATCH)


WIN, WH, WHD = 64, 4, 16
LEFT = WIN - 1 - WIN // 2
EXT = PAD + WIN - 1
WSPAN = TP + WIN - 1
FAR = -1e30
MASK_VAL = -100.0


def window_stage(nc, io, H, xT, ident):
    k_rest = WSPAN - 128
    qD = nc.dram_tensor("scratch_win_q", [UNITS, 128, TP], F32).ap()
    kD = nc.dram_tensor("scratch_win_k", [UNITS, 128, WSPAN], F32).ap()
    xD = nc.dram_tensor("scratch_win_x", [UNITS, AUG, WSPAN], F32).ap()
    bD = nc.dram_tensor("scratch_win_bias", [WH, TP * WSPAN], F32).ap()
    bias_ctx = ExitStack()
    sb0 = Space(nc, bias_ctx, "win")
    bias = sb0.sb("bias", [TP, WH, WSPAN])
    wv = sb0.sb("wv", [AUG, DIM])
    wp = sb0.sb("wp", [AUG, DIM])
    with ExitStack() as ctx:
        s = Space(nc, ctx, "winp")
        wq = s.sb("wq", [AUG, 128])
        wk = s.sb("wk", [AUG, 128])
        xE = s.sb("xE", [AUG, EXT])
        qT = s.sb("qT", [128, PAD])
        kT = s.sb("kT", [128, EXT])
        far = s.sb("far", [TP, WH, WSPAN])
        psq, psk = s.ps("psq", (128, 3, 512)), s.ps("psk", (128, 3, 512))
        init, w_in, b_fill, b_in, ext, proj, q_out, k_out = (
            s.sem(n) for n in ("init", "w_in", "b_fill", "b_in", "ext", "proj", "q_out", "k_out"))
        x_st, q_st, k_st = s.sem("x_stored"), s.sem("q_stored"), s.sem("k_stored")
        block = ctx.enter_context(nc.Block())
        w3, b3 = io["L0_attn_W_qkv"], io["L0_attn_b_qkv"].unsqueeze(0)

        @block.vector
        def _(dve):
            nc.vector.memset(wq[:, :], 0.0).then_inc(init, 1)
            nc.vector.memset(wk[:, :], 0.0).then_inc(init, 1)
            nc.vector.memset(far[:, :, :], FAR).then_inc(init, 1)
            dve.wait_ge(init, 3)
            nc.vector.memset(wq[DIM:AUG, :].rearrange("p (h c) -> p h c", h=WH)[:, :, 0:1], 1.0).then_inc(init, 1)
            with dve.Fori(0, BATCH) as b:
                dve.wait_ge(x_st, b * 16)
                dve.wait_ge(proj, b)
                xb = xT[:, bass.ds(b, 1), :].rearrange("p b n -> p (b n)")
                nc.vector.tensor_copy(xE[:, LEFT:LEFT + SEQ], xb[:, 0:SEQ]).then_inc(ext, 1)
                nc.vector.tensor_copy(xE[:, 0:LEFT], xb[:, 0:1].to_broadcast([AUG, LEFT])).then_inc(ext, 1)
                nc.vector.tensor_copy(xE[:, LEFT + SEQ:EXT],
                                      xb[:, SEQ - 1:SEQ].to_broadcast([AUG, EXT - LEFT - SEQ])).then_inc(ext, 1)
                dve.wait_ge(proj, b + 1)
                dve.wait_ge(k_st, b * 16)
                nc.vector.tensor_copy(kT[:, :].rearrange("p (c n) -> p c n", c=3), psk[:, :, 0:EXT // 3]).then_inc(k_out, 1)
                dve.wait_ge(k_out, b * (1 + 2 * WH) + 1)
                for h in range(WH):
                    for cols in (slice(0, LEFT), slice(LEFT + SEQ, EXT)):
                        nc.vector.memset(kT[32 * h:32 * h + 1, cols], MASK_VAL / WHD ** -0.5).then_inc(k_out, 1)

        @block.sync
        def _(sp):
            sp.wait_ge(init, 4)
            for h in range(WH):
                sp.dma_start(wq[0:DIM, 32 * h + 1:32 * h + 1 + WHD], w3[:, h * WHD:(h + 1) * WHD]).then_inc(w_in, 16)
                sp.dma_start(wq[DIM:AUG, 32 * h + 1:32 * h + 1 + WHD], b3[:, h * WHD:(h + 1) * WHD]).then_inc(w_in, 16)
                kc = slice(DIM + h * WHD, DIM + (h + 1) * WHD)
                sp.dma_start(wk[0:DIM, 32 * h + 1:32 * h + 1 + WHD], w3[:, kc]).then_inc(w_in, 16)
                sp.dma_start(wk[DIM:AUG, 32 * h + 1:32 * h + 1 + WHD], b3[:, kc]).then_inc(w_in, 16)
            sp.dma_start(wv[0:DIM, :], w3[:, 2 * DIM:3 * DIM]).then_inc(w_in, 16)
            sp.dma_start(wv[DIM:AUG, :], b3[:, 2 * DIM:3 * DIM]).then_inc(w_in, 16)
            sp.dma_start(wp[0:DIM, :], io["L0_attn_W_proj"]).then_inc(w_in, 16)
            sp.dma_start(wp[DIM:AUG, :], io["L0_attn_b_proj"].unsqueeze(0)).then_inc(w_in, 16)
            sp.dma_start(bD.rearrange("h (p c) -> p h c", p=TP), far[:, :, :]).then_inc(b_fill, 16)
            sp.wait_ge(b_fill, 16)
            diagonal = bass.AP(tensor=bD.tensor, offset=0, ap=[[WSPAN + 1, TP], [TP * WSPAN, WH], [1, WIN]])
            sp.dma_start(diagonal, io["L0_attn_rel_bias"].rearrange("a h b w -> (a b) h w").to_broadcast([TP, WH, WIN]))\
              .then_inc(b_fill, 16)
            sp.wait_ge(b_fill, 32)
            sp.dma_start(bias[:, :, :], bD.rearrange("h (p c) -> p h c", p=TP)).then_inc(b_in, 16)

            def windows(a, parts):
                return bass.AP(tensor=a.tensor, offset=a.offset, ap=[a.ap[0], [TP, TILES], [1, WSPAN]])

            with sp.Fori(0, BATCH) as b:
                sp.wait_ge(ext, b * 3 + 3)
                sp.dma_start(xD[bass.ds(b * TILES, TILES)].rearrange("t p c -> p t c"),
                             windows(xE[:, :], AUG)).then_inc(x_st, 16)
                sp.wait_ge(q_out, b + 1)
                sp.dma_start(qD[bass.ds(b * TILES, TILES)].rearrange("t p c -> p t c"),
                             qT[:, :].rearrange("p (t c) -> p t c", t=TILES)).then_inc(q_st, 16)
                sp.wait_ge(k_out, (b + 1) * (1 + 2 * WH))
                sp.dma_start(kD[bass.ds(b * TILES, TILES)].rearrange("t p c -> p t c"),
                             windows(kT[:, :], 128)).then_inc(k_st, 16)
            sp.wait_ge(x_st, BATCH * 16)
            sp.wait_ge(q_st, BATCH * 16)
            sp.wait_ge(k_st, BATCH * 16)
            sp.wait_ge(b_in, 16)

        @block.tensor
        def _(pe):
            pe.wait_ge(w_in, 16 * 20)
            with pe.Fori(0, BATCH) as b:
                pe.wait_ge(ext, b * 3 + 3)
                pe.wait_ge(q_out, b)
                pe.wait_ge(k_out, b * (1 + 2 * WH))
                for c in range(3):
                    nc.tensor.matmul(psq[:, c, 0:HALF], wq[:, :], xE[:, LEFT + c * HALF:LEFT + (c + 1) * HALF],
                                     start=True, stop=True)
                    last = nc.tensor.matmul(psk[:, c, 0:EXT // 3], wk[:, :], xE[:, c * (EXT // 3):(c + 1) * (EXT // 3)],
                                            start=True, stop=True)
                last.then_inc(proj, 1)

        @block.scalar
        def _(act):
            with act.Fori(0, BATCH) as b:
                act.wait_ge(proj, b + 1)
                act.wait_ge(q_st, b * 16)
                nc.scalar.activation(qT[:, :].rearrange("p (c n) -> p c n", c=3), psq[:, :, 0:HALF],
                                     ACT.Copy).then_inc(q_out, 1)

    with ExitStack() as ctx:
        s = Space(nc, ctx, "wina")
        qw = s.sb("q", [128, 2, TP])
        kw = s.sb("k", [128, 2, WSPAN])
        xw = s.sb("x", [AUG, 2, WSPAN])
        S = s.sb("scores", [TP, 2, WH, WSPAN])
        P = s.sb("probs", [TP, 2, WH, WSPAN])
        PT = s.sb("probsT", [128, WH, TP])
        PT2 = s.sb("probsT2", [k_rest, WH, TP])
        v1 = s.sb("v1", [128, 2, DIM])
        v2 = s.sb("v2", [k_rest, 2, DIM])
        nmax = s.sb("neg_max", [TP, 2, WH])
        sums = s.sb("sums", [TP, 2, WH])
        rs = s.sb("inv_sums", [TP, 2, WH])
        o = s.sb("o", [TP, DIM])
        oT = s.sb("oT", [AUG, TP])
        psS = s.ps("psS", (128, WH, 512))
        psT = s.ps("psT", (128, 2, WH, 128))
        psV = s.ps("psV", (128, 512))
        psO = s.ps("psO", (128, 512))
        w_q = [s.sem(f"q_in{k}") for k in range(2)]
        w_k = [s.sem(f"k_in{k}") for k in range(2)]
        w_x = [s.sem(f"x_in{k}") for k in range(2)]
        init, scored, v_mm, v_done, biased, maxed = (s.sem(n) for n in ("init", "scored", "v_mm", "v_done", "biased", "maxed"))
        exped, turned, pt_done, pt2_done, inv, pv = (s.sem(n) for n in ("exped", "turned", "pt_done", "pt2_done", "inv", "pv"))
        o_done, o_turned, oT_done, y_mm, added = (s.sem(n) for n in ("o_done", "o_turned", "oT_done", "y_mm", "added"))
        block = ctx.enter_context(nc.Block())
        PAIRS = UNITS // 2

        @block.sync
        def _(sp):
            def load(u, k):
                sp.dma_start(qw[:, k, :], qD[bass.ds(u, 1)].rearrange("a p c -> (a p) c")).then_inc(w_q[k], 16)
                sp.dma_start(kw[:, k, :], kD[bass.ds(u, 1)].rearrange("a p c -> (a p) c")).then_inc(w_k[k], 16)
                sp.dma_start(xw[:, k, :], xD[bass.ds(u, 1)].rearrange("a p c -> (a p) c")).then_inc(w_x[k], 16)
            for k in range(2):
                load(k, k)
            with sp.Fori(0, PAIRS - 1) as i:
                for k in range(2):
                    sp.wait_ge(scored, i * 2 + k + 1)
                    sp.wait_ge(v_mm, i * 2 + k + 1)
                    load(i * 2 + 2 + k, k)

        @block.tensor
        def _(pe):
            def score(i, k):
                pe.wait_ge(w_q[k], i * 16 + 16)
                pe.wait_ge(w_k[k], i * 16 + 16)
                pe.wait_ge(biased, i * 2 + k)
                for h in range(WH):
                    last = nc.tensor.matmul(psS[0:TP, h, 0:WSPAN], qw[32 * h:32 * h + 32, k, :],
                                            kw[32 * h:32 * h + 32, k, :], start=True, stop=True)
                last.then_inc(scored, 1)
                pe.wait_ge(w_x[k], i * 16 + 16)
                pe.wait_ge(v_done, (i * 2 + k) * 2)
                nc.tensor.matmul(psV[:, 0:DIM], xw[:, k, 0:128], wv[:, :], start=True, stop=True)
                nc.tensor.matmul(psV[0:k_rest, DIM:2 * DIM], xw[:, k, 128:WSPAN], wv[:, :],
                                 start=True, stop=True).then_inc(v_mm, 1)

            def attend(i, k):
                u = i * 2 + k
                pe.wait_ge(exped, (u + 1) * WH)
                pe.wait_ge(pt_done, u)
                pe.wait_ge(pt2_done, u)
                for h in range(WH):
                    nc.tensor.transpose(psT[:, 0, h, 0:TP], P[:, k, h, 0:128], ident[0:TP, 0:TP])
                    last = nc.tensor.transpose(psT[0:k_rest, 1, h, 0:TP], P[:, k, h, 128:WSPAN], ident[0:TP, 0:TP])
                last.then_inc(turned, 1)
                pe.wait_ge(pt_done, u + 1)
                pe.wait_ge(pt2_done, u + 1)
                pe.wait_ge(v_done, (u + 1) * 2)
                pe.wait_ge(added, u)
                for h in range(WH):
                    cols = slice(h * WHD, (h + 1) * WHD)
                    nc.tensor.matmul(psO[0:TP, cols], PT[:, h, :], v1[:, k, cols], start=True, stop=False)
                    last = nc.tensor.matmul(psO[0:TP, cols], PT2[:, h, :], v2[:, k, cols], start=False, stop=True)
                last.then_inc(pv, 1)
                pe.wait_ge(init, 1)
                pe.wait_ge(o_done, u + 1)
                turn(nc, psO[0:DIM, 128:128 + TP], o[:, :], ident[0:TP, 0:TP], after_wait=True).then_inc(o_turned, 1)
                pe.wait_ge(oT_done, u + 1)
                nc.tensor.matmul(psO[0:TP, 256:256 + DIM], oT[:, :], wp[:, :], start=True, stop=True).then_inc(y_mm, 1)

            score(0, 0)
            with pe.Fori(0, PAIRS - 1) as i:
                score(i, 1)
                attend(i, 0)
                score(i + 1, 0)
                attend(i, 1)
            score(PAIRS - 1, 1)
            attend(PAIRS - 1, 0)
            attend(PAIRS - 1, 1)

        @block.vector
        def _(dve):
            nc.vector.memset(oT[DIM:AUG, :], 1.0).then_inc(init, 1)

            def soften(i, k):
                u = i * 2 + k
                dve.wait_ge(scored, u + 1)
                dve.wait_ge(exped, u * WH)
                nc.vector.scalar_tensor_tensor(S[:, k, :, :], psS[0:TP, :, 0:WSPAN], WHD ** -0.5, bias[:, :, :],
                                               ALU.mult, ALU.add).then_inc(biased, 1)
                dve.wait_ge(biased, u + 1)
                nc.vector.tensor_reduce(nmax[:, k, :], S[:, k, :, :], op=ALU.max, axis=AX.X, negate=True).then_inc(maxed, 1)

            def finish(i, k):
                u = i * 2 + k
                dve.wait_ge(turned, u + 1)
                dve.wait_ge(pv, u)
                nc.vector.tensor_copy(PT2[:, :, :], psT[0:k_rest, 1, :, 0:TP]).then_inc(pt2_done, 1)
                dve.wait_ge(exped, (u + 1) * WH)
                nc.vector.reciprocal(rs[:, k, :], sums[:, k, :]).then_inc(inv, 1)
                dve.wait_ge(pv, u + 1)
                dve.wait_ge(inv, u + 1)
                nc.vector.tensor_tensor(o[:, :].rearrange("p (h d) -> p h d", h=WH),
                                        psO[0:TP, 0:DIM].rearrange("p (h d) -> p h d", h=WH),
                                        bc_free(rs[:, k, :], TP, WHD), ALU.mult).then_inc(o_done, 1)
                dve.wait_ge(y_mm, u + 1)
                Hu = H[:, bass.ds(u, 1), :].rearrange("p a d -> p (a d)")
                nc.vector.tensor_tensor(Hu, Hu, psO[0:TP, 256:256 + DIM], ALU.add).then_inc(added, 1)

            soften(0, 0)
            with dve.Fori(0, PAIRS - 1) as i:
                soften(i, 1)
                finish(i, 0)
                soften(i + 1, 0)
                finish(i, 1)
            soften(PAIRS - 1, 1)
            finish(PAIRS - 1, 0)
            finish(PAIRS - 1, 1)

        @block.scalar
        def _(act):
            def exps(i, k):
                u = i * 2 + k
                act.wait_ge(v_mm, u + 1)
                nc.scalar.activation(v1[:, k, :], psV[:, 0:DIM], ACT.Copy).then_inc(v_done, 1)
                nc.scalar.activation(v2[:, k, :], psV[0:k_rest, DIM:2 * DIM], ACT.Copy).then_inc(v_done, 1)
                act.wait_ge(maxed, u + 1)
                for h in range(WH):
                    nc.scalar.activation(P[:, k, h, :], S[:, k, h, :], ACT.Exp, bias=nmax[:, k, h:h + 1],
                                         accum_out=sums[:, k, h:h + 1]).then_inc(exped, 1)

            def turn(i, k):
                u = i * 2 + k
                act.wait_ge(turned, u + 1)
                nc.scalar.activation(PT[:, :, :], psT[:, 0, :, 0:TP], ACT.Copy).then_inc(pt_done, 1)
                act.wait_ge(o_turned, u + 1)
                nc.scalar.activation(oT[0:DIM, :], psO[0:DIM, 128:128 + TP], ACT.Copy).then_inc(oT_done, 1)

            exps(0, 0)
            with act.Fori(0, PAIRS - 1) as i:
                exps(i, 1)
                turn(i, 0)
                exps(i + 1, 0)
                turn(i, 1)
            exps(PAIRS - 1, 1)
            turn(PAIRS - 1, 0)
            turn(PAIRS - 1, 1)
    bias_ctx.close()


PH, PK, PDK, TOPK = 8, 64, 32, 16
GROUPS = 2 * PH
SLOTS = PK * PK
CHUNKS = SLOTS // 128
STAIRS = [(0, 1, 16, 0), (1, 1, 8, 16), (2, 2, 5, 24), (4, 4, 3, 34), (8, 8, 1, 46)]
CAND = 54


def select_stage(nc, io, xT, e01D, theta, inv_z):
    with ExitStack() as ctx:
        s = Space(nc, ctx, "sel")
        wT = s.sb("wT", [PDK, GROUPS, DIM])
        keys = s.sb("keys", [PDK, GROUPS, PK])
        A = s.sb("A", [DIM, GROUPS * PK])
        xs = s.sb("xs", [DIM, 2, TP])
        nmx = s.sb("neg_max", [TP, GROUPS])
        d = s.sb("shifted", [TP, 2, GROUPS, PK])
        e = s.sb("e01", [TP, 2, GROUPS, PK])
        rest = s.sb("rest", [TP, GROUPS, PK])
        top = s.sb("top", [TP, GROUPS, TOPK])
        cand = s.sb("cand", [TP, PH, CAND])
        crest = s.sb("cand_rest", [TP, PH, CAND])
        best = s.sb("best", [TP, PH, TOPK])
        z = s.sb("z", [TP, PH])
        gate = s.sb("gate", [TP, 1])
        ps = [s.ps(f"ps{k}", (128, GROUPS, PK)) for k in range(2)]
        w_in, a_mm, a_done, x_cp, sims, shifted, exped = (
            s.sem(n) for n in ("w_in", "a_mm", "a_done", "x_copied", "sims", "shifted", "exped"))
        step, tops_done = s.sem("step"), s.sem("tops_done")
        stored = [s.sem(f"stored{k}") for k in range(2)]
        block = ctx.enter_context(nc.Block())
        PAIRS = UNITS // 2

        @block.sync
        def _(sp):
            for p in range(2):
                sp.dma_start(wT[:, p:GROUPS:2, :],
                             io["L0_ffn_Wq_pkT"][p * PH * PDK:(p + 1) * PH * PDK, :].rearrange("(h d) c -> d h c", d=PDK)).then_inc(w_in, 16)
                sp.dma_start(keys[:, p:GROUPS:2, :], io["L0_ffn_pk_keysT"][p].rearrange("h d k -> d h k")).then_inc(w_in, 16)
            with sp.Fori(0, PAIRS) as i:
                for k in range(2):
                    sp.wait_ge(exped, i * 2 + k + 1)
                    sp.dma_start(e01D[bass.ds(i * 2 + k, 1)].rearrange("a p c -> (a p) c"),
                                 e[:, k, :, :].rearrange("p g c -> p (g c)")).then_inc(stored[k], 16)
            for k in range(2):
                sp.wait_ge(stored[k], 16 * PAIRS)

        @block.tensor
        def _(pe):
            pe.wait_ge(w_in, 16 * 4)
            for g in range(GROUPS):
                last = nc.tensor.matmul(ps[0][0:DIM, g, :], wT[:, g, :], keys[:, g, :], start=True, stop=True)
            last.then_inc(a_mm, 1)
            pe.wait_ge(a_done, 1)
            with pe.Fori(0, PAIRS) as i:
                for k in range(2):
                    pe.wait_ge(x_cp, i * 2 + k + 1)
                    pe.wait_ge(shifted, i * 2)
                    for c in range(2):
                        last = nc.tensor.matmul(ps[k][0:TP, c * 8:(c + 1) * 8, :].rearrange("p g c -> p (g c)"), xs[:, k, :],
                                                A[:, c * 512:(c + 1) * 512], start=True, stop=True)
                    last.then_inc(sims, 1)

        @block.scalar
        def _(act):
            act.wait_ge(a_mm, 1)
            nc.scalar.activation(A[:, :].rearrange("p (g c) -> p g c", g=GROUPS), ps[0][0:DIM, :, :], ACT.Copy).then_inc(a_done, 1)
            xTf = xT[0:DIM, :, :].rearrange("p b n -> p (b n)")
            with act.Fori(0, PAIRS) as i:
                for k in range(2):
                    act.wait_ge(sims, i * 2)
                    nc.scalar.activation(xs[:, k, :], xTf[:, bass.ds((i * 2 + k) * TP, TP)], ACT.Copy).then_inc(x_cp, 1)
                for k in range(2):
                    act.wait_ge(shifted, i * 2 + k + 1)
                    act.wait_ge(stored[k], i * 16)
                    act.wait_ge(tops_done, i * 2)
                    nc.scalar.activation(e[:, k, :, :], d[:, k, :, :], ACT.Exp).then_inc(exped, 1)

        @block.vector
        def _(dve):
            with dve.Fori(0, PAIRS) as i:
                st = Steps(dve, step, i * 2 * SEL_STEPS)
                for k in range(2):
                    u = i * 2 + k
                    dve.wait_ge(sims, u + 1)
                    st.link(nc.vector.tensor_reduce(nmx[:, :], ps[k][0:TP, :, :], op=ALU.max, axis=AX.X, negate=True))
                    dve.wait_ge(exped, i * 2)
                    nc.vector.tensor_tensor(d[:, k, :, :], ps[k][0:TP, :, :], bc_free(nmx[:, :], TP, PK),
                                            ALU.add).then_inc(shifted, 1)
                    dve.wait_ge(exped, u + 1)
                    st.mark(nc.vector.memset(gate[:, :], 0.0))
                    for g in range(GROUPS):
                        st.mark(nc.vector.max(top[:, g, 0:8], e[:, k, g, :]))
                    st.settle()
                    st.mark(nc.vector.memset(gate[:, :], 0.0))
                    for g in range(GROUPS):
                        st.mark(nc.vector.match_replace(rest[:, g, :], top[:, g, 0:8], e[:, k, g, :], -1.0))
                    st.settle()
                    st.mark(nc.vector.memset(gate[:, :], 0.0))
                    for g in range(GROUPS):
                        st.mark(nc.vector.max(top[:, g, 8:16], rest[:, g, :]))
                    st.settle()
                    for a, na, nb, col in STAIRS:
                        shape = [TP, PH, na, nb]
                        st.mark(nc.vector.tensor_tensor(
                            cand[:, :, col:col + na * nb].rearrange("p h (a b) -> p h a b", a=na),
                            top[:, 0:GROUPS:2, a:a + na].unsqueeze(3).to_broadcast(shape),
                            top[:, 1:GROUPS:2, 0:nb].unsqueeze(2).to_broadcast(shape), ALU.mult))
                    st.settle()
                    st.mark(nc.vector.memset(gate[:, :], 0.0))
                    for h in range(PH):
                        st.mark(nc.vector.max(best[:, h, 0:8], cand[:, h, :]))
                    st.settle()
                    st.mark(nc.vector.memset(gate[:, :], 0.0))
                    for h in range(PH):
                        st.mark(nc.vector.match_replace(crest[:, h, :], best[:, h, 0:8], cand[:, h, :], -1.0))
                    st.settle()
                    st.mark(nc.vector.memset(gate[:, :], 0.0))
                    for h in range(PH):
                        st.mark(nc.vector.max(best[:, h, 8:16], crest[:, h, :]))
                    st.settle()
                    st.mark(nc.vector.tensor_reduce(z[:, :], best[:, :, :], op=ALU.add, axis=AX.X))
                    st.link(nc.vector.tensor_copy(theta[:, bass.ds(u, 1), :].rearrange("p a h -> p (a h)"), best[:, :, TOPK - 1]))
                    nc.vector.reciprocal(inv_z[:, bass.ds(u, 1), :].rearrange("p a h -> p (a h)"), z[:, :]).then_inc(tops_done, 1)
                    dve.wait_ge(tops_done, u + 1)
                assert st.n == 2 * SEL_STEPS, st.n


SEL_STEPS = 1 + 3 * (1 + GROUPS) + len(STAIRS) + 3 * (1 + PH) + 2


def memory_stage(nc, io, H, xT, ident, e01D, theta, inv_z):
    with ExitStack() as ctx:
        s = Space(nc, ctx, "mem")
        table = s.sb("table", [128, CHUNKS, 2 * DIM])
        wq, wo = s.sb("wq", [AUG, DIM]), s.sb("wo", [DIM, DIM])
        xb, kb = s.sb("tokens_batch", [AUG, PAD]), s.sb("key_batch", [DIM, PAD])
        mask = s.sb("causal", [TP, TP])
        e01 = s.sb("e01", [TP, 2, 2 * PK])
        W = s.sb("weights", [TP, 2, SLOTS])
        WT = s.sb("weightsT", [128, 2, CHUNKS * TP])
        ks = s.sb("key", [TP, 2, DIM])
        kT = s.sb("keyT", [DIM, NODES])
        V = s.sb("value", [TP, UNITS, DIM])
        Vb = s.sb("value_batch", [TP, TILES, DIM])
        qb = s.sb("queryT", [DIM, PAD])
        P = s.sb("probs", [TP, 2, PAD])
        PT = s.sb("probsT", [TP, PAD])
        nm = s.sb("neg_max", [TP, 2, 4])
        sums = s.sb("sums", [TP, 2, 2])
        rs = s.sb("inv_sums", [TP, 2])
        oT = s.sb("outT", [DIM, TP])
        set_a, set_b = s.ps("set_a", (128, 3, 512)), s.ps("set_b", (128, 3, 512))
        ps_c, ps_d = s.ps("ps_c", (128, 512)), s.ps("ps_d", (128, 512))
        t_in, w_in = s.sem("table_in"), s.sem("w_in")
        e_in = [s.sem(f"e_in{k}") for k in range(2)]
        m_done, step, weighted, w_turned, wT_done, kv_mm, kv_done, k_turned, kT_done = (
            s.sem(n) for n in ("mask_done", "step", "weighted", "w_turned", "wT_done", "kv_mm", "kv_done", "k_turned", "kT_done"))
        x_cp, k_cp = s.sem("x_copied"), s.sem("k_copied")
        step2, inv1 = s.sem("max_step"), s.sem("summed")
        q_mm, q_done, v_cp, scored, maxed, exped, turned, pt_done, pv, oT_done, y_mm, added, inv = (
            s.sem(n) for n in ("q_mm", "q_done", "v_copied", "scored", "maxed", "exped", "turned", "pt_done", "pv",
                               "oT_done", "y_mm", "added", "inv"))
        block = ctx.enter_context(nc.Block())
        PAIRS = UNITS // 2
        TPARTS = 4
        GR = 4
        NG = CHUNKS // GR
        LAG = 2
        turn_banks = [set_a[:, n, :] for n in range(3)] + [set_b[:, 2, :]]
        groups = [[list(range(a, min(a + GR, t + 1))) for a in range(0, t + 1, GR)] for t in range(TILES)]
        before = [sum(len(groups[x]) for x in range(t)) for t in range(TILES + 1)]

        max_before = [sum(1 + ((x + 1) % 3 > 0 and x > 2) for x in range(t)) for t in range(TILES + 1)]
        MAX_STEPS = max_before[TILES]

        @block.sync
        def _(sp):
            def load_table(h):
                for n in range(TPARTS):
                    part = CHUNKS // TPARTS
                    sp.dma_start(table[:, n * part:(n + 1) * part, :],
                                 io["L0_ffn_tables"][bass.ds(h * SLOTS + n * part * 128, part * 128), :]
                                 .rearrange("(c p) d -> p c d", p=128)).then_inc(t_in, 16)

            def load_e(h, u, k):
                sp.dma_start(e01[:, k, :], e01D[bass.ds(u, 1), :, bass.ds(h * 2 * PK, 2 * PK)].rearrange("a p c -> (a p) c")).then_inc(e_in[k], 16)

            load_table(0)
            def head(h):
                sp.wait_ge(added, h * UNITS)
                sp.dma_start(wq[0:DIM, :], io["L0_ffn_Wq"][:, bass.ds(h * DIM, DIM)]).then_inc(w_in, 16)
                sp.dma_start(wo[:, :], io["L0_ffn_Wo"][bass.ds(h * DIM, DIM), :]).then_inc(w_in, 16)
                with sp.Fori(0, PAIRS) as i:
                    for k in range(2):
                        sp.wait_ge(weighted, h * UNITS + i * 2)
                        load_e(h, i * 2 + k, k)

            with sp.Fori(0, PH - 1) as h:
                head(h)
                sp.wait_ge(kv_mm, h * UNITS + UNITS)
                load_table(h + 1)
            head(PH - 1)

        @block.gpsimd
        def _(pool):
            nc.gpsimd.memset(mask[:, :], 0.0).then_inc(m_done, 1)
            pool.wait_ge(m_done, 1)
            nc.gpsimd.affine_select(out=mask[:, :], in_=mask[:, :], compare_op=ALU.is_ge, fill=FAR, base=0,
                                    pattern=[[-1, TP]], channel_multiplier=1).then_inc(m_done, 1)
            pool.wait_ge(m_done, 2)
            nc.gpsimd.memset(wq[DIM:AUG, :], 0.0).then_inc(m_done, 1)
            pool.wait_ge(m_done, 3)
            with pool.Fori(0, PH) as h:
                with pool.Fori(0, BATCH) as b:
                    hb = h * BATCH + b
                    pool.wait_ge(q_mm, hb)
                    nc.gpsimd.tensor_copy(xb[:, :], xT[:, bass.ds(b, 1), :].rearrange("p a n -> p (a n)")).then_inc(x_cp, 1)
                    pool.wait_ge(pv, hb * TILES)
                    pool.wait_ge(kT_done, h * UNITS + UNITS)
                    nc.gpsimd.tensor_copy(kb[:, :], kT[:, bass.ds(b * PAD, PAD)]).then_inc(k_cp, 1)
                    pool.wait_ge(kv_done, (h * UNITS + UNITS) * 2)
                    nc.gpsimd.tensor_copy(Vb[:, :, :], V[:, bass.ds(b * TILES, TILES), :]).then_inc(v_cp, 1)

        @block.tensor
        def _(pe):
            pe.wait_ge(m_done, 3)
            with pe.Fori(0, PH) as h:
                def combine(i, k):
                    first = isinstance(i, int) and i == 0 and k == 0
                    g = h * UNITS + i * 2 + k
                    pe.wait_ge(t_in, (h + 1) * 16 * TPARTS)
                    pe.wait_ge(weighted, g + 1)
                    if first:
                        pe.wait_ge(exped, h * UNITS)
                        pe.wait_ge(q_done, h * BATCH)
                    if not (isinstance(i, int) and i == 0):
                        pe.wait_ge(kv_done, (g - 1) * 2)
                    for j in range(NG + LAG):
                        if j < NG:
                            if not first or j >= len(turn_banks):
                                pe.wait_ge(wT_done, g * NG + j - len(turn_banks) + 1)
                            for c in range(GR):
                                ch = j * GR + c
                                last = nc.tensor.transpose(turn_banks[j % 4][:, c * TP:(c + 1) * TP],
                                                           W[:, k, ch * 128:(ch + 1) * 128], ident[0:TP, 0:TP])
                            last.then_inc(w_turned, 1)
                        if j >= LAG:
                            pe.wait_ge(wT_done, g * NG + j - LAG + 1)
                            for c in range(GR):
                                ch = (j - LAG) * GR + c
                                last = nc.tensor.matmul(set_b[0:TP, k, 0:2 * DIM], WT[:, k, ch * TP:(ch + 1) * TP],
                                                        table[:, ch, :], start=(ch == 0), stop=(ch == CHUNKS - 1))
                    last.then_inc(kv_mm, 1)

                def turn_key(i, k):
                    g = h * UNITS + i * 2 + k
                    if isinstance(i, int) and i == 0 and k == 0:
                        pe.wait_ge(pt_done, h * BATCH * before[TILES])
                    pe.wait_ge(kT_done, g)
                    pe.wait_ge(kv_done, g * 2 + 2)
                    turn(nc, ps_c[0:DIM, 0:TP], ks[:, k, :], ident[0:TP, 0:TP], after_wait=True).then_inc(k_turned, 1)

                combine(0, 0)
                combine(0, 1)
                turn_key(0, 0)
                with pe.Fori(1, PAIRS) as i:
                    combine(i, 0)
                    turn_key(i - 1, 1)
                    combine(i, 1)
                    turn_key(i, 0)
                turn_key(PAIRS - 1, 1)

                with pe.Fori(0, BATCH) as b:
                    hb = h * BATCH + b
                    base = hb * TILES

                    def score(t):
                        if t < 2:
                            pe.wait_ge(exped, base)
                        else:
                            pe.wait_ge(exped, base + t - 1)
                        dst = (set_a, set_b)[t % 2]
                        width = (t + 1) * TP
                        for c in range(0, width, HALF):
                            n = min(HALF, width - c)
                            diag = c + n == width
                            last = nc.tensor.matmul(dst[0:TP, c // HALF, 0:n], qb[:, t * TP:(t + 1) * TP],
                                                    kb[:, c:c + n], start=True, stop=not diag)
                            if diag:
                                last = nc.tensor.matmul(dst[0:TP, c // HALF, n - TP:n], ident[0:TP, 0:TP], mask[:, :],
                                                        start=False, stop=True)
                        last.then_inc(scored, 1)

                    def attend(t):
                        for x, blocks in enumerate(groups[t]):
                            pe.wait_ge(exped, base + t + 1)
                            pe.wait_ge(pt_done, hb * before[TILES] + before[t] + x)
                            for y, kt in enumerate(blocks):
                                last = nc.tensor.transpose(ps_c[0:TP, y * TP:(y + 1) * TP], P[:, t % 2, kt * TP:(kt + 1) * TP],
                                                           ident[0:TP, 0:TP])
                            last.then_inc(turned, 1)
                            if x == 0 and t > 0:
                                project(t - 1)
                            if x == 0:
                                pe.wait_ge(added, base + t)
                            pe.wait_ge(pt_done, hb * before[TILES] + before[t] + x + 1)
                            for kt in blocks:
                                last = nc.tensor.matmul(ps_d[0:DIM, 0:TP], Vb[:, kt, :], PT[:, kt * TP:(kt + 1) * TP],
                                                        start=(kt == 0), stop=(kt == t))
                        last.then_inc(pv, 1)

                    def project(t):
                        pe.wait_ge(oT_done, base + t + 1)
                        nc.tensor.matmul(ps_d[0:TP, 256:256 + DIM], oT[:, :], wo[:, :], start=True, stop=True).then_inc(y_mm, 1)

                    pe.wait_ge(w_in, h * 32 + 32)
                    pe.wait_ge(kT_done, h * UNITS + UNITS)
                    pe.wait_ge(kv_done, (h * UNITS + UNITS) * 2)
                    pe.wait_ge(x_cp, hb + 1)
                    pe.wait_ge(exped, base)
                    for c in range(3):
                        last = nc.tensor.matmul(set_b[0:DIM, c, 0:HALF], wq[:, :], xb[:, c * HALF:(c + 1) * HALF],
                                                start=True, stop=True)
                    last.then_inc(q_mm, 1)
                    pe.wait_ge(q_done, hb + 1)
                    pe.wait_ge(k_cp, hb + 1)
                    pe.wait_ge(v_cp, hb + 1)
                    score(0)
                    for t in range(TILES):
                        if t + 1 < TILES:
                            score(t + 1)
                        attend(t)
                    project(TILES - 1)

        @block.scalar
        def _(act):
            with act.Fori(0, PH) as h:
                def copy_turned(i, k):
                    g = h * UNITS + i * 2 + k
                    for j in range(NG):
                        act.wait_ge(w_turned, g * NG + j + 1)
                        if j == 0 and not (isinstance(i, int) and i == 0):
                            act.wait_ge(kv_mm, g - 1)
                        nc.scalar.activation(WT[:, k, j * GR * TP:(j + 1) * GR * TP], turn_banks[j % 4][:, 0:GR * TP],
                                             ACT.Copy).then_inc(wT_done, 1)

                def copy_key(i, k):
                    g = h * UNITS + i * 2 + k
                    act.wait_ge(k_turned, g + 1)
                    act.wait_ge(k_cp, h * BATCH)
                    nc.scalar.activation(kT[:, bass.ds((i * 2 + k) * TP, TP)], ps_c[0:DIM, 0:TP], ACT.Copy).then_inc(kT_done, 1)

                copy_turned(0, 0)
                copy_turned(0, 1)
                copy_key(0, 0)
                with act.Fori(1, PAIRS) as i:
                    copy_turned(i, 0)
                    copy_key(i - 1, 1)
                    copy_turned(i, 1)
                    copy_key(i, 0)
                copy_key(PAIRS - 1, 1)
                with act.Fori(0, BATCH) as b:
                    hb = h * BATCH + b
                    base = hb * TILES
                    act.wait_ge(q_mm, hb + 1)
                    act.wait_ge(scored, base)
                    nc.scalar.activation(qb[:, :].rearrange("p (c n) -> p c n", c=3), set_b[0:DIM, :, 0:HALF], ACT.Copy,
                                         scale=DIM ** -0.5).then_inc(q_done, 1)

                    def exps(t):
                        act.wait_ge(maxed, base + t + 1)
                        if t >= 2:
                            act.wait_ge(pv, base + t - 1)
                        else:
                            act.wait_ge(pv, base)
                            act.wait_ge(inv, base)
                        src = (set_a, set_b)[t % 2]
                        full, rest = divmod((t + 1) * TP, HALF)
                        if full:
                            last = nc.scalar.activation(P[:, t % 2, 0:full * HALF].rearrange("p (c n) -> p c n", c=full),
                                                        src[0:TP, 0:full, 0:HALF], ACT.Exp, bias=nm[:, t % 2, 2:3],
                                                        accum_out=sums[:, t % 2, 0:1])
                        if rest:
                            last = nc.scalar.activation(P[:, t % 2, full * HALF:full * HALF + rest], src[0:TP, full, 0:rest],
                                                        ACT.Exp, bias=nm[:, t % 2, 2:3],
                                                        accum_out=sums[:, t % 2, 1:2] if full else sums[:, t % 2, 0:1])
                        last.then_inc(exped, 1)

                    exps(0)
                    for t in range(TILES):
                        if t + 1 < TILES:
                            exps(t + 1)
                        act.wait_ge(pv, base + t + 1)
                        act.wait_ge(y_mm, base + t)
                        nc.scalar.activation(oT[:, :], ps_d[0:DIM, 0:TP], ACT.Copy).then_inc(oT_done, 1)

        @block.vector
        def _(dve):
            with dve.Fori(0, PH) as h:
                if PAIRS > 1:
                    def weigh(i, k):
                        g = h * UNITS + i * 2 + k
                        st = Steps(dve, step, g)
                        dve.wait_ge(e_in[k], (h * PAIRS + i) * 16 + 16)
                        if not (isinstance(i, int) and i == 0):
                            dve.wait_ge(w_turned, (g - 1) * NG)
                        Wk = W[:, k, :].rearrange("p (a b) -> p a b", a=PK)
                        shape = [TP, PK, PK]
                        st.link(nc.vector.tensor_tensor(Wk, e01[:, k, PK:2 * PK].unsqueeze(2).to_broadcast(shape),
                                                        e01[:, k, 0:PK].unsqueeze(1).to_broadcast(shape), ALU.mult))
                        nc.vector.scalar_tensor_tensor(
                            W[:, k, :], W[:, k, :],
                            theta[:, bass.ds(i * 2 + k, 1), bass.ds(h, 1)].rearrange("p a h -> p (a h)"),
                            W[:, k, :], ALU.is_ge, ALU.mult).then_inc(weighted, 1)

                    def normalise(i, k):
                        g = h * UNITS + i * 2 + k
                        dve.wait_ge(kv_mm, g + 1)
                        if isinstance(i, int) and i == 0:
                            dve.wait_ge(k_turned, h * UNITS)
                        else:
                            dve.wait_ge(k_turned, g - 1)
                        z = inv_z[:, bass.ds(i * 2 + k, 1), bass.ds(h, 1)].rearrange("p a h -> p (a h)")
                        nc.vector.tensor_scalar(ks[:, k, :], set_b[0:TP, k, 0:DIM], z, None, ALU.mult).then_inc(kv_done, 1)
                        nc.vector.tensor_scalar(V[:, bass.ds(i * 2 + k, 1), :].rearrange("p a d -> p (a d)"),
                                                set_b[0:TP, k, DIM:2 * DIM], z, None, ALU.mult).then_inc(kv_done, 1)

                    weigh(0, 0)
                    weigh(0, 1)
                    normalise(0, 0)
                    weigh(1, 0)
                    normalise(0, 1)
                    with dve.Fori(1, PAIRS - 1) as i:
                        weigh(i, 1)
                        normalise(i, 0)
                        weigh(i + 1, 0)
                        normalise(i, 1)
                    weigh(PAIRS - 1, 1)
                    normalise(PAIRS - 1, 0)
                    normalise(PAIRS - 1, 1)
                with dve.Fori(0, BATCH) as b:
                    hb = h * BATCH + b
                    base = hb * TILES

                    def maxes(t):
                        dve.wait_ge(scored, base + t + 1)
                        if t < 2:
                            dve.wait_ge(exped, base)
                        else:
                            dve.wait_ge(exped, base + t - 1)
                        src = (set_a, set_b)[t % 2]
                        full, rest = divmod((t + 1) * TP, HALF)
                        mt = Steps(dve, step2, hb * MAX_STEPS + max_before[t])
                        cols = []
                        if full:
                            mt.mark(nc.vector.tensor_reduce(nm[:, t % 2, 0:1], src[0:TP, 0:full, 0:HALF], op=ALU.max, axis=AX.XY))
                            cols.append(0)
                        if rest:
                            mt.mark(nc.vector.tensor_reduce(nm[:, t % 2, 1:2], src[0:TP, full, 0:rest], op=ALU.max, axis=AX.X))
                            cols.append(1)
                        mt.settle()
                        assert mt.n == max_before[t + 1] - max_before[t]
                        nc.vector.tensor_reduce(nm[:, t % 2, 2:3], nm[:, t % 2, cols[0]:cols[-1] + 1], op=ALU.max, axis=AX.X,
                                                negate=True).then_inc(maxed, 1)

                    def add(t):
                        dve.wait_ge(inv, base + t + 1)
                        dve.wait_ge(y_mm, base + t + 1)
                        Hu = H[:, bass.ds(b * TILES + t, 1), :].rearrange("p a d -> p (a d)")
                        nc.vector.scalar_tensor_tensor(Hu, ps_d[0:TP, 256:256 + DIM], rs[:, t % 2:t % 2 + 1], Hu,
                                                       ALU.mult, ALU.add).then_inc(added, 1)

                    maxes(0)
                    for t in range(TILES):
                        if t + 1 < TILES:
                            maxes(t + 1)
                        for x, blocks in enumerate(groups[t]):
                            dve.wait_ge(turned, hb * before[TILES] + before[t] + x + 1)
                            dve.wait_ge(pv, base + t)
                            nc.vector.tensor_copy(PT[:, blocks[0] * TP:(blocks[-1] + 1) * TP],
                                                  ps_c[0:TP, 0:len(blocks) * TP]).then_inc(pt_done, 1)
                            if x == 0 and t > 0:
                                add(t - 1)
                        dve.wait_ge(exped, base + t + 1)
                        if divmod((t + 1) * TP, HALF)[0] and divmod((t + 1) * TP, HALF)[1]:
                            nc.vector.tensor_reduce(nm[:, t % 2, 3:4], sums[:, t % 2, 0:2], op=ALU.add, axis=AX.X).then_inc(inv1, 1)
                        else:
                            nc.vector.tensor_copy(nm[:, t % 2, 3:4], sums[:, t % 2, 0:1]).then_inc(inv1, 1)
                        dve.wait_ge(inv1, base + t + 1)
                        nc.vector.reciprocal(rs[:, t % 2:t % 2 + 1], nm[:, t % 2, 3:4]).then_inc(inv, 1)
                    add(TILES - 1)


MH, MHD = 8, 8
MG = 2


def heads_stage(nc, io, H, xT, ident):
    with ExitStack() as ctx:
        s = Space(nc, ctx, "mha")
        wq, wk = s.sb("wq", [AUG, MG, 128]), s.sb("wk", [AUG, MG, 128])
        wv, wo = s.sb("wv", [AUG, DIM]), s.sb("wo", [AUG, DIM])
        xb = s.sb("tokens_batch", [AUG, PAD])
        qT = s.sb("queryT", [128, MG, PAD + TP])
        kT = s.sb("keyT", [128, MG, PAD])
        V = s.sb("value", [TP, TILES, MH, MHD + 1])
        qs = s.sb("query_tile", [128, MG, TP])
        qa = s.sb("query_ahead", [32, TP])
        P = s.sb("probs", [TP, 2, PAD])
        PT = s.sb("probsT", [TP, PAD])
        nm = s.sb("neg_max", [TP, 2])
        rs = s.sb("inv_sums", [TP, MH])
        o = s.sb("o", [TP, MH, MHD])
        oT = s.sb("oT", [AUG, TP])
        sets = [s.ps(f"set{k}", (128, 3, 512)) for k in range(2)]
        ps_t, ps_o = s.ps("ps_t", (128, 512)), s.ps("ps_o", (128, 512))
        qa0_cp = s.sem("first_qa_copied")
        w_in, init, x_cp, proj, copied, pad_cp, qs_cp, qa_cp = (
            s.sem(n) for n in ("w_in", "init", "x_copied", "proj", "copied", "pad_copied", "qs_copied", "qa_copied"))
        scored, maxed, exped, turned, pt_done, pv, inv, o_done, o_turned, oT_done, y_mm, added = (
            s.sem(n) for n in ("scored", "maxed", "exped", "turned", "pt_done", "pv", "inv", "o_done", "o_turned",
                               "oT_done", "y_mm", "added"))
        block = ctx.enter_context(nc.Block())
        TURNS = [range(0, 4), range(4, 8), range(8, 9)]
        NT = len(TURNS)
        PER_B = TILES * MH
        SC_B = PER_B + 1
        PROJ = 5

        @block.sync
        def _(sp):
            sp.wait_ge(init, 4)
            for w, n in ((wq, "q"), (wk, "k")):
                for h in range(MH):
                    c = 32 * (h % 4)
                    sp.dma_start(w[0:DIM, h // 4, c:c + MHD], io[f"L1_attn_W{n}T"][:, h * MHD:(h + 1) * MHD]).then_inc(w_in, 16)
                    sp.dma_start(w[DIM:AUG, h // 4, c:c + MHD],
                                 io[f"L1_attn_b{n}"][h * MHD:(h + 1) * MHD].unsqueeze(0)).then_inc(w_in, 16)
            for w, n in ((wv, "v"), (wo, "o")):
                sp.dma_start(w[0:DIM, :], io[f"L1_attn_W{n}T"]).then_inc(w_in, 16)
                sp.dma_start(w[DIM:AUG, :], io[f"L1_attn_b{n}"].unsqueeze(0)).then_inc(w_in, 16)

        @block.gpsimd
        def _(pool):
            with pool.Fori(0, BATCH) as b:
                pool.wait_ge(proj, b * PROJ)
                nc.gpsimd.tensor_copy(xb[:, :], xT[:, bass.ds(b, 1), :].rearrange("p a n -> p (a n)")).then_inc(x_cp, 1)
                with pool.Fori(0, TILES) as t:
                    pool.wait_ge(copied, b * (PROJ + 1) + 2)
                    pool.wait_ge(qa0_cp, b + 1)
                    pool.wait_ge(scored, b * SC_B + t * MH)
                    nc.gpsimd.tensor_copy(qs[:, :, :], qT[:, :, bass.ds(t * TP, TP)]).then_inc(qs_cp, 1)
                    pool.wait_ge(scored, b * SC_B + t * MH + 1)
                    nc.gpsimd.tensor_copy(qa[:, :], qT[0:32, 0, bass.ds(t * TP + TP, TP)]).then_inc(qa_cp, 1)

        @block.tensor
        def _(pe):
            pe.wait_ge(w_in, 16 * (4 * MH + 4))
            pe.wait_ge(init, 5)

            def score(j, s0, e0, c):
                if c == 0:
                    pe.wait_ge(exped, e0 + j - 1) if j > 0 else None
                qbuf = qa[0:32, :] if j % MH == 0 else qs[32 * (j % 4):32 * (j % 4) + 32, j // 4, :]
                jj = j % MH
                return nc.tensor.matmul(sets[jj % 2][0:TP, c, 0:HALF], qbuf,
                                        kT[32 * (jj % 4):32 * (jj % 4) + 32, jj // 4, c * HALF:(c + 1) * HALF],
                                        start=True, stop=True)

            with pe.Fori(0, BATCH) as b:
                pe.wait_ge(x_cp, b + 1)
                pe.wait_ge(exped, b * PER_B)
                c0 = b * (PROJ + 1)
                for r, (w, dst) in enumerate(((wq, 0), (wq, 1), (wk, 0), (wk, 1))):
                    if r >= 2:
                        pe.wait_ge(copied, c0 + r - 1)
                    for c in range(3):
                        last = nc.tensor.matmul(sets[dst][:, c, 0:HALF], w[:, r % 2, :], xb[:, c * HALF:(c + 1) * HALF],
                                                start=True, stop=True)
                    last.then_inc(proj, 1)
                pe.wait_ge(copied, c0 + 3)
                for t in range(TILES):
                    last = nc.tensor.matmul(sets[0][0:TP, t // 8, t % 8 * DIM:(t % 8 + 1) * DIM],
                                            xb[:, t * TP:(t + 1) * TP], wv[:, :], start=True, stop=True)
                last.then_inc(proj, 1)
                pe.wait_ge(copied, c0 + 6)
                pe.wait_ge(pad_cp, b + 1)
                pe.wait_ge(qa0_cp, b + 1)
                for c in range(3):
                    last = score(0, 0, 0, c)
                last.then_inc(scored, 1)
                with pe.Fori(0, TILES) as t:
                    u = b * TILES + t
                    e0 = u * MH
                    for j in range(MH):
                        n = e0 + j
                        pe.wait_ge(exped, n + 1)
                        for x, tiles in enumerate(TURNS):
                            pe.wait_ge(pt_done, n * NT + x)
                            if j == 0 and x == 0:
                                pe.wait_ge(added, u)
                            for y, kt in enumerate(tiles):
                                last = nc.tensor.transpose(ps_t[0:TP, y * TP:(y + 1) * TP], P[:, j % 2, kt * TP:(kt + 1) * TP],
                                                           ident[0:TP, 0:TP])
                            last.then_inc(turned, 1)
                            if x == 0:
                                if j == 0:
                                    pe.wait_ge(qs_cp, u + 1)
                                    pe.wait_ge(o_done, u)
                                if j == MH - 1:
                                    pe.wait_ge(qa_cp, u + 1)
                            last = score(j + 1, 0, e0, x)
                            if x == NT - 1:
                                last.then_inc(scored, 1)
                            pe.wait_ge(pt_done, n * NT + x + 1)
                            for kt in tiles:
                                rows = TP - 1 if kt == TILES - 1 else TP
                                last = nc.tensor.matmul(ps_o[0:TP, j * (MHD + 1):(j + 1) * (MHD + 1)],
                                                        PT[0:rows, kt * TP:(kt + 1) * TP], V[0:rows, kt, j, :],
                                                        start=(kt == 0), stop=(kt == TILES - 1))
                            if x == NT - 1:
                                last.then_inc(pv, 1)
                    pe.wait_ge(o_done, u + 1)
                    turn(nc, ps_t[0:DIM, 0:TP], o[:, :, :].rearrange("p h d -> p (h d)"), ident[0:TP, 0:TP],
                         after_wait=True).then_inc(o_turned, 1)
                    pe.wait_ge(oT_done, u + 1)
                    nc.tensor.matmul(ps_t[0:TP, 256:256 + DIM], oT[:, :], wo[:, :], start=True, stop=True).then_inc(y_mm, 1)

        @block.scalar
        def _(act):
            with act.Fori(0, BATCH) as b:
                p0 = b * PROJ
                for r, dst in enumerate((qT, qT, kT, kT)):
                    act.wait_ge(proj, p0 + r + 1)
                    nc.scalar.activation(dst[:, r % 2, 0:PAD].rearrange("p (c n) -> p c n", c=3), sets[r % 2][:, :, 0:HALF],
                                         ACT.Copy, scale=MHD ** -0.5 if r < 2 else 1.0).then_inc(copied, 1)
                act.wait_ge(copied, b * (PROJ + 1) + 2)
                nc.scalar.activation(qa[:, :], qT[0:32, 0, 0:TP], ACT.Copy).then_inc(qa0_cp, 1)
                act.wait_ge(proj, p0 + PROJ)
                act.wait_ge(init, 5)
                for t0, tn in ((0, 8), (8, 1)):
                    nc.scalar.activation(V[:, t0:t0 + tn, :, 0:MHD],
                                         sets[0][0:TP, t0 // 8, 0:tn * DIM].rearrange("p (t h d) -> p t h d", t=tn, h=MH),
                                         ACT.Copy).then_inc(copied, 1)

                def exps(j, e0):
                    act.wait_ge(maxed, e0 + j + 1)
                    act.wait_ge(pv, e0 + j - 1 if j > 0 else e0)
                    nc.scalar.activation(P[:, j % 2, :].rearrange("p (c n) -> p c n", c=3), sets[j % 2][0:TP, :, 0:HALF],
                                         ACT.Exp, bias=nm[:, j % 2:j % 2 + 1]).then_inc(exped, 1)

                with act.Fori(0, TILES) as t:
                    u = b * TILES + t
                    e0 = u * MH
                    exps(0, e0)
                    for j in range(MH):
                        n = e0 + j
                        act.wait_ge(turned, n * NT + 1)
                        act.wait_ge(pv, n)
                        nc.scalar.activation(PT[:, 0:4 * TP], ps_t[0:TP, 0:4 * TP], ACT.Copy).then_inc(pt_done, 1)
                        if j + 1 < MH:
                            exps(j + 1, e0)
                    act.wait_ge(o_turned, u + 1)
                    nc.scalar.activation(oT[0:DIM, :], ps_t[0:DIM, 0:TP], ACT.Copy).then_inc(oT_done, 1)

        @block.vector
        def _(dve):
            nc.vector.memset(wq[:, :, :], 0.0).then_inc(init, 1)
            nc.vector.memset(wk[:, :, :], 0.0).then_inc(init, 1)
            nc.vector.memset(qT[:, :, PAD:PAD + TP], 0.0).then_inc(init, 1)
            nc.vector.memset(V[:, :, :, MHD:MHD + 1], 1.0).then_inc(init, 1)
            nc.vector.memset(oT[DIM:AUG, :], 1.0).then_inc(init, 1)
            with dve.Fori(0, BATCH) as b:
                dve.wait_ge(copied, b * (PROJ + 1) + 4)
                nc.vector.tensor_copy(kT[:, :, PAD - 1:PAD], kT[:, :, PAD - 2:PAD - 1]).then_inc(pad_cp, 1)

                def maxes(j, s0, e0):
                    dve.wait_ge(scored, s0 + j + 1)
                    dve.wait_ge(exped, e0 + j - 1 if j > 0 else e0)
                    nc.vector.tensor_reduce(nm[:, j % 2:j % 2 + 1], sets[j % 2][0:TP, :, 0:HALF], op=ALU.max, axis=AX.XY,
                                            negate=True).then_inc(maxed, 1)

                with dve.Fori(0, TILES) as t:
                    u = b * TILES + t
                    e0 = u * MH
                    s0 = b * SC_B + t * MH
                    maxes(0, s0, e0)
                    for j in range(MH):
                        n = e0 + j
                        dve.wait_ge(turned, n * NT + 2)
                        nc.vector.tensor_copy(PT[:, 4 * TP:8 * TP], ps_t[0:TP, 0:4 * TP]).then_inc(pt_done, 1)
                        dve.wait_ge(turned, n * NT + 3)
                        nc.vector.tensor_copy(PT[:, 8 * TP:9 * TP], ps_t[0:TP, 0:TP]).then_inc(pt_done, 1)
                        if j + 1 < MH:
                            maxes(j + 1, s0, e0)
                    dve.wait_ge(pv, e0 + MH)
                    pso = ps_o[0:TP, 0:MH * (MHD + 1)].rearrange("p (h d) -> p h d", h=MH)
                    nc.vector.reciprocal(rs[:, :], pso[:, :, MHD]).then_inc(inv, 1)
                    dve.wait_ge(inv, u + 1)
                    nc.vector.tensor_tensor(o[:, :, :], pso[:, :, 0:MHD], bc_free(rs[:, :], TP, MHD), ALU.mult).then_inc(o_done, 1)
                    dve.wait_ge(y_mm, u + 1)
                    Hu = H[:, bass.ds(u, 1), :].rearrange("p a d -> p (a d)")
                    nc.vector.tensor_tensor(Hu, Hu, ps_t[0:TP, 256:256 + DIM], ALU.add).then_inc(added, 1)


EDGES = 262144
ECOLS = EDGES // 128
LAST = BATCH * SEQ - 1
LAST_PAD = LAST + BATCH - 1
SENTINEL = -3.0e7
SHIFT = float(2 ** 23)
MAGIC = 12582912.0
SELCOL = 16
GH, GE = 4, 4
GF = GH * GE
MASK_STRIDE = NODES
JUNK = NODES * MASK_STRIDE
NODE_F = 20


def edge_stage(nc, io, ident, maskD, slots, n_rounds, hist):
    src_l, dst_l, u_l, p_l = slots
    with ExitStack() as ctx:
        s = Space(nc, ctx, "edge")
        raw = s.sb("raw", [128, ECOLS], I32)
        sp_ = s.sb("source", [128, ECOLS])
        dp = s.sb("destination", [128, ECOLS])
        a = s.sb("a", [128, ECOLS])
        c = s.sb("c", [128, ECOLS])
        vd = s.sb("valid", [128, ECOLS])
        hu = s.sb("hist_tile", [128, ECOLS])
        hp = s.sb("hist_row", [128, ECOLS])
        key = s.sb("key", [128, ECOLS])
        iota = s.sb("iota", [128, TP])
        iota_p = s.sb("iota_p", [128, 1])
        cnt = s.sb("count", [128, 1])
        cmax = s.sb("count_max", [1, 2])
        neg = s.sb("neg", [TP, MASK_STRIDE], BF16)
        zero = s.sb("zero", [128, 128], BF16)
        oh_p = s.sb("onehot_row", [128, 2, SELCOL, TP], BF16)
        oh_u = s.sb("onehot_tile", [128, 2, SELCOL, UNITS], BF16)
        gate = s.sb("gate", [128, 1])
        pgate = s.sb("gate_pool", [128, 2])
        pgated = s.sem("gated_pool")
        L = s.sb("largest", [128, 8])
        w = [s.sb(f"w{n}", [128, 8]) for n in range(10)]
        oi = s.sb("offset_i", [128, 2, 8], I32)
        off = s.sb("offset", [128, 8], I32)
        ps_h = s.ps("ps_h", (128, 512))
        ps_c = s.ps("ps_c", (128, 512))
        e_in, step, init, iota_done, counted, c_turned, rounds_done = (
            s.sem(n) for n in ("edges_in", "step", "init", "iota_done", "counted", "count_turned", "rounds_done"))
        filled, hot, h_mm, h_done, lstep, off_done, marked, raw_in2 = (
            s.sem(n) for n in ("filled", "onehot", "h_mm", "h_done", "loop_step", "off_done", "marked", "dst_in"))
        ready = s.sem("lists_ready")
        block = ctx.enter_context(nc.Block())
        edges = io["L1_ffn_edge_index"]

        @block.sync
        def _(sp):
            sp.dma_start(raw[:, :], edges[0].rearrange("(p c) -> p c", p=128)).then_inc(e_in, 16)
            sp.wait_ge(init, 1)
            with sp.Fori(0, UNITS) as u:
                sp.dma_start(maskD[bass.ds(u * TP * MASK_STRIDE, TP * MASK_STRIDE), :].rearrange("(p c) a -> p (c a)", p=TP),
                             neg[:, :]).then_inc(filled, 16)
            sp.wait_ge(ready, 1)
            sp.dma_start(raw[:, :], edges[1].rearrange("(p c) -> p c", p=128)).then_inc(raw_in2, 16)

        @block.gpsimd
        def _(pool):
            nc.gpsimd.iota(iota[:, :], pattern=[[1, TP]], base=0, channel_multiplier=0,
                           allow_small_or_imprecise_dtypes=True).then_inc(iota_done, 1)
            nc.gpsimd.iota(iota_p[:, :], pattern=[[1, 1]], base=0, channel_multiplier=1,
                           allow_small_or_imprecise_dtypes=True).then_inc(iota_done, 1)
            nc.gpsimd.memset(pgate[:, :], 0.0).then_inc(iota_done, 1)
            pool.wait_ge(iota_done, 3)
            pool.wait_ge(filled, 16 * UNITS)
            pool.wait_ge(rounds_done, 1)
            n = pool.value_load(n_rounds[0:1, 0:1], min_val=1, max_val=ECOLS // 8)
            with pool.Fori(0, n) as r:
                pool.wait_ge(off_done, r + 1)
                for j in range(8):
                    pool.wait_ge(pgated, r * 8 + j)
                    nc.gpsimd.tensor_tensor(pgate[:, 1:2], pgate[:, 0:1], pgate[:, 0:1], ALU.add).then_inc(pgated, 1)
                    nc.gpsimd.indirect_dma_start(
                        out=maskD, out_offset=bass.IndirectOffsetOnAxis(ap=off[:, j:j + 1], axis=0),
                        in_=zero[:, 0:1], in_offset=None).then_inc(marked, 16)
                    pool.wait_ge(marked, r * 128 + 16 * (j + 1))

        @block.tensor
        def _(pe):
            pe.wait_ge(counted, 1)
            nc.tensor.transpose(ps_c[0:1, 0:128], cnt[:, :], ident[:, :]).then_inc(c_turned, 1)
            pe.wait_ge(init, 2)
            nc.tensor.matmul(ps_h[0:TP, 0:UNITS], zero[:, 0:TP], zero[:, 0:UNITS], start=True, stop=False)
            with pe.Fori(0, ECOLS // SELCOL // 2) as i:
                for k in range(2):
                    pe.wait_ge(hot, i * 4 + 2 * k + 2)
                    for j in range(SELCOL):
                        last = nc.tensor.matmul(ps_h[0:TP, 0:UNITS], oh_p[:, k, j, :], oh_u[:, k, j, :], start=False, stop=False)
                    last.then_inc(h_mm, 1)
            nc.tensor.matmul(ps_h[0:TP, 0:UNITS], zero[:, 0:TP], zero[:, 0:UNITS], start=False, stop=True).then_inc(h_done, 1)

        @block.vector
        def _(dve):
            st = Steps(dve, step)
            V = nc.vector
            V.memset(neg[:, :], FAR).then_inc(init, 1)
            V.memset(zero[:, :], 0.0).then_inc(init, 1)

            def pad_number(dst, a):
                st.link(V.scalar_tensor_tensor(dst[:, :], a[:, :], float(SEQ), a[:, :], ALU.is_ge, ALU.add))
                for b in range(2, BATCH):
                    st.link(V.scalar_tensor_tensor(dst[:, :], a[:, :], float(SEQ * b), dst[:, :], ALU.is_ge, ALU.add))

            def tile_and_row(u, p, d):
                st.link(V.tensor_scalar(u, d, 1.0 / TP, 0.5 / TP - 0.5, ALU.mult, ALU.add))
                st.link(V.tensor_scalar(u, u, MAGIC, MAGIC, ALU.add, ALU.subtract))
                st.link(V.scalar_tensor_tensor(p, u, -float(TP), d, ALU.mult, ALU.add))

            dve.wait_ge(e_in, 16)
            st.link(V.tensor_copy(a[:, :], raw[:, :]))
            dve.wait_ge(step, st.n)
            V.tensor_scalar(a[:, :], a[:, :], float(LAST), None, ALU.min).then_inc(ready, 1)
            dve.wait_ge(ready, 1)
            pad_number(sp_, a)
            dve.wait_ge(raw_in2, 16)
            st.link(V.tensor_copy(c[:, :], raw[:, :]))
            st.link(V.tensor_scalar(vd[:, :], c[:, :], float(LAST + 1), None, ALU.is_lt))
            pad_number(dp, c)
            tile_and_row(hu[:, :], hp[:, :], dp[:, :])
            st.link(V.scalar_tensor_tensor(c[:, :], a[:, :], float(LAST), vd[:, :], ALU.is_equal, ALU.mult))
            st.link(V.scalar_tensor_tensor(hp[:, :], hp[:, :], 1.0, c[:, :], ALU.add, ALU.mult))
            st.link(V.tensor_scalar(hp[:, :], hp[:, :], -1.0, None, ALU.add))
            st.link(V.tensor_tensor(vd[:, :], vd[:, :], c[:, :], ALU.subtract))
            st.link(V.tensor_scalar(a[:, :], sp_[:, :], float(NODES), SHIFT, ALU.mult, ALU.subtract))
            st.link(V.tensor_tensor(a[:, :], a[:, :], dp[:, :], ALU.add))
            st.link(V.tensor_tensor(a[:, :], a[:, :], vd[:, :], ALU.mult))
            st.link(V.tensor_scalar(c[:, :], vd[:, :], -SENTINEL, SENTINEL, ALU.mult, ALU.add))
            st.link(V.tensor_tensor(key[:, :], a[:, :], c[:, :], ALU.add))
            V.tensor_reduce(cnt[:, :], vd[:, :], op=ALU.add, axis=AX.X).then_inc(counted, 1)
            dve.wait_ge(c_turned, 1)
            st.link(V.tensor_reduce(cmax[:, 0:1], ps_c[0:1, 0:128], op=ALU.max, axis=AX.X))
            st.link(V.tensor_scalar(cmax[:, 1:2], cmax[:, 0:1], 1.0 / 8, 7.0 / 8 - 7.0 / 16, ALU.mult, ALU.add))
            st.link(V.tensor_scalar(cmax[:, 1:2], cmax[:, 1:2], MAGIC, MAGIC, ALU.add, ALU.subtract))
            V.tensor_scalar(n_rounds[:, :], cmax[:, 1:2], 1.0, None, ALU.max).then_inc(rounds_done, 1)
            dve.wait_ge(rounds_done, 1)
            dve.wait_ge(iota_done, 2)
            n = dve.value_load(n_rounds[0:1, 0:1], min_val=1, max_val=ECOLS // 8)
            valid, q, rem, t, src, dst, u, p, fo, fs = (x[:, :] for x in w)
            with dve.Fori(0, n) as r:
                st = Steps(dve, lstep, r * LOOP_STEPS)
                col = bass.ds(r * 8, 8)
                st.mark(V.memset(gate[:, :], 0.0))
                st.link(V.max(L[:, :], key[:, :]))
                st.mark(V.memset(gate[:, :], 0.0))
                st.mark(V.match_replace(key[:, :], L[:, :], key[:, :], SENTINEL))
                st.link(V.tensor_scalar(valid, L[:, :], -SHIFT - 1.0, None, ALU.is_gt))
                st.link(V.tensor_scalar(L[:, :], L[:, :], -SHIFT, None, ALU.max))
                st.link(V.tensor_scalar(q, L[:, :], 1.0 / NODES, SHIFT / NODES - 0.5, ALU.mult, ALU.add))
                st.link(V.tensor_scalar(q, q, MAGIC, MAGIC, ALU.add, ALU.subtract))
                st.link(V.tensor_scalar(rem, q, float(NODES), SHIFT, ALU.mult, ALU.subtract))
                st.link(V.tensor_tensor(rem, L[:, :], rem, ALU.subtract))
                st.link(V.tensor_scalar(t, rem, 0.0, None, ALU.is_lt))
                st.link(V.tensor_tensor(q, q, t, ALU.subtract))
                st.link(V.scalar_tensor_tensor(rem, t, float(NODES), rem, ALU.mult, ALU.add))
                st.link(V.tensor_scalar(t, rem, float(NODES), None, ALU.is_ge))
                st.link(V.tensor_tensor(src, q, t, ALU.add))
                st.link(V.scalar_tensor_tensor(dst, t, -float(NODES), rem, ALU.mult, ALU.add))
                st.link(V.tensor_scalar(u, dst, 1.0 / TP, 0.5 / TP - 0.5, ALU.mult, ALU.add))
                st.link(V.tensor_scalar(u, u, MAGIC, MAGIC, ALU.add, ALU.subtract))
                st.link(V.scalar_tensor_tensor(p, u, -float(TP), dst, ALU.mult, ALU.add))
                st.link(V.scalar_tensor_tensor(p, p, 1.0, valid, ALU.add, ALU.mult))
                st.link(V.tensor_scalar(p, p, -1.0, None, ALU.add))
                st.mark(V.tensor_copy(src_l[:, col], src))
                st.mark(V.tensor_copy(dst_l[:, col], dst))
                st.mark(V.tensor_copy(u_l[:, col], u))
                st.mark(V.tensor_copy(p_l[:, col], p))
                st.mark(V.tensor_scalar(fo, dst, float(MASK_STRIDE), -float(JUNK), ALU.mult, ALU.add))
                st.link(V.tensor_scalar(fs, src, iota_p[:, 0:1], None, ALU.subtract))
                st.mark(V.tensor_tensor(fo, fo, valid, ALU.mult))
                st.link(V.tensor_tensor(fs, fs, valid, ALU.mult))
                st.mark(V.tensor_scalar(oi[:, 0, :], fo, float(JUNK), None, ALU.add))
                st.link(V.tensor_scalar(oi[:, 1, :], fs, iota_p[:, 0:1], None, ALU.add))
                dve.wait_ge(marked, r * 128)
                st.mark(V.memset(gate[:, :], 0.0))
                V.tensor_tensor(off[:, :], oi[:, 0, :], oi[:, 1, :], ALU.add).then_inc(off_done, 1)
                dve.wait_ge(off_done, r + 1)
                assert st.n == LOOP_STEPS, st.n
            with dve.Fori(0, ECOLS // SELCOL // 2) as i:
                for k in range(2):
                    dve.wait_ge(h_mm, i * 2)
                    cc = bass.ds((i * 2 + k) * SELCOL, SELCOL)
                    V.tensor_tensor(oh_p[:, k, :, :], hp[:, cc].unsqueeze(2).to_broadcast([128, SELCOL, TP]),
                                    iota[:, :].unsqueeze(1).to_broadcast([128, SELCOL, TP]), ALU.is_equal).then_inc(hot, 1)
                    V.tensor_tensor(oh_u[:, k, :, :], hu[:, cc].unsqueeze(2).to_broadcast([128, SELCOL, UNITS]),
                                    iota[:, 0:UNITS].unsqueeze(1).to_broadcast([128, SELCOL, UNITS]), ALU.is_equal).then_inc(hot, 1)
            dve.wait_ge(h_done, 1)
            V.tensor_copy(hist[:, :], ps_h[0:TP, 0:UNITS]).then_inc(counted, 1)
            dve.wait_ge(counted, 2)


LOOP_STEPS = 32


def graph_stage(nc, io, H, xT, maskD, slots, n_rounds, hist, gates):
    src_l, dst_l, u_l, p_l = slots
    srcD = nc.dram_tensor("scratch_nodes", [NODES, NODE_F], F32).ap()
    dstD = nc.dram_tensor("scratch_dst", [NODES, 2 * GH], F32).ap()
    with ExitStack() as ctx:
        s = Space(nc, ctx, "gat")
        wg = s.sb("w_gat", [DIM, GF])
        was = s.sb("w_src", [DIM, GH])
        wab = s.sb("w_src_wide", [DIM, GH, TP])
        prod = s.sb("prod", [DIM, GF])
        att = [s.sb(f"att{n}", [TP, GF]) for n in ("s", "d")]
        rows = {n: s.sb(n, [TP, GF]) for n in ("b_gat", "ln_gamma", "ln_beta")}
        xb = s.sb("tokens_batch", [AUG, PAD])
        TS = s.sb("node_rows", [TP, UNITS, NODE_F])
        TD = s.sb("dst_rows", [TP, UNITS, 2 * GH])
        big = s.sb("big", [TP, UNITS, GF])
        asb = s.sb("src_score", [TP, GH, NODES])
        mk = s.sb("mask", [TP, 2, NODES], BF16)
        junk = s.sb("junk", [TP, NODES], BF16)
        mx = s.sb("mx", [TP, 2, GH])
        M = s.sb("src_max", [TP, UNITS, GH])
        lastr = s.sb("last_row", [TP, NODE_F])
        lm = s.sb("last_mask", [TP, UNITS])
        z = [s.sb(f"z{n}", [TP, UNITS, GH]) for n in range(3)]
        gate = s.sb("gate", [TP, 1])
        sem = s.sem
        w_in, step, xcp, h_mm, h_cp, as_mm, as_cp, ts_st, last_in, td_st = (
            sem(n) for n in ("w_in", "step", "x_copied", "h_mm", "h_copied", "as_mm", "as_copied", "rows_stored",
                             "last_in", "dst_stored"))
        m_in = [sem(f"mask_in{k}") for k in range(2)]
        mstep, was_done, ts_done, td_done = sem("max_step"), sem("was_done"), sem("rows_done"), sem("dst_done")
        with ExitStack() as inner:
            ps = [inner.enter_context(nc.psum_tensor(f"gat_ps{k}", [128, 512], F32)) for k in range(4)]
            block = inner.enter_context(nc.Block())

            @block.sync
            def _(sp):
                sp.dma_start(wg[:, :], io["L1_ffn_W_gat"]).then_inc(w_in, 16)
                for n, d in (("L1_ffn_att_src", att[0]), ("L1_ffn_att_dst", att[1])):
                    sp.dma_start(d[:, :], io[n].rearrange("h e -> (h e)").unsqueeze(0).to_broadcast([TP, GF])).then_inc(w_in, 16)
                for n, d in rows.items():
                    sp.dma_start(d[:, :], io["L1_ffn_" + n].unsqueeze(0).to_broadcast([TP, GF])).then_inc(w_in, 16)
                sp.wait_ge(ts_done, 1)
                sp.dma_start(srcD.rearrange("(u p) f -> p u f", p=TP), TS[:, :, :]).then_inc(ts_st, 16)
                sp.wait_ge(ts_st, 16)
                sp.dma_start(lastr[:, :], srcD[LAST_PAD:LAST_PAD + 1, :].to_broadcast([TP, NODE_F])).then_inc(last_in, 16)
                for k in range(2):
                    sp.dma_start(mk[:, k, :], maskD[k * TP * MASK_STRIDE:(k + 1) * TP * MASK_STRIDE, :]
                                 .rearrange("(p c) a -> p (c a)", p=TP)).then_inc(m_in[k], 16)
                pairs = maskD[0:JUNK, :].rearrange("(i k p c) a -> i k p (c a)", k=2, p=TP, c=MASK_STRIDE)
                with sp.Fori(1, UNITS // 2) as i:
                    for k in range(2):
                        sp.wait_ge(mstep, (i - 1) * MAX_STEPS + (k + 1) * MAX_STEPS // 2)
                        sp.dma_start(mk[:, k, :], pairs[bass.ds(i, 1), k].rearrange("i p c -> (i p) c")).then_inc(m_in[k], 16)
                sp.wait_ge(td_done, 1)
                sp.dma_start(dstD.rearrange("(u p) f -> p u f", p=TP), TD[:, :, :]).then_inc(td_st, 16)
                sp.wait_ge(td_st, 16)

            @block.gpsimd
            def _(pool):
                with pool.Fori(0, BATCH) as b:
                    pool.wait_ge(as_mm, b * 12)
                    nc.gpsimd.tensor_copy(xb[:, :], xT[:, bass.ds(b, 1), :].rearrange("p a n -> p (a n)")).then_inc(xcp, 1)

            @block.tensor
            def _(pe):
                pe.wait_ge(w_in, 16 * 6)
                with pe.Fori(0, BATCH) as b:
                    pe.wait_ge(h_cp, b)
                    pe.wait_ge(xcp, b + 1)
                    for t in range(TILES):
                        last = nc.tensor.matmul(ps[0][0:TP, t * GF:(t + 1) * GF], xb[0:DIM, t * TP:(t + 1) * TP], wg[:, :],
                                                start=True, stop=True)
                    last.then_inc(h_mm, 1)
                    pe.wait_ge(was_done, 1)
                    for h in range(GH):
                        for c in range(3):
                            n = h * 3 + c
                            pe.wait_ge(as_cp, b * 12 + max(n - 1, 0))
                            nc.tensor.matmul(ps[2 + n % 2][0:TP, 0:HALF], wab[:, h, :], xb[0:DIM, c * HALF:(c + 1) * HALF],
                                             start=True, stop=True).then_inc(as_mm, 1)

            @block.scalar
            def _(act):
                with act.Fori(0, BATCH) as b:
                    act.wait_ge(h_mm, b + 1)
                    nc.scalar.activation(TS[:, bass.ds(b * TILES, TILES), 0:GF],
                                         ps[0][0:TP, 0:TILES * GF].rearrange("p (t f) -> p t f", t=TILES), ACT.Copy).then_inc(h_cp, 1)
                    for n in range(12):
                        act.wait_ge(as_mm, b * 12 + n + 1)
                        nc.scalar.activation(asb[:, n // 3, bass.ds(b * PAD + n % 3 * HALF, HALF)], ps[2 + n % 2][0:TP, 0:HALF],
                                             ACT.Copy).then_inc(as_cp, 1)

            @block.vector
            def _(dve):
                st = Steps(dve, step)
                V = nc.vector
                dve.wait_ge(w_in, 16 * 6)
                st.link(V.tensor_tensor(prod[:, :], wg[:, :], att[0][0:DIM, :], ALU.mult))
                st.link(V.tensor_reduce(was[:, :], prod[:, :].rearrange("p (h e) -> p h e", h=GH), op=ALU.add, axis=AX.X))
                V.tensor_copy(wab[:, :, :], bc_free(was[:, :], DIM, TP)).then_inc(was_done, 1)
                dve.wait_ge(h_cp, BATCH)
                hview = TS[:, :, 0:GF]
                for n, dst in ((0, TS[:, :, GF:NODE_F]), (1, TD[:, :, 0:GH])):
                    st.link(V.tensor_tensor(big[:, :, :], hview, att[n][:, :].unsqueeze(1).to_broadcast([TP, UNITS, GF]), ALU.mult))
                    ins = V.tensor_reduce(dst, big[:, :, :].rearrange("p u (h e) -> p u h e", h=GH), op=ALU.add, axis=AX.X)
                    st.link(ins) if n else ins.then_inc(ts_done, 1)
                    dve.wait_ge(ts_done, 1)
                dve.wait_ge(as_cp, BATCH * 12)
                with dve.Fori(0, UNITS // 2) as i:
                    mt = Steps(dve, mstep, i * MAX_STEPS)
                    for k in range(2):
                        dve.wait_ge(m_in[k], i * 16 + 16)
                        mt.mark(V.memset(gate[:, :], 0.0))
                        for h in range(GH):
                            mt.mark(V.tensor_tensor_reduce(out=junk[:, :], in0=mk[:, k, :], in1=asb[:, h, :], scale=1.0,
                                                           scalar=FAR, op0=ALU.add, op1=ALU.max, accum_out=mx[:, k, h:h + 1]))
                            if h < GH - 1:
                                mt.settle()
                                mt.mark(V.memset(gate[:, :], 0.0))
                        mt.settle()
                        mt.mark(V.tensor_copy(M[:, bass.ds(i * 2 + k, 1), :].rearrange("p a h -> p (a h)"), mx[:, k, :]))
                    assert mt.n == MAX_STEPS, mt.n
                dve.wait_ge(mstep, (UNITS // 2) * MAX_STEPS)
                dve.wait_ge(last_in, 16)
                asrc, adst = TS[:, :, GF:NODE_F], TD[:, :, 0:GH]
                st.link(V.tensor_tensor(M[:, :, :], M[:, :, :], asrc, ALU.max))
                st.link(V.tensor_scalar(lm[:, :], hist[:, :], 0.0, None, ALU.is_gt))
                st.link(V.tensor_scalar(lm[:, :], lm[:, :], -FAR, FAR, ALU.mult, ALU.add))
                for h in range(GH):
                    st.link(V.scalar_tensor_tensor(M[:, :, h], lm[:, :], lastr[:, GF + h:GF + h + 1], M[:, :, h], ALU.add, ALU.max))
                st.link(V.tensor_tensor(z[0][:, :, :], M[:, :, :], adst, ALU.add))
                V.scalar_tensor_tensor(TD[:, :, GH:2 * GH], z[0][:, :, :], 0.2, z[0][:, :, :], ALU.mult, ALU.max).then_inc(td_done, 1)
                dve.wait_ge(td_done, 1)

        pgate = s.sb("gate_pool", [128, 2])
        pgated = s.sem("gated_pool")
        gs = s.sb("src_gathered", [128, 2, 8, NODE_F])
        gd = s.sb("dst_gathered", [128, 2, 8, 2 * GH])
        ix = s.sb("indices", [128, 2, 8], I32)
        iota = s.sb("iota", [128, TP])
        zf = s.sb("zeros", [128, 512])
        sc = s.sb("edge_score", [128, 8, GH])
        sl = s.sb("edge_leaky", [128, 8, GH])
        we = s.sb("edge_weight", [128, 8, GH])
        msg = s.sb("message", [128, 8, NODE_F])
        up = s.sb("tile_row", [128, 2, 8])
        oh_p = s.sb("onehot_row", [128, 8, TP])
        oh_u = s.sb("onehot_tile", [128, 8, UNITS])
        om = s.sb("tile_message", [128, 8, UNITS * NODE_F])
        acc = s.sb("sums", [TP, UNITS, NODE_F])
        estep, init, iota_done, idx_done, gathered, shifted, exped, spread, sc_mm, opened, fin = (
            sem(n) for n in ("edge_step", "init2", "iota_done", "idx_done", "gathered", "shifted", "exped", "spread",
                             "sc_mm", "opened", "finished"))
        g_s = [sem(f"g_src{j}") for j in range(8)]
        g_d = [sem(f"g_dst{j}") for j in range(8)]
        w_e, w_ed, fstep, f_sqrt, f_root = sem("w_arg"), sem("w_exped"), sem("fstep"), sem("f_var"), sem("f_root")
        g_arg, g_exp = sem("g_arg"), sem("g_exp")
        ps_a, ps_b = s.ps("acc_a", (128, 512)), s.ps("acc_b", (128, 512))
        HU = UNITS // 2 * NODE_F
        ws, wl = s.sb("w_self", [TP, UNITS, GH]), s.sb("w_last", [TP, UNITS, GH])
        stat, root = s.sb("stat", [TP, UNITS]), s.sb("root", [TP, UNITS])
        scr = s.sb("scores", [TP, GE, UNITS])
        ge = s.sb("gate_exp", [TP, GE, UNITS])
        rank, cmp_ = s.sb("rank", [TP, GE, UNITS]), s.sb("cmp", [TP, UNITS])
        top = s.sb("top_score", [TP, UNITS])
        block = ctx.enter_context(nc.Block())

        @block.gpsimd
        def _(pool):
            nc.gpsimd.iota(iota[:, :], pattern=[[1, TP]], base=0, channel_multiplier=0,
                           allow_small_or_imprecise_dtypes=True).then_inc(iota_done, 1)
            nc.gpsimd.memset(pgate[:, :], 0.0).then_inc(iota_done, 1)
            pool.wait_ge(iota_done, 2)
            n = pool.value_load(n_rounds[0:1, 0:1], min_val=1, max_val=ECOLS // 8)
            with pool.Fori(0, n) as r:
                pool.wait_ge(idx_done, r * 4 + 2)
                pool.wait_ge(pgated, r)
                nc.gpsimd.tensor_tensor(pgate[:, 1:2], pgate[:, 0:1], pgate[:, 0:1], ALU.add).then_inc(pgated, 1)
                for j in range(8):
                    nc.gpsimd.indirect_dma_start(out=gs[:, 0, j, :], out_offset=None, in_=srcD,
                                                 in_offset=bass.IndirectOffsetOnAxis(ap=ix[:, 0, j:j + 1], axis=0)).then_inc(g_s[j], 16)
                    nc.gpsimd.indirect_dma_start(out=gd[:, 0, j, :], out_offset=None, in_=dstD,
                                                 in_offset=bass.IndirectOffsetOnAxis(ap=ix[:, 1, j:j + 1], axis=0)).then_inc(g_d[j], 16)

        @block.scalar
        def _(act):
            n = act.value_load(n_rounds[0:1, 0:1], min_val=1, max_val=ECOLS // 8)
            with act.Fori(0, n) as r:
                act.wait_ge(shifted, r + 1)
                act.wait_ge(spread, r)
                nc.scalar.activation(we[:, :, :], sl[:, :, :], ACT.Exp).then_inc(exped, 1)
            act.wait_ge(w_e, 2)
            nc.scalar.activation(ws[:, :, :], z[1][:, :, :], ACT.Exp).then_inc(w_ed, 1)
            nc.scalar.activation(wl[:, :, :], z[2][:, :, :], ACT.Exp).then_inc(w_ed, 1)
            act.wait_ge(f_sqrt, 1)
            nc.scalar.activation(root[:, :], stat[:, :], ACT.Sqrt).then_inc(f_root, 1)
            act.wait_ge(g_arg, 1)
            nc.scalar.activation(ge[:, :, :], scr[:, :, :], ACT.Exp).then_inc(g_exp, 1)

        @block.tensor
        def _(pe):
            pe.wait_ge(init, 1)
            nc.tensor.matmul(ps_a[0:TP, 0:HU], zf[:, 0:TP], zf[:, 0:HU], start=True, stop=False)
            nc.tensor.matmul(ps_b[0:TP, 0:HU], zf[:, 0:TP], zf[:, 0:HU], start=True, stop=False)
            n = pe.value_load(n_rounds[0:1, 0:1], min_val=1, max_val=ECOLS // 8)
            with pe.Fori(0, n) as r:
                pe.wait_ge(spread, r + 1)
                for j in range(8):
                    nc.tensor.matmul(ps_a[0:TP, 0:HU], oh_p[:, j, :], om[:, j, 0:HU], start=False, stop=False)
                    last = nc.tensor.matmul(ps_b[0:TP, 0:HU], oh_p[:, j, :], om[:, j, HU:2 * HU], start=False, stop=False)
                last.then_inc(sc_mm, 1)
            nc.tensor.matmul(ps_a[0:TP, 0:HU], zf[:, 0:TP], zf[:, 0:HU], start=False, stop=True)
            nc.tensor.matmul(ps_b[0:TP, 0:HU], zf[:, 0:TP], zf[:, 0:HU], start=False, stop=True).then_inc(opened, 1)

        @block.vector
        def _(dve):
            V = nc.vector
            V.memset(zf[:, :], 0.0).then_inc(init, 1)
            dve.wait_ge(iota_done, 1)
            n = dve.value_load(n_rounds[0:1, 0:1], min_val=1, max_val=ECOLS // 8)
            with dve.Fori(0, n) as r:
                col = bass.ds(r * 8, 8)
                st = Steps(dve, estep, r * EDGE_STEPS)
                V.tensor_copy(ix[:, 0, :], src_l[:, col]).then_inc(idx_done, 1)
                V.tensor_copy(ix[:, 1, :], dst_l[:, col]).then_inc(idx_done, 1)
                V.tensor_copy(up[:, 0, :], u_l[:, col]).then_inc(idx_done, 1)
                V.tensor_copy(up[:, 1, :], p_l[:, col]).then_inc(idx_done, 1)
                dve.wait_ge(idx_done, r * 4 + 4)
                dve.wait_ge(sc_mm, r)
                st.mark(V.tensor_tensor(oh_p[:, :, :], up[:, 1, :].unsqueeze(2).to_broadcast([128, 8, TP]),
                                        iota[:, :].unsqueeze(1).to_broadcast([128, 8, TP]), ALU.is_equal))
                st.link(V.tensor_tensor(oh_u[:, :, :], up[:, 0, :].unsqueeze(2).to_broadcast([128, 8, UNITS]),
                                        iota[:, 0:UNITS].unsqueeze(1).to_broadcast([128, 8, UNITS]), ALU.is_equal))
                for j in range(8):
                    dve.wait_ge(g_s[j], r * 16 + 16)
                    dve.wait_ge(g_d[j], r * 16 + 16)
                st.link(V.tensor_tensor(sc[:, :, :], gs[:, 0, :, GF:NODE_F], gd[:, 0, :, 0:GH], ALU.add))
                st.link(V.scalar_tensor_tensor(sl[:, :, :], sc[:, :, :], 0.2, sc[:, :, :], ALU.mult, ALU.max))
                V.tensor_tensor(sl[:, :, :], sl[:, :, :], gd[:, 0, :, GH:2 * GH], ALU.subtract).then_inc(shifted, 1)
                dve.wait_ge(exped, r + 1)
                st.mark(V.tensor_tensor(msg[:, :, 0:GF].rearrange("p j (h e) -> p j h e", h=GH),
                                        gs[:, 0, :, 0:GF].rearrange("p j (h e) -> p j h e", h=GH),
                                        we[:, :, :].unsqueeze(3).to_broadcast([128, 8, GH, GE]), ALU.mult))
                st.link(V.tensor_copy(msg[:, :, GF:NODE_F], we[:, :, :]))
                for j in range(8):
                    ins = V.tensor_tensor(om[:, j, :].rearrange("p (u f) -> p u f", u=UNITS), bc_free(oh_u[:, j, :], 128, NODE_F),
                                          msg[:, j, :].unsqueeze(1).to_broadcast([128, UNITS, NODE_F]), ALU.mult)
                    st.mark(ins) if j < 7 else ins.then_inc(spread, 1)
                dve.wait_ge(spread, r + 1)
                st.settle()
                assert st.n == EDGE_STEPS, st.n
            st = Steps(dve, fstep)
            asrc, adst, m = TS[:, :, GF:NODE_F], TD[:, :, 0:GH], TD[:, :, GH:2 * GH]
            st.link(V.tensor_tensor(z[0][:, :, :], asrc, adst, ALU.add))
            st.link(V.scalar_tensor_tensor(z[1][:, :, :], z[0][:, :, :], 0.2, z[0][:, :, :], ALU.mult, ALU.max))
            V.tensor_tensor(z[1][:, :, :], z[1][:, :, :], m, ALU.subtract).then_inc(w_e, 1)
            st.link(V.tensor_tensor(z[0][:, :, :], adst, lastr[:, GF:NODE_F].unsqueeze(1).to_broadcast([TP, UNITS, GH]), ALU.add))
            st.link(V.scalar_tensor_tensor(z[2][:, :, :], z[0][:, :, :], 0.2, z[0][:, :, :], ALU.mult, ALU.max))
            st.link(V.tensor_tensor(z[2][:, :, :], z[2][:, :, :], m, ALU.subtract))
            V.tensor_scalar(z[2][:, :, :], z[2][:, :, :], 0.0, None, ALU.min).then_inc(w_e, 1)
            dve.wait_ge(w_ed, 2)
            st.link(V.tensor_tensor(wl[:, :, :], wl[:, :, :], bc_free(hist[:, :], TP, GH), ALU.mult))
            dve.wait_ge(opened, 1)
            st.mark(V.tensor_copy(acc[:, 0:UNITS // 2, :].rearrange("p u f -> p (u f)"), ps_a[0:TP, 0:HU]))
            st.link(V.tensor_copy(acc[:, UNITS // 2:UNITS, :].rearrange("p u f -> p (u f)"), ps_b[0:TP, 0:HU]))
            num, den = acc[:, :, 0:GF], acc[:, :, GF:NODE_F]
            four = lambda ap: ap.rearrange("p u (h e) -> p u h e", h=GH)
            hrow = lastr[:, 0:GF].unsqueeze(1).to_broadcast([TP, UNITS, GF])
            st.link(V.tensor_tensor(den, den, ws[:, :, :], ALU.add))
            st.link(V.tensor_tensor(den, den, wl[:, :, :], ALU.add))
            for h in range(GH):
                hs = slice(h * GE, (h + 1) * GE)
                st.link(V.tensor_tensor(big[:, :, hs], TS[:, :, hs], bc_free(ws[:, :, h], TP, GE), ALU.mult))
            st.link(V.tensor_tensor(num, num, big[:, :, :], ALU.add))
            for h in range(GH):
                hs = slice(h * GE, (h + 1) * GE)
                st.link(V.tensor_tensor(big[:, :, hs], hrow[:, :, hs], bc_free(wl[:, :, h], TP, GE), ALU.mult))
            st.link(V.tensor_tensor(num, num, big[:, :, :], ALU.add))
            st.link(V.tensor_scalar(z[0][:, :, :], den, 1e-16, None, ALU.add))
            st.link(V.reciprocal(z[1][:, :, :], z[0][:, :, :]))
            for h in range(GH):
                hs = slice(h * GE, (h + 1) * GE)
                st.link(V.tensor_tensor(big[:, :, hs], acc[:, :, hs], bc_free(z[1][:, :, h], TP, GE), ALU.mult))

            def row(n):
                return rows[n][:, :].unsqueeze(1).to_broadcast([TP, UNITS, GF])

            st.link(V.tensor_tensor(big[:, :, :], big[:, :, :], row("b_gat"), ALU.add))
            st.link(V.tensor_reduce(stat[:, :], big[:, :, :], op=ALU.add, axis=AX.X))
            st.link(V.tensor_scalar(stat[:, :], stat[:, :], 1.0 / GF, None, ALU.mult))
            st.link(V.tensor_tensor(big[:, :, :], big[:, :, :], bc_free(stat[:, :], TP, GF), ALU.subtract))
            st.link(V.tensor_tensor(num, big[:, :, :], big[:, :, :], ALU.mult))
            st.link(V.tensor_reduce(stat[:, :], num, op=ALU.add, axis=AX.X))
            V.tensor_scalar(stat[:, :], stat[:, :], 1.0 / GF, EPS, ALU.mult, ALU.add).then_inc(f_sqrt, 1)
            dve.wait_ge(f_root, 1)
            st.link(V.reciprocal(stat[:, :], root[:, :]))
            st.link(V.tensor_tensor(big[:, :, :], big[:, :, :], bc_free(stat[:, :], TP, GF), ALU.mult))
            st.link(V.tensor_tensor(big[:, :, :], big[:, :, :], row("ln_gamma"), ALU.mult))
            st.link(V.tensor_tensor(big[:, :, :], big[:, :, :], row("ln_beta"), ALU.add))
            for e in range(GE):
                st.mark(V.tensor_reduce(scr[:, e, :], big[:, :, e:GF:GE], op=ALU.add, axis=AX.X))
            st.settle()
            st.link(V.tensor_scalar(scr[:, :, :], scr[:, :, :], 1.0 / GH, None, ALU.mult))
            st.link(V.memset(rank[:, :, :], 0.0))
            for e in range(GE):
                for o in range(GE):
                    if o != e:
                        st.link(V.tensor_tensor(cmp_[:, :], scr[:, o, :], scr[:, e, :], ALU.is_ge if o < e else ALU.is_gt))
                        st.link(V.tensor_tensor(rank[:, e, :], rank[:, e, :], cmp_[:, :], ALU.add))
            st.link(V.tensor_tensor(top[:, :], scr[:, 0, :], scr[:, 1, :], ALU.max))
            for e in (2, 3):
                st.link(V.tensor_tensor(top[:, :], top[:, :], scr[:, e, :], ALU.max))
            V.tensor_tensor(scr[:, :, :], scr[:, :, :], top[:, :].unsqueeze(1).to_broadcast([TP, GE, UNITS]),
                            ALU.subtract).then_inc(g_arg, 1)
            dve.wait_ge(g_exp, 1)
            st.link(V.scalar_tensor_tensor(ge[:, :, :], rank[:, :, :], 2.0, ge[:, :, :], ALU.is_lt, ALU.mult))
            st.link(V.tensor_tensor(top[:, :], ge[:, 0, :], ge[:, 1, :], ALU.add))
            for e in (2, 3):
                st.link(V.tensor_tensor(top[:, :], top[:, :], ge[:, e, :], ALU.add))
            st.link(V.reciprocal(cmp_[:, :], top[:, :]))
            st.link(V.tensor_tensor(gates[:, :, :], ge[:, :, :], cmp_[:, :].unsqueeze(1).to_broadcast([TP, GE, UNITS]), ALU.mult))


MAX_STEPS = 2 * (1 + GH + GH - 1 + 1)
EDGE_STEPS = 2 + 2 + 2 + 7


def expert_stage(nc, io, H, xT, gates, out):
    HID = 2 * DIM
    with ExitStack() as ctx:
        s = Space(nc, ctx, "ffn")
        w1 = s.sb("w1", [AUG, GE, HID])
        w2 = s.sb("w2", [HID, GE, DIM])
        b2 = s.sb("b2", [1, GE, DIM])
        one = s.sb("one", [1, TP])
        xb = s.sb("tokens_batch", [AUG, PAD])
        hh = s.sb("hidden", [HID, 2, PAD])
        acc = s.sb("sum", [TP, TILES, DIM])
        tmp = s.sb("gated", [TP, TILES, DIM])
        ps_u = s.ps("up", (128, 3, 512))
        ps_d = [s.ps(f"down{k}", (128, 1024)) for k in range(2)]
        w_in, init, xcp, up, act_done, down, gated, summed, st_a, started = (
            s.sem(n) for n in ("w_in", "init", "x_copied", "up", "act_done", "down", "gated", "summed", "stored", "started"))
        block = ctx.enter_context(nc.Block())

        @block.sync
        def _(sp):
            sp.dma_start(w1[0:DIM, :, :], io["L1_ffn_W1"].rearrange("e c f -> c e f")).then_inc(w_in, 16)
            sp.dma_start(w1[DIM:AUG, :, :], io["L1_ffn_b1"].unsqueeze(0)).then_inc(w_in, 16)
            sp.dma_start(w2[:, :, :], io["L1_ffn_W2"].rearrange("e c f -> c e f")).then_inc(w_in, 16)
            sp.dma_start(b2[:, :, :], io["L1_ffn_b2"].unsqueeze(0)).then_inc(w_in, 16)
            with sp.Fori(0, BATCH) as b:
                sp.wait_ge(st_a, b * 16)
                sp.wait_ge(started, b * 16)
                sp.wait_ge(summed, (b + 1) * (GE + 1))
                ob = out[bass.ds(b, 1)].rearrange("a n d -> (a n) d")
                sp.dma_start(ob[0:8 * TP, :].rearrange("(t p) d -> p t d", p=TP), acc[:, 0:8, :]).then_inc(st_a, 16)
                sp.dma_start(ob[8 * TP:SEQ, :], acc[0:TP - 1, 8, :]).then_inc(started, 16)
            sp.wait_ge(st_a, BATCH * 16)
            sp.wait_ge(started, BATCH * 16)

        @block.gpsimd
        def _(pool):
            with pool.Fori(0, BATCH) as b:
                pool.wait_ge(up, b * GE)
                nc.gpsimd.tensor_copy(xb[:, :], xT[:, bass.ds(b, 1), :].rearrange("p a n -> p (a n)")).then_inc(xcp, 1)

        @block.tensor
        def _(pe):
            pe.wait_ge(w_in, 64)
            pe.wait_ge(init, 1)
            with pe.Fori(0, BATCH) as b:
                pe.wait_ge(xcp, b + 1)

                def go_up(e):
                    n = b * GE + e
                    pe.wait_ge(act_done, n)
                    for c in range(3):
                        last = nc.tensor.matmul(ps_u[:, c, 0:HALF], w1[:, e, :], xb[:, c * HALF:(c + 1) * HALF], start=True, stop=True)
                    last.then_inc(up, 1)

                def go_down(e):
                    n = b * GE + e
                    pe.wait_ge(act_done, n + 1)
                    if e >= 2:
                        pe.wait_ge(gated, n - 1)
                    else:
                        pe.wait_ge(gated, b * GE)
                    for t in range(TILES):
                        dst = ps_d[e % 2][0:TP, t * DIM:(t + 1) * DIM]
                        nc.tensor.matmul(dst, hh[:, e % 2, t * TP:(t + 1) * TP], w2[:, e, :], start=True, stop=False)
                        last = nc.tensor.matmul(dst, one[:, :], b2[:, e, :], start=False, stop=True)
                    last.then_inc(down, 1)

                go_up(0)
                for e in range(GE):
                    if e + 1 < GE:
                        go_up(e + 1)
                    go_down(e)

        @block.scalar
        def _(act):
            with act.Fori(0, BATCH) as b:
                for e in range(GE):
                    n = b * GE + e
                    act.wait_ge(up, n + 1)
                    act.wait_ge(down, n - 1 if e >= 2 else b * GE)
                    nc.scalar.activation(hh[:, e % 2, :].rearrange("p (c n) -> p c n", c=3), ps_u[:, :, 0:HALF],
                                         ACT.Gelu).then_inc(act_done, 1)

        @block.vector
        def _(dve):
            nc.vector.memset(one[:, :], 1.0).then_inc(init, 1)
            with dve.Fori(0, BATCH) as b:
                s0 = b * (GE + 1)
                dve.wait_ge(st_a, b * 16)
                dve.wait_ge(started, b * 16)
                nc.vector.tensor_copy(acc[:, :, :], H[:, bass.ds(b * TILES, TILES), :]).then_inc(summed, 1)
                for e in range(GE):
                    n = b * GE + e
                    dve.wait_ge(down, n + 1)
                    dve.wait_ge(summed, s0 + e + 1)
                    nc.vector.tensor_tensor(tmp[:, :, :], ps_d[e % 2][0:TP, 0:TILES * DIM].rearrange("p (t d) -> p t d", t=TILES),
                                            gates[:, e, bass.ds(b * TILES, TILES)].unsqueeze(2).to_broadcast([TP, TILES, DIM]),
                                            ALU.mult).then_inc(gated, 1)
                    dve.wait_ge(gated, n + 1)
                    nc.vector.tensor_tensor(acc[:, :, :], acc[:, :, :], tmp[:, :, :], ALU.add).then_inc(summed, 1)


def lay_out(inputs):
    arrays = {n: np.ascontiguousarray(a) for n, a in inputs.items()}
    arrays["L0_tok_gammaT"] = np.ascontiguousarray(arrays.pop("L0_tok_d_gamma_batched").T)
    arrays["L0_ffn_Wq_pkT"] = np.ascontiguousarray(arrays.pop("L0_ffn_Wq_pk").T)
    arrays["L0_ffn_pk_keysT"] = np.ascontiguousarray(arrays.pop("L0_ffn_pk_keys").transpose(0, 2, 3, 1))
    arrays["L0_ffn_tables"] = np.concatenate([arrays.pop("L0_ffn_keys_table"), arrays.pop("L0_ffn_values_table")], axis=1)
    for n in "qkvo":
        arrays[f"L1_attn_W{n}T"] = np.ascontiguousarray(arrays.pop(f"L1_attn_W{n}").T)
    arrays["L0_tok_prelu_a"] = arrays["L0_tok_prelu_a"].reshape(1, 1)
    return arrays


def window_layer(nc, io, H, xT, ident):
    norm_stage(nc, "norm_win", H, xT, ident)
    window_stage(nc, io, H, xT, ident)


def memory_layer(nc, io, H, xT, ident):
    norm_stage(nc, "norm_mem", H, xT, ident)
    e01D = nc.dram_tensor("scratch_e01", [UNITS, TP, GROUPS * PK], F32).ap()
    with nc.sbuf_tensor("theta", [TP, UNITS, PH], F32) as theta, nc.sbuf_tensor("inv_z", [TP, UNITS, PH], F32) as inv_z:
        select_stage(nc, io, xT, e01D, theta, inv_z)
        memory_stage(nc, io, H, xT, ident, e01D, theta, inv_z)


def heads_layer(nc, io, H, xT, ident):
    norm_stage(nc, "norm_mha", H, xT, ident)
    heads_stage(nc, io, H, xT, ident)


def expert_layer(nc, io, H, xT, ident, out):
    norm_stage(nc, "norm_gat", H, xT, ident)
    maskD = nc.dram_tensor("scratch_mask", [JUNK + 128, 1], BF16).ap()
    with ExitStack() as ctx:
        s = Space(nc, ctx, "moe")
        slots = (s.sb("slot_src", [128, ECOLS], I32), s.sb("slot_dst", [128, ECOLS], I32),
                 s.sb("slot_tile", [128, ECOLS]), s.sb("slot_row", [128, ECOLS]))
        n_rounds, clipped = s.sb("n_rounds", [1, 1], I32), s.sb("clipped_count", [TP, UNITS])
        gates = s.sb("gates", [TP, GE, UNITS])
        edge_stage(nc, io, ident, maskD, slots, n_rounds, clipped)
        graph_stage(nc, io, H, xT, maskD, slots, n_rounds, clipped, gates)
        expert_stage(nc, io, H, xT, gates, out)


def program(nc, io, out):
    with ExitStack() as ctx:
        H = ctx.enter_context(nc.sbuf_tensor("hidden", [TP, UNITS, DIM], F32))
        ident = ctx.enter_context(nc.sbuf_tensor("identity", [128, 128], F32))
        ones = ctx.enter_context(nc.sbuf_tensor("ones", [1, 128], F32))
        constants_stage(nc, ident, ones)
        tok_stage(nc, io, H, ident)
        xT = ctx.enter_context(nc.sbuf_tensor("normedT", [AUG, BATCH, PAD], F32))
        window_layer(nc, io, H, xT, ident)
        memory_layer(nc, io, H, xT, ident)
        heads_layer(nc, io, H, xT, ident)
        expert_layer(nc, io, H, xT, ident, out)


def kernel(**inputs):
    import concourse.bacc as bacc
    from concourse.bass_utils import run_bass_kernel_spmd

    nc = bacc.Bacc("TRN2", target_bir_lowering=False, num_devices=1)
    arrays, io = {}, {}
    for name, a in lay_out(inputs).items():
        arrays[f"in_{name}_dram"] = a
        io[name] = nc.dram_tensor(f"in_{name}_dram", a.shape, mybir.dt.from_np(a.dtype), kind="ExternalInput").ap()
    out = nc.dram_tensor("out_0_dram", (BATCH, SEQ, DIM), F32, kind="ExternalOutput").ap()
    program(nc, io, out)
    r = run_bass_kernel_spmd(nc, [arrays], core_ids=[0])
    return r.results[0]["out_0_dram"]
```

```python
import concourse.bass as bass
from concourse import mybir
from contextlib import ExitStack
import numpy as np

F32 = mybir.dt.float32
BF16 = mybir.dt.bfloat16
I32 = mybir.dt.int32
ALU = mybir.AluOpType
ACT = mybir.ActivationFunctionType
AX = mybir.AxisListType

BATCH, TOK, DIM = 4, 1024, 64
SEQ = TOK + 1
TP = 114
TILES = 9
PAD = TP * TILES
UNITS = BATCH * TILES
NODES = BATCH * PAD
AUG = DIM + 1
HALF = 3 * TP
EPS = 1e-5


class Steps:

    def __init__(self, eng, sem, base=0):
        self.eng, self.sem, self.base, self.n = eng, sem, base, 0

    def mark(self, ins):
        self.n += 1
        ins.then_inc(self.sem, 1)

    def settle(self):
        self.eng.wait_ge(self.sem, self.base + self.n)

    def link(self, ins):
        self.mark(ins)
        self.settle()


class Space:

    def __init__(self, nc, ctx, stage):
        self.nc, self.ctx, self.stage = nc, ctx, stage
        self.sems = []
        ctx.callback(self.close)

    def close(self):
        if self.sems:
            self.nc.clear_and_free_semaphores(self.sems)
            self.nc.all_engine_barrier()

    def sb(self, name, shape, dtype=F32):
        return self.ctx.enter_context(self.nc.sbuf_tensor(f"{self.stage}_{name}", shape, dtype))

    def ps(self, name, shape=(128, 1024)):
        return self.ctx.enter_context(self.nc.psum_tensor(f"{self.stage}_{name}", list(shape), F32))

    def sem(self, name):
        handle = self.nc.alloc_semaphore(name=f"{self.stage}_{name}")
        self.sems.append(handle)
        return handle


def bc_free(ap, parts, inner):
    return ap.unsqueeze(2).to_broadcast([parts, ap.shape[1], inner])


def turn(nc, out, in_, identity, after_wait=False):
    if after_wait:
        return nc.tensor.matmul(out, in_, identity, start=True, stop=True)
    return nc.tensor.transpose(out, in_, identity)


def constants_stage(nc, ident, ones):
    with ExitStack() as ctx:
        s = Space(nc, ctx, "const")
        done = s.sem("done")
        block = ctx.enter_context(nc.Block())

        @block.gpsimd
        def _(pool):
            nc.gpsimd.memset(ident[:, :], 0.0).then_inc(done, 1)
            nc.gpsimd.memset(ones[:, :], 1.0).then_inc(done, 1)
            pool.wait_ge(done, 2)
            nc.gpsimd.affine_select(out=ident[:, :], in_=ident[:, :], compare_op=ALU.not_equal,
                                    fill=1.0, base=0, pattern=[[-1, 128]],
                                    channel_multiplier=1).then_inc(done, 1)
            pool.wait_ge(done, 3)


def tok_stage(nc, io, H, ident):
    ST = TOK // 128
    with ExitStack() as ctx:
        s = Space(nc, ctx, "tok")
        gT = s.sb("gammaT", [128, ST, TOK])
        xb = s.sb("x", [128, ST, DIM])
        xT = s.sb("xT", [AUG, TOK])
        qT = s.sb("qT", [DIM, TOK])
        kT = s.sb("kT", [DIM, TOK])
        v = s.sb("v", [128, ST * DIM])
        pT = s.sb("weightedT", [128, 2, TOK])
        retT = s.sb("retainedT", [AUG, PAD])
        neg = s.sb("negative", [TP, TILES * DIM])
        wq, wk, wv, wo = (s.sb(n, [AUG, DIM]) for n in ("wq", "wk", "wv", "wo"))
        slope = s.sb("slope", [TP, 1])
        psA, psB, psC, psD = (s.ps(n) for n in ("psA", "psB", "psC", "psD"))
        w_in, g_in, x_in, init = s.sem("w_in"), s.sem("g_in"), s.sem("x_in"), s.sem("init")
        x_tr, xT_done, qkv_mm, q_done, k_done, v_done = (
            s.sem(n) for n in ("x_tr", "xT_done", "qkv_mm", "q_done", "k_done", "v_done"))
        sc_mm, weighted, ret_mm, ret_done, y_mm = (
            s.sem(n) for n in ("sc_mm", "weighted", "ret_mm", "ret_done", "y_mm"))
        neg_done, h_done, cls_in = s.sem("neg_done"), s.sem("h_done"), s.sem("cls_in")
        block = ctx.enter_context(nc.Block())
        x_dram = io["x"].rearrange("b c (s p) d -> (b c) p s d", p=128)

        @block.sync
        def _(sp):
            sp.dma_start(xb[:, :, :], x_dram[0]).then_inc(x_in, 16)
            for w, n in ((wq, "q"), (wk, "k"), (wv, "v"), (wo, "o")):
                sp.dma_start(w[0:DIM, :], io[f"L0_tok_W{n}"]).then_inc(w_in, 16)
                sp.dma_start(w[DIM:AUG, :], io[f"L0_tok_b{n}"].unsqueeze(0)).then_inc(w_in, 16)
            sp.dma_start(slope[:, :], io["L0_tok_prelu_a"].to_broadcast([TP, 1])).then_inc(w_in, 16)
            sp.dma_start(gT[:, :, :], io["L0_tok_gammaT"].rearrange("(s p) t -> p s t", p=128)).then_inc(g_in, 16)
            with sp.Fori(1, BATCH) as b:
                sp.wait_ge(x_tr, b)
                sp.dma_start(xb[:, :, :], x_dram[bass.ds(b, 1)].rearrange("a p s d -> (a p) s d")).then_inc(x_in, 16)
            sp.wait_ge(h_done, BATCH)
            sp.dma_start(H[0:1, 0:UNITS:TILES, :], io["cls_tok"].to_broadcast([1, BATCH, DIM])).then_inc(cls_in, 16)
            sp.wait_ge(cls_in, 16)

        @block.tensor
        def _(pe):
            pe.wait_ge(w_in, 16 * 9)
            pe.wait_ge(init, 2)
            with pe.Fori(0, BATCH) as b:
                pe.wait_ge(x_in, b * 16 + 16)
                pe.wait_ge(weighted, b * ST)
                for t in range(ST):
                    last = turn(nc, psA[0:DIM, t * 128:(t + 1) * 128], xb[:, t, :], ident[:, :], after_wait=t == 0)
                last.then_inc(x_tr, 1)
                pe.wait_ge(xT_done, b + 1)
                pe.wait_ge(ret_done, b)
                pe.wait_ge(h_done, b)
                for c in range(2):
                    cols = slice(c * 512, (c + 1) * 512)
                    nc.tensor.matmul(psB[0:DIM, cols], wq[:, :], xT[:, cols], start=True, stop=True)
                    nc.tensor.matmul(psC[0:DIM, cols], wk[:, :], xT[:, cols], start=True, stop=True)
                for t in range(ST):
                    last = nc.tensor.matmul(psD[:, t * DIM:(t + 1) * DIM], xT[:, t * 128:(t + 1) * 128], wv[:, :],
                                            start=True, stop=True)
                last.then_inc(qkv_mm, 1)
                pe.wait_ge(q_done, b + 1)
                pe.wait_ge(k_done, b + 1)
                for t in range(ST + 1):
                    if t < ST:
                        if t >= 2:
                            pe.wait_ge(weighted, b * ST + t - 1)
                        for c in range(2):
                            cols = slice(c * 512, (c + 1) * 512)
                            last = nc.tensor.matmul((psA, psB)[t % 2][:, cols], kT[:, t * 128:(t + 1) * 128],
                                                    qT[:, cols], start=True, stop=True)
                        last.then_inc(sc_mm, 1)
                    if t == 0:
                        pe.wait_ge(v_done, b + 1)
                    else:
                        u = t - 1
                        pe.wait_ge(weighted, b * ST + u + 1)
                        for c in range(2):
                            cols = slice(c * 512, (c + 1) * 512)
                            last = nc.tensor.matmul(psC[0:DIM, cols], v[:, u * DIM:(u + 1) * DIM], pT[:, u % 2, cols],
                                                    start=(u == 0), stop=(u == ST - 1))
                        last.then_inc(ret_mm, 1)
                pe.wait_ge(ret_done, b + 1)
                for j in range(TILES):
                    last = nc.tensor.matmul(psD[0:TP, j * DIM:(j + 1) * DIM], retT[:, j * TP:(j + 1) * TP], wo[:, :],
                                            start=True, stop=True)
                last.then_inc(y_mm, 1)

        @block.scalar
        def _(act):
            with act.Fori(0, BATCH) as b:
                act.wait_ge(x_tr, b + 1)
                act.wait_ge(qkv_mm, b)
                nc.scalar.activation(xT[0:DIM, :], psA[0:DIM, :], ACT.Copy).then_inc(xT_done, 1)
                act.wait_ge(qkv_mm, b + 1)
                act.wait_ge(ret_mm, b * ST)
                nc.scalar.activation(v[:, :], psD[:, 0:ST * DIM], ACT.Copy).then_inc(v_done, 1)
                act.wait_ge(ret_mm, b * ST + ST)
                act.wait_ge(y_mm, b)
                nc.scalar.activation(retT[0:DIM, 1:1 + TOK], psC[0:DIM, :], ACT.Copy).then_inc(ret_done, 1)

        @block.vector
        def _(dve):
            nc.vector.memset(xT[DIM:AUG, :], 1.0).then_inc(init, 1)
            nc.vector.memset(retT[DIM:AUG, :], 1.0).then_inc(init, 1)
            nc.vector.memset(retT[0:DIM, 0:1], 0.0).then_inc(init, 1)
            nc.vector.memset(retT[0:DIM, PAD - 1:PAD], 0.0).then_inc(init, 1)
            dve.wait_ge(g_in, 16)
            dve.wait_ge(w_in, 16 * 9)
            with dve.Fori(0, BATCH) as b:
                dve.wait_ge(qkv_mm, b + 1)
                dve.wait_ge(sc_mm, b * ST)
                nc.vector.tensor_copy(qT[:, :], psB[0:DIM, :]).then_inc(q_done, 1)
                nc.vector.tensor_copy(kT[:, :], psC[0:DIM, :]).then_inc(k_done, 1)
                for t in range(ST):
                    dve.wait_ge(sc_mm, b * ST + t + 1)
                    if t >= 2:
                        dve.wait_ge(ret_mm, b * ST + t - 1)
                    nc.vector.tensor_tensor(pT[:, t % 2, :], (psA, psB)[t % 2][:, :], gT[:, t, :],
                                            ALU.mult).then_inc(weighted, 1)
                dve.wait_ge(y_mm, b + 1)
                dve.wait_ge(h_done, b)
                nc.vector.tensor_scalar(neg[:, :], psD[0:TP, 0:TILES * DIM], 0.0, slope[:, 0:1],
                                        ALU.min, ALU.mult).then_inc(neg_done, 1)
                dve.wait_ge(neg_done, b + 1)
                nc.vector.scalar_tensor_tensor(
                    H[:, bass.ds(b * TILES, TILES), :].rearrange("p t d -> p (t d)"), psD[0:TP, 0:TILES * DIM], 0.0,
                    neg[:, :], ALU.max, ALU.add).then_inc(h_done, 1)


def norm_stage(nc, name, H, xT, ident):
    with ExitStack() as ctx:
        s = Space(nc, ctx, name)
        stat = s.sb("stat", [TP, UNITS])
        rstd = s.sb("rstd", [TP, UNITS])
        root = s.sb("root", [TP, UNITS])
        xc = s.sb("centred", [TP, UNITS, DIM])
        sq = s.sb("square", [TP, UNITS, DIM])
        xn = s.sb("normed", [TP, 2, TILES, DIM])
        ps = [s.ps(f"ps{k}", (128, 3, 512)) for k in range(2)]
        step, var_done, root_done = s.sem("step"), s.sem("var_done"), s.sem("root_done")
        normed, turned, copied = s.sem("normed"), s.sem("turned"), s.sem("copied")
        block = ctx.enter_context(nc.Block())

        @block.vector
        def _(dve):
            st = Steps(dve, step)
            st.mark(nc.vector.memset(xT[DIM:AUG, :, :], 1.0))
            st.link(nc.vector.tensor_reduce(stat[:, :], H[:, :, :], op=ALU.add, axis=AX.X))
            st.link(nc.vector.tensor_scalar(stat[:, :], stat[:, :], 1.0 / DIM, None, ALU.mult))
            st.link(nc.vector.tensor_tensor(xc[:, :, :], H[:, :, :], bc_free(stat[:, :], TP, DIM), ALU.subtract))
            st.link(nc.vector.tensor_tensor(sq[:, :, :], xc[:, :, :], xc[:, :, :], ALU.mult))
            st.link(nc.vector.tensor_reduce(stat[:, :], sq[:, :, :], op=ALU.add, axis=AX.X))
            nc.vector.tensor_scalar(rstd[:, :], stat[:, :], 1.0 / DIM, EPS, ALU.mult, ALU.add).then_inc(var_done, 1)
            dve.wait_ge(root_done, 1)
            st.link(nc.vector.reciprocal(rstd[:, :], root[:, :]))
            with dve.Fori(0, BATCH // 2) as i:
                for k in range(2):
                    dve.wait_ge(turned, i * 2)
                    nc.vector.tensor_tensor(
                        xn[:, k, :, :], xc[:, bass.ds(i * 2 * TILES + k * TILES, TILES), :],
                        rstd[:, bass.ds(i * 2 * TILES + k * TILES, TILES)].unsqueeze(2).to_broadcast([TP, TILES, DIM]),
                        ALU.mult).then_inc(normed, 1)

        @block.tensor
        def _(pe):
            with pe.Fori(0, BATCH // 2) as i:
                for k in range(2):
                    pe.wait_ge(normed, i * 2 + k + 1)
                    pe.wait_ge(copied, i * 2)
                    for t in range(TILES):
                        last = turn(nc, ps[k][0:DIM, t // 3, t % 3 * TP:(t % 3 + 1) * TP],
                                    xn[:, k, t, :], ident[0:TP, 0:TP], after_wait=t == 0)
                    last.then_inc(turned, 1)

        @block.scalar
        def _(act):
            act.wait_ge(var_done, 1)
            nc.scalar.activation(root[:, :], rstd[:, :], ACT.Sqrt).then_inc(root_done, 1)
            with act.Fori(0, BATCH // 2) as i:
                for k in range(2):
                    act.wait_ge(turned, i * 2 + k + 1)
                    nc.scalar.activation(
                        xT[0:DIM, bass.ds(i * 2 + k, 1), :].rearrange("p b (c n) -> p (b c) n", c=3),
                        ps[k][0:DIM, :, 0:HALF], ACT.Copy).then_inc(copied, 1)
            act.wait_ge(copied, BATCH)


WIN, WH, WHD = 64, 4, 16
LEFT = WIN - 1 - WIN // 2
EXT = PAD + WIN - 1
WSPAN = TP + WIN - 1
FAR = -1e30
MASK_VAL = -100.0


def window_stage(nc, io, H, xT, ident):
    k_rest = WSPAN - 128
    qD = nc.dram_tensor("scratch_win_q", [UNITS, 128, TP], F32).ap()
    kD = nc.dram_tensor("scratch_win_k", [UNITS, 128, WSPAN], F32).ap()
    xD = nc.dram_tensor("scratch_win_x", [UNITS, AUG, WSPAN], F32).ap()
    bD = nc.dram_tensor("scratch_win_bias", [WH, TP * WSPAN], F32).ap()
    bias_ctx = ExitStack()
    sb0 = Space(nc, bias_ctx, "win")
    bias = sb0.sb("bias", [TP, WH, WSPAN])
    wv = sb0.sb("wv", [AUG, DIM])
    wp = sb0.sb("wp", [AUG, DIM])
    with ExitStack() as ctx:
        s = Space(nc, ctx, "winp")
        wq = s.sb("wq", [AUG, 128])
        wk = s.sb("wk", [AUG, 128])
        xE = s.sb("xE", [AUG, EXT])
        qT = s.sb("qT", [128, PAD])
        kT = s.sb("kT", [128, EXT])
        far = s.sb("far", [TP, WH, WSPAN])
        psq, psk = s.ps("psq", (128, 3, 512)), s.ps("psk", (128, 3, 512))
        init, w_in, b_fill, b_in, ext, proj, q_out, k_out = (
            s.sem(n) for n in ("init", "w_in", "b_fill", "b_in", "ext", "proj", "q_out", "k_out"))
        x_st, q_st, k_st = s.sem("x_stored"), s.sem("q_stored"), s.sem("k_stored")
        block = ctx.enter_context(nc.Block())
        w3, b3 = io["L0_attn_W_qkv"], io["L0_attn_b_qkv"].unsqueeze(0)

        @block.vector
        def _(dve):
            nc.vector.memset(wq[:, :], 0.0).then_inc(init, 1)
            nc.vector.memset(wk[:, :], 0.0).then_inc(init, 1)
            nc.vector.memset(far[:, :, :], FAR).then_inc(init, 1)
            dve.wait_ge(init, 3)
            nc.vector.memset(wq[DIM:AUG, :].rearrange("p (h c) -> p h c", h=WH)[:, :, 0:1], 1.0).then_inc(init, 1)
            with dve.Fori(0, BATCH) as b:
                dve.wait_ge(x_st, b * 16)
                dve.wait_ge(proj, b)
                xb = xT[:, bass.ds(b, 1), :].rearrange("p b n -> p (b n)")
                nc.vector.tensor_copy(xE[:, LEFT:LEFT + SEQ], xb[:, 0:SEQ]).then_inc(ext, 1)
                nc.vector.tensor_copy(xE[:, 0:LEFT], xb[:, 0:1].to_broadcast([AUG, LEFT])).then_inc(ext, 1)
                nc.vector.tensor_copy(xE[:, LEFT + SEQ:EXT],
                                      xb[:, SEQ - 1:SEQ].to_broadcast([AUG, EXT - LEFT - SEQ])).then_inc(ext, 1)
                dve.wait_ge(proj, b + 1)
                dve.wait_ge(k_st, b * 16)
                nc.vector.tensor_copy(kT[:, :].rearrange("p (c n) -> p c n", c=3), psk[:, :, 0:EXT // 3]).then_inc(k_out, 1)
                dve.wait_ge(k_out, b * (1 + 2 * WH) + 1)
                for h in range(WH):
                    for cols in (slice(0, LEFT), slice(LEFT + SEQ, EXT)):
                        nc.vector.memset(kT[32 * h:32 * h + 1, cols], MASK_VAL / WHD ** -0.5).then_inc(k_out, 1)

        @block.sync
        def _(sp):
            sp.wait_ge(init, 4)
            for h in range(WH):
                sp.dma_start(wq[0:DIM, 32 * h + 1:32 * h + 1 + WHD], w3[:, h * WHD:(h + 1) * WHD]).then_inc(w_in, 16)
                sp.dma_start(wq[DIM:AUG, 32 * h + 1:32 * h + 1 + WHD], b3[:, h * WHD:(h + 1) * WHD]).then_inc(w_in, 16)
                kc = slice(DIM + h * WHD, DIM + (h + 1) * WHD)
                sp.dma_start(wk[0:DIM, 32 * h + 1:32 * h + 1 + WHD], w3[:, kc]).then_inc(w_in, 16)
                sp.dma_start(wk[DIM:AUG, 32 * h + 1:32 * h + 1 + WHD], b3[:, kc]).then_inc(w_in, 16)
            sp.dma_start(wv[0:DIM, :], w3[:, 2 * DIM:3 * DIM]).then_inc(w_in, 16)
            sp.dma_start(wv[DIM:AUG, :], b3[:, 2 * DIM:3 * DIM]).then_inc(w_in, 16)
            sp.dma_start(wp[0:DIM, :], io["L0_attn_W_proj"]).then_inc(w_in, 16)
            sp.dma_start(wp[DIM:AUG, :], io["L0_attn_b_proj"].unsqueeze(0)).then_inc(w_in, 16)
            sp.dma_start(bD.rearrange("h (p c) -> p h c", p=TP), far[:, :, :]).then_inc(b_fill, 16)
            sp.wait_ge(b_fill, 16)
            diagonal = bass.AP(tensor=bD.tensor, offset=0, ap=[[WSPAN + 1, TP], [TP * WSPAN, WH], [1, WIN]])
            sp.dma_start(diagonal, io["L0_attn_rel_bias"].rearrange("a h b w -> (a b) h w").to_broadcast([TP, WH, WIN]))\
              .then_inc(b_fill, 16)
            sp.wait_ge(b_fill, 32)
            sp.dma_start(bias[:, :, :], bD.rearrange("h (p c) -> p h c", p=TP)).then_inc(b_in, 16)

            def windows(a, parts):
                return bass.AP(tensor=a.tensor, offset=a.offset, ap=[a.ap[0], [TP, TILES], [1, WSPAN]])

            with sp.Fori(0, BATCH) as b:
                sp.wait_ge(ext, b * 3 + 3)
                sp.dma_start(xD[bass.ds(b * TILES, TILES)].rearrange("t p c -> p t c"),
                             windows(xE[:, :], AUG)).then_inc(x_st, 16)
                sp.wait_ge(q_out, b + 1)
                sp.dma_start(qD[bass.ds(b * TILES, TILES)].rearrange("t p c -> p t c"),
                             qT[:, :].rearrange("p (t c) -> p t c", t=TILES)).then_inc(q_st, 16)
                sp.wait_ge(k_out, (b + 1) * (1 + 2 * WH))
                sp.dma_start(kD[bass.ds(b * TILES, TILES)].rearrange("t p c -> p t c"),
                             windows(kT[:, :], 128)).then_inc(k_st, 16)
            sp.wait_ge(x_st, BATCH * 16)
            sp.wait_ge(q_st, BATCH * 16)
            sp.wait_ge(k_st, BATCH * 16)
            sp.wait_ge(b_in, 16)

        @block.tensor
        def _(pe):
            pe.wait_ge(w_in, 16 * 20)
            with pe.Fori(0, BATCH) as b:
                pe.wait_ge(ext, b * 3 + 3)
                pe.wait_ge(q_out, b)
                pe.wait_ge(k_out, b * (1 + 2 * WH))
                for c in range(3):
                    nc.tensor.matmul(psq[:, c, 0:HALF], wq[:, :], xE[:, LEFT + c * HALF:LEFT + (c + 1) * HALF],
                                     start=True, stop=True)
                    last = nc.tensor.matmul(psk[:, c, 0:EXT // 3], wk[:, :], xE[:, c * (EXT // 3):(c + 1) * (EXT // 3)],
                                            start=True, stop=True)
                last.then_inc(proj, 1)

        @block.scalar
        def _(act):
            with act.Fori(0, BATCH) as b:
                act.wait_ge(proj, b + 1)
                act.wait_ge(q_st, b * 16)
                nc.scalar.activation(qT[:, :].rearrange("p (c n) -> p c n", c=3), psq[:, :, 0:HALF],
                                     ACT.Copy).then_inc(q_out, 1)

    with ExitStack() as ctx:
        s = Space(nc, ctx, "wina")
        qw = s.sb("q", [128, 2, TP])
        kw = s.sb("k", [128, 2, WSPAN])
        xw = s.sb("x", [AUG, 2, WSPAN])
        S = s.sb("scores", [TP, 2, WH, WSPAN])
        P = s.sb("probs", [TP, 2, WH, WSPAN])
        PT = s.sb("probsT", [128, WH, TP])
        PT2 = s.sb("probsT2", [k_rest, WH, TP])
        v1 = s.sb("v1", [128, 2, DIM])
        v2 = s.sb("v2", [k_rest, 2, DIM])
        nmax = s.sb("neg_max", [TP, 2, WH])
        sums = s.sb("sums", [TP, 2, WH])
        rs = s.sb("inv_sums", [TP, 2, WH])
        o = s.sb("o", [TP, DIM])
        oT = s.sb("oT", [AUG, TP])
        psS = s.ps("psS", (128, WH, 512))
        psT = s.ps("psT", (128, 2, WH, 128))
        psV = s.ps("psV", (128, 512))
        psO = s.ps("psO", (128, 512))
        w_q = [s.sem(f"q_in{k}") for k in range(2)]
        w_k = [s.sem(f"k_in{k}") for k in range(2)]
        w_x = [s.sem(f"x_in{k}") for k in range(2)]
        init, scored, v_mm, v_done, biased, maxed = (s.sem(n) for n in ("init", "scored", "v_mm", "v_done", "biased", "maxed"))
        exped, turned, pt_done, pt2_done, inv, pv = (s.sem(n) for n in ("exped", "turned", "pt_done", "pt2_done", "inv", "pv"))
        o_done, o_turned, oT_done, y_mm, added = (s.sem(n) for n in ("o_done", "o_turned", "oT_done", "y_mm", "added"))
        block = ctx.enter_context(nc.Block())
        PAIRS = UNITS // 2

        @block.sync
        def _(sp):
            def load(u, k):
                sp.dma_start(qw[:, k, :], qD[bass.ds(u, 1)].rearrange("a p c -> (a p) c")).then_inc(w_q[k], 16)
                sp.dma_start(kw[:, k, :], kD[bass.ds(u, 1)].rearrange("a p c -> (a p) c")).then_inc(w_k[k], 16)
                sp.dma_start(xw[:, k, :], xD[bass.ds(u, 1)].rearrange("a p c -> (a p) c")).then_inc(w_x[k], 16)
            for k in range(2):
                load(k, k)
            with sp.Fori(0, PAIRS - 1) as i:
                for k in range(2):
                    sp.wait_ge(scored, i * 2 + k + 1)
                    sp.wait_ge(v_mm, i * 2 + k + 1)
                    load(i * 2 + 2 + k, k)

        @block.tensor
        def _(pe):
            def score(i, k):
                pe.wait_ge(w_q[k], i * 16 + 16)
                pe.wait_ge(w_k[k], i * 16 + 16)
                pe.wait_ge(biased, i * 2 + k)
                for h in range(WH):
                    last = nc.tensor.matmul(psS[0:TP, h, 0:WSPAN], qw[32 * h:32 * h + 32, k, :],
                                            kw[32 * h:32 * h + 32, k, :], start=True, stop=True)
                last.then_inc(scored, 1)
                pe.wait_ge(w_x[k], i * 16 + 16)
                pe.wait_ge(v_done, (i * 2 + k) * 2)
                nc.tensor.matmul(psV[:, 0:DIM], xw[:, k, 0:128], wv[:, :], start=True, stop=True)
                nc.tensor.matmul(psV[0:k_rest, DIM:2 * DIM], xw[:, k, 128:WSPAN], wv[:, :],
                                 start=True, stop=True).then_inc(v_mm, 1)

            def attend(i, k):
                u = i * 2 + k
                pe.wait_ge(exped, (u + 1) * WH)
                pe.wait_ge(pt_done, u)
                pe.wait_ge(pt2_done, u)
                for h in range(WH):
                    nc.tensor.transpose(psT[:, 0, h, 0:TP], P[:, k, h, 0:128], ident[0:TP, 0:TP])
                    last = nc.tensor.transpose(psT[0:k_rest, 1, h, 0:TP], P[:, k, h, 128:WSPAN], ident[0:TP, 0:TP])
                last.then_inc(turned, 1)
                pe.wait_ge(pt_done, u + 1)
                pe.wait_ge(pt2_done, u + 1)
                pe.wait_ge(v_done, (u + 1) * 2)
                pe.wait_ge(added, u)
                for h in range(WH):
                    cols = slice(h * WHD, (h + 1) * WHD)
                    nc.tensor.matmul(psO[0:TP, cols], PT[:, h, :], v1[:, k, cols], start=True, stop=False)
                    last = nc.tensor.matmul(psO[0:TP, cols], PT2[:, h, :], v2[:, k, cols], start=False, stop=True)
                last.then_inc(pv, 1)
                pe.wait_ge(init, 1)
                pe.wait_ge(o_done, u + 1)
                turn(nc, psO[0:DIM, 128:128 + TP], o[:, :], ident[0:TP, 0:TP], after_wait=True).then_inc(o_turned, 1)
                pe.wait_ge(oT_done, u + 1)
                nc.tensor.matmul(psO[0:TP, 256:256 + DIM], oT[:, :], wp[:, :], start=True, stop=True).then_inc(y_mm, 1)

            score(0, 0)
            with pe.Fori(0, PAIRS - 1) as i:
                score(i, 1)
                attend(i, 0)
                score(i + 1, 0)
                attend(i, 1)
            score(PAIRS - 1, 1)
            attend(PAIRS - 1, 0)
            attend(PAIRS - 1, 1)

        @block.vector
        def _(dve):
            nc.vector.memset(oT[DIM:AUG, :], 1.0).then_inc(init, 1)

            def soften(i, k):
                u = i * 2 + k
                dve.wait_ge(scored, u + 1)
                dve.wait_ge(exped, u * WH)
                nc.vector.scalar_tensor_tensor(S[:, k, :, :], psS[0:TP, :, 0:WSPAN], WHD ** -0.5, bias[:, :, :],
                                               ALU.mult, ALU.add).then_inc(biased, 1)
                dve.wait_ge(biased, u + 1)
                nc.vector.tensor_reduce(nmax[:, k, :], S[:, k, :, :], op=ALU.max, axis=AX.X, negate=True).then_inc(maxed, 1)

            def finish(i, k):
                u = i * 2 + k
                dve.wait_ge(turned, u + 1)
                dve.wait_ge(pv, u)
                nc.vector.tensor_copy(PT2[:, :, :], psT[0:k_rest, 1, :, 0:TP]).then_inc(pt2_done, 1)
                dve.wait_ge(exped, (u + 1) * WH)
                nc.vector.reciprocal(rs[:, k, :], sums[:, k, :]).then_inc(inv, 1)
                dve.wait_ge(pv, u + 1)
                dve.wait_ge(inv, u + 1)
                nc.vector.tensor_tensor(o[:, :].rearrange("p (h d) -> p h d", h=WH),
                                        psO[0:TP, 0:DIM].rearrange("p (h d) -> p h d", h=WH),
                                        bc_free(rs[:, k, :], TP, WHD), ALU.mult).then_inc(o_done, 1)
                dve.wait_ge(y_mm, u + 1)
                Hu = H[:, bass.ds(u, 1), :].rearrange("p a d -> p (a d)")
                nc.vector.tensor_tensor(Hu, Hu, psO[0:TP, 256:256 + DIM], ALU.add).then_inc(added, 1)

            soften(0, 0)
            with dve.Fori(0, PAIRS - 1) as i:
                soften(i, 1)
                finish(i, 0)
                soften(i + 1, 0)
                finish(i, 1)
            soften(PAIRS - 1, 1)
            finish(PAIRS - 1, 0)
            finish(PAIRS - 1, 1)

        @block.scalar
        def _(act):
            def exps(i, k):
                u = i * 2 + k
                act.wait_ge(v_mm, u + 1)
                nc.scalar.activation(v1[:, k, :], psV[:, 0:DIM], ACT.Copy).then_inc(v_done, 1)
                nc.scalar.activation(v2[:, k, :], psV[0:k_rest, DIM:2 * DIM], ACT.Copy).then_inc(v_done, 1)
                act.wait_ge(maxed, u + 1)
                for h in range(WH):
                    nc.scalar.activation(P[:, k, h, :], S[:, k, h, :], ACT.Exp, bias=nmax[:, k, h:h + 1],
                                         accum_out=sums[:, k, h:h + 1]).then_inc(exped, 1)

            def turn(i, k):
                u = i * 2 + k
                act.wait_ge(turned, u + 1)
                nc.scalar.activation(PT[:, :, :], psT[:, 0, :, 0:TP], ACT.Copy).then_inc(pt_done, 1)
                act.wait_ge(o_turned, u + 1)
                nc.scalar.activation(oT[0:DIM, :], psO[0:DIM, 128:128 + TP], ACT.Copy).then_inc(oT_done, 1)

            exps(0, 0)
            with act.Fori(0, PAIRS - 1) as i:
                exps(i, 1)
                turn(i, 0)
                exps(i + 1, 0)
                turn(i, 1)
            exps(PAIRS - 1, 1)
            turn(PAIRS - 1, 0)
            turn(PAIRS - 1, 1)
    bias_ctx.close()


PH, PK, PDK, TOPK = 8, 64, 32, 16
GROUPS = 2 * PH
SLOTS = PK * PK
CHUNKS = SLOTS // 128
STAIRS = [(0, 1, 16, 0), (1, 1, 8, 16), (2, 2, 5, 24), (4, 4, 3, 34), (8, 8, 1, 46)]
CAND = 54


def select_stage(nc, io, xT, e01D, theta, inv_z):
    with ExitStack() as ctx:
        s = Space(nc, ctx, "sel")
        wT = s.sb("wT", [PDK, GROUPS, DIM])
        keys = s.sb("keys", [PDK, GROUPS, PK])
        A = s.sb("A", [DIM, GROUPS * PK])
        xs = s.sb("xs", [DIM, 2, TP])
        nmx = s.sb("neg_max", [TP, GROUPS])
        d = s.sb("shifted", [TP, 2, GROUPS, PK])
        e = s.sb("e01", [TP, 2, GROUPS, PK])
        rest = s.sb("rest", [TP, GROUPS, PK])
        top = s.sb("top", [TP, GROUPS, TOPK])
        cand = s.sb("cand", [TP, PH, CAND])
        crest = s.sb("cand_rest", [TP, PH, CAND])
        best = s.sb("best", [TP, PH, TOPK])
        z = s.sb("z", [TP, PH])
        gate = s.sb("gate", [TP, 1])
        ps = [s.ps(f"ps{k}", (128, GROUPS, PK)) for k in range(2)]
        w_in, a_mm, a_done, x_cp, sims, shifted, exped = (
            s.sem(n) for n in ("w_in", "a_mm", "a_done", "x_copied", "sims", "shifted", "exped"))
        step, tops_done = s.sem("step"), s.sem("tops_done")
        stored = [s.sem(f"stored{k}") for k in range(2)]
        block = ctx.enter_context(nc.Block())
        PAIRS = UNITS // 2

        @block.sync
        def _(sp):
            for p in range(2):
                sp.dma_start(wT[:, p:GROUPS:2, :],
                             io["L0_ffn_Wq_pkT"][p * PH * PDK:(p + 1) * PH * PDK, :].rearrange("(h d) c -> d h c", d=PDK)).then_inc(w_in, 16)
                sp.dma_start(keys[:, p:GROUPS:2, :], io["L0_ffn_pk_keysT"][p].rearrange("h d k -> d h k")).then_inc(w_in, 16)
            with sp.Fori(0, PAIRS) as i:
                for k in range(2):
                    sp.wait_ge(exped, i * 2 + k + 1)
                    sp.dma_start(e01D[bass.ds(i * 2 + k, 1)].rearrange("a p c -> (a p) c"),
                                 e[:, k, :, :].rearrange("p g c -> p (g c)")).then_inc(stored[k], 16)
            for k in range(2):
                sp.wait_ge(stored[k], 16 * PAIRS)

        @block.tensor
        def _(pe):
            pe.wait_ge(w_in, 16 * 4)
            for g in range(GROUPS):
                last = nc.tensor.matmul(ps[0][0:DIM, g, :], wT[:, g, :], keys[:, g, :], start=True, stop=True)
            last.then_inc(a_mm, 1)
            pe.wait_ge(a_done, 1)
            with pe.Fori(0, PAIRS) as i:
                for k in range(2):
                    pe.wait_ge(x_cp, i * 2 + k + 1)
                    pe.wait_ge(shifted, i * 2)
                    for c in range(2):
                        last = nc.tensor.matmul(ps[k][0:TP, c * 8:(c + 1) * 8, :].rearrange("p g c -> p (g c)"), xs[:, k, :],
                                                A[:, c * 512:(c + 1) * 512], start=True, stop=True)
                    last.then_inc(sims, 1)

        @block.scalar
        def _(act):
            act.wait_ge(a_mm, 1)
            nc.scalar.activation(A[:, :].rearrange("p (g c) -> p g c", g=GROUPS), ps[0][0:DIM, :, :], ACT.Copy).then_inc(a_done, 1)
            xTf = xT[0:DIM, :, :].rearrange("p b n -> p (b n)")
            with act.Fori(0, PAIRS) as i:
                for k in range(2):
                    act.wait_ge(sims, i * 2)
                    nc.scalar.activation(xs[:, k, :], xTf[:, bass.ds((i * 2 + k) * TP, TP)], ACT.Copy).then_inc(x_cp, 1)
                for k in range(2):
                    act.wait_ge(shifted, i * 2 + k + 1)
                    act.wait_ge(stored[k], i * 16)
                    act.wait_ge(tops_done, i * 2)
                    nc.scalar.activation(e[:, k, :, :], d[:, k, :, :], ACT.Exp).then_inc(exped, 1)

        @block.vector
        def _(dve):
            with dve.Fori(0, PAIRS) as i:
                st = Steps(dve, step, i * 2 * SEL_STEPS)
                for k in range(2):
                    u = i * 2 + k
                    dve.wait_ge(sims, u + 1)
                    st.link(nc.vector.tensor_reduce(nmx[:, :], ps[k][0:TP, :, :], op=ALU.max, axis=AX.X, negate=True))
                    dve.wait_ge(exped, i * 2)
                    nc.vector.tensor_tensor(d[:, k, :, :], ps[k][0:TP, :, :], bc_free(nmx[:, :], TP, PK),
                                            ALU.add).then_inc(shifted, 1)
                    dve.wait_ge(exped, u + 1)
                    st.mark(nc.vector.memset(gate[:, :], 0.0))
                    for g in range(GROUPS):
                        st.mark(nc.vector.max(top[:, g, 0:8], e[:, k, g, :]))
                    st.settle()
                    st.mark(nc.vector.memset(gate[:, :], 0.0))
                    for g in range(GROUPS):
                        st.mark(nc.vector.match_replace(rest[:, g, :], top[:, g, 0:8], e[:, k, g, :], -1.0))
                    st.settle()
                    st.mark(nc.vector.memset(gate[:, :], 0.0))
                    for g in range(GROUPS):
                        st.mark(nc.vector.max(top[:, g, 8:16], rest[:, g, :]))
                    st.settle()
                    for a, na, nb, col in STAIRS:
                        shape = [TP, PH, na, nb]
                        st.mark(nc.vector.tensor_tensor(
                            cand[:, :, col:col + na * nb].rearrange("p h (a b) -> p h a b", a=na),
                            top[:, 0:GROUPS:2, a:a + na].unsqueeze(3).to_broadcast(shape),
                            top[:, 1:GROUPS:2, 0:nb].unsqueeze(2).to_broadcast(shape), ALU.mult))
                    st.settle()
                    st.mark(nc.vector.memset(gate[:, :], 0.0))
                    for h in range(PH):
                        st.mark(nc.vector.max(best[:, h, 0:8], cand[:, h, :]))
                    st.settle()
                    st.mark(nc.vector.memset(gate[:, :], 0.0))
                    for h in range(PH):
                        st.mark(nc.vector.match_replace(crest[:, h, :], best[:, h, 0:8], cand[:, h, :], -1.0))
                    st.settle()
                    st.mark(nc.vector.memset(gate[:, :], 0.0))
                    for h in range(PH):
                        st.mark(nc.vector.max(best[:, h, 8:16], crest[:, h, :]))
                    st.settle()
                    st.mark(nc.vector.tensor_reduce(z[:, :], best[:, :, :], op=ALU.add, axis=AX.X))
                    st.link(nc.vector.tensor_copy(theta[:, bass.ds(u, 1), :].rearrange("p a h -> p (a h)"), best[:, :, TOPK - 1]))
                    nc.vector.reciprocal(inv_z[:, bass.ds(u, 1), :].rearrange("p a h -> p (a h)"), z[:, :]).then_inc(tops_done, 1)
                    dve.wait_ge(tops_done, u + 1)
                assert st.n == 2 * SEL_STEPS, st.n


SEL_STEPS = 1 + 3 * (1 + GROUPS) + len(STAIRS) + 3 * (1 + PH) + 2


def memory_stage(nc, io, e01D, theta, inv_z, ident, kTD, vD):
    with ExitStack() as ctx:
        s = Space(nc, ctx, "mem")
        table = s.sb("table", [128, 2, CHUNKS, 2 * DIM])
        e01 = s.sb("e01", [TP, 2, 2 * PK])
        W = s.sb("weights", [TP, 2, SLOTS])
        WT = s.sb("weightsT", [128, 2, CHUNKS * TP])
        ks = s.sb("key", [TP, 2, DIM])
        kT = s.sb("keyT", [DIM, 2, NODES])
        V = s.sb("value", [TP, 2, UNITS, DIM])
        turn_banks = [s.ps(f"turn{k}", (128, 512)) for k in range(4)]
        ps_kv = [s.ps(f"kv{k}", (128, 512)) for k in range(2)]
        ps_k = s.ps("keys_turned", (128, 512))
        t_in = [s.sem(f"table_in{k}") for k in range(2)]
        e_in = [s.sem(f"e_in{k}") for k in range(2)]
        kv_st = [s.sem(f"kv_stored{k}") for k in range(2)]
        step, weighted, w_turned, wT_done, kv_mm, kv_done, k_turned, kT_done = (
            s.sem(n) for n in ("step", "weighted", "w_turned", "wT_done", "kv_mm", "kv_done", "k_turned", "kT_done"))
        block = ctx.enter_context(nc.Block())
        PAIRS = UNITS // 2
        TPARTS = 4
        GR = 4
        NG = CHUNKS // GR
        LAG = 2

        @block.sync
        def _(sp):
            def load_table(h):
                part = CHUNKS // TPARTS
                for n in range(TPARTS):
                    rows = slice(h * SLOTS + n * part * 128, h * SLOTS + (n + 1) * part * 128)
                    sp.dma_start(table[:, h % 2, n * part:(n + 1) * part, :],
                                 io["L0_ffn_tables"][rows, :].rearrange("(c p) d -> p c d", p=128)).then_inc(t_in[h % 2], 16)

            def load_e(h, first, last):
                with sp.Fori(first, last) as i:
                    for k in range(2):
                        sp.wait_ge(weighted, h * UNITS + i * 2)
                        sp.dma_start(e01[:, k, :], e01D[bass.ds(i * 2 + k, 1), :, h * 2 * PK:(h + 1) * 2 * PK]
                                     .rearrange("a p c -> (a p) c")).then_inc(e_in[k], 16)

            def store(h):
                sp.wait_ge(kv_done, (h + 1) * UNITS * 2)
                sp.dma_start(vD[h].rearrange("u p d -> p u d"), V[:, h % 2, :, :]).then_inc(kv_st[h % 2], 16)
                sp.wait_ge(kT_done, (h + 1) * UNITS)
                sp.dma_start(kTD[h], kT[:, h % 2, :]).then_inc(kv_st[h % 2], 16)

            load_table(0)
            for h in range(PH):
                load_e(h, 0, PAIRS // 2)
                if h > 0:
                    store(h - 1)
                if h + 1 < PH:
                    sp.wait_ge(kv_mm, h * UNITS)
                    load_table(h + 1)
                load_e(h, PAIRS // 2, PAIRS)
            store(PH - 1)
            for k in range(2):
                sp.wait_ge(kv_st[k], PH // 2 * 32)

        @block.tensor
        def _(pe):
            with pe.Fori(0, PH // 2) as pair:
                for q in range(2):
                    h = pair * 2 + q

                    def combine(i, k):
                        first = q == 0 and isinstance(i, int) and i == 0 and k == 0
                        g = h * UNITS + i * 2 + k
                        pe.wait_ge(weighted, g + 1)
                        if isinstance(i, int):
                            pe.wait_ge(kv_done, h * UNITS * 2)
                        else:
                            pe.wait_ge(kv_done, (g - 1) * 2)
                        for j in range(NG + LAG):
                            if j < NG:
                                pe.wait_ge(wT_done, g * NG + (max(j - len(turn_banks) + 1, 0) if first else j - len(turn_banks) + 1))
                                for c in range(GR):
                                    ch = j * GR + c
                                    last = nc.tensor.transpose(turn_banks[j % 4][:, c * TP:(c + 1) * TP],
                                                               W[:, k, ch * 128:(ch + 1) * 128], ident[0:TP, 0:TP])
                                last.then_inc(w_turned, 1)
                            if j == LAG:
                                pe.wait_ge(t_in[q], (pair + 1) * 16 * TPARTS)
                            if j >= LAG:
                                pe.wait_ge(wT_done, g * NG + j - LAG + 1)
                                for c in range(GR):
                                    ch = (j - LAG) * GR + c
                                    last = nc.tensor.matmul(ps_kv[k][0:TP, 0:2 * DIM], WT[:, k, ch * TP:(ch + 1) * TP],
                                                            table[:, q, ch, :], start=(ch == 0), stop=(ch == CHUNKS - 1))
                        last.then_inc(kv_mm, 1)

                    def turn_key(i, k):
                        g = h * UNITS + i * 2 + k
                        pe.wait_ge(kT_done, g)
                        pe.wait_ge(kv_done, g * 2 + 2)
                        turn(nc, ps_k[0:DIM, 0:TP], ks[:, k, :], ident[0:TP, 0:TP], after_wait=True).then_inc(k_turned, 1)

                    combine(0, 0)
                    combine(0, 1)
                    turn_key(0, 0)
                    with pe.Fori(1, PAIRS) as i:
                        combine(i, 0)
                        turn_key(i - 1, 1)
                        combine(i, 1)
                        turn_key(i, 0)
                    turn_key(PAIRS - 1, 1)

        @block.scalar
        def _(act):
            with act.Fori(0, PH // 2) as pair:
                for q in range(2):
                    h = pair * 2 + q

                    def copy_turned(i, k):
                        g = h * UNITS + i * 2 + k
                        for j in range(NG):
                            act.wait_ge(w_turned, g * NG + j + 1)
                            if j == 0 and isinstance(i, int):
                                act.wait_ge(kv_mm, h * UNITS)
                            elif j == 0:
                                act.wait_ge(kv_mm, g - 1)
                            nc.scalar.activation(WT[:, k, j * GR * TP:(j + 1) * GR * TP], turn_banks[j % 4][:, 0:GR * TP],
                                                 ACT.Copy).then_inc(wT_done, 1)

                    def copy_key(i, k):
                        g = h * UNITS + i * 2 + k
                        act.wait_ge(k_turned, g + 1)
                        act.wait_ge(kv_st[q], pair * 32)
                        nc.scalar.activation(kT[:, q, bass.ds((i * 2 + k) * TP, TP)], ps_k[0:DIM, 0:TP], ACT.Copy).then_inc(kT_done, 1)

                    copy_turned(0, 0)
                    copy_turned(0, 1)
                    copy_key(0, 0)
                    with act.Fori(1, PAIRS) as i:
                        copy_turned(i, 0)
                        copy_key(i - 1, 1)
                        copy_turned(i, 1)
                        copy_key(i, 0)
                    copy_key(PAIRS - 1, 1)

        @block.vector
        def _(dve):
            with dve.Fori(0, PH // 2) as pair:
                for q in range(2):
                    h = pair * 2 + q

                    def weigh(i, k):
                        g = h * UNITS + i * 2 + k
                        st = Steps(dve, step, g)
                        dve.wait_ge(e_in[k], (h * PAIRS + i) * 16 + 16)
                        if isinstance(i, int) and i == 0:
                            dve.wait_ge(w_turned, h * UNITS * NG)
                        else:
                            dve.wait_ge(w_turned, (g - 1) * NG)
                        Wk = W[:, k, :].rearrange("p (a b) -> p a b", a=PK)
                        shape = [TP, PK, PK]
                        st.link(nc.vector.tensor_tensor(Wk, e01[:, k, PK:2 * PK].unsqueeze(2).to_broadcast(shape),
                                                        e01[:, k, 0:PK].unsqueeze(1).to_broadcast(shape), ALU.mult))
                        nc.vector.scalar_tensor_tensor(
                            W[:, k, :], W[:, k, :],
                            theta[:, bass.ds(i * 2 + k, 1), bass.ds(h, 1)].rearrange("p a h -> p (a h)"),
                            W[:, k, :], ALU.is_ge, ALU.mult).then_inc(weighted, 1)

                    def normalise(i, k):
                        g = h * UNITS + i * 2 + k
                        dve.wait_ge(kv_mm, g + 1)
                        dve.wait_ge(kv_st[q], pair * 32)
                        if isinstance(i, int) and i == 0:
                            dve.wait_ge(k_turned, h * UNITS)
                        else:
                            dve.wait_ge(k_turned, g - 1)
                        z = inv_z[:, bass.ds(i * 2 + k, 1), bass.ds(h, 1)].rearrange("p a h -> p (a h)")
                        nc.vector.tensor_scalar(ks[:, k, :], ps_kv[k][0:TP, 0:DIM], z, None, ALU.mult).then_inc(kv_done, 1)
                        nc.vector.tensor_scalar(V[:, q, bass.ds(i * 2 + k, 1), :].rearrange("p a d -> p (a d)"),
                                                ps_kv[k][0:TP, DIM:2 * DIM], z, None, ALU.mult).then_inc(kv_done, 1)

                    weigh(0, 0)
                    weigh(0, 1)
                    normalise(0, 0)
                    weigh(1, 0)
                    normalise(0, 1)
                    with dve.Fori(1, PAIRS - 1) as i:
                        weigh(i, 1)
                        normalise(i, 0)
                        weigh(i + 1, 0)
                        normalise(i, 1)
                    weigh(PAIRS - 1, 1)
                    normalise(PAIRS - 1, 0)
                    normalise(PAIRS - 1, 1)


RECALL_MAX = 96


def recall_stage(nc, io, H, xT, ident, kTD, vD):
    qD = nc.dram_tensor("scratch_mem_q", [PH * DIM, BATCH, PAD], F32).ap()
    with ExitStack() as ctx:
        s = Space(nc, ctx, "memq")
        wq = s.sb("wq", [DIM, PH * DIM])
        xb = s.sb("tokens", [DIM, BATCH, PAD])
        qo = s.sb("q", [128, 4, PAD])
        ps = [s.ps(f"ps{k}", (128, 3, 512)) for k in range(2)]
        w_in, x_cp, mm, cp = (s.sem(n) for n in ("w_in", "x_copied", "mm", "copied"))
        st = [s.sem(f"stored{k}") for k in range(4)]
        block = ctx.enter_context(nc.Block())
        ROUNDS = BATCH * PH // 2

        @block.sync
        def _(sp):
            sp.dma_start(wq[:, :], io["L0_ffn_Wq"]).then_inc(w_in, 16)
            for n in range(ROUNDS):
                b, hh = divmod(n, PH // 2)
                sp.wait_ge(cp, n + 1)
                sp.dma_start(qD[hh * 128:(hh + 1) * 128, b, :], qo[:, n % 4, :]).then_inc(st[n % 4], 16)
            for k in range(4):
                sp.wait_ge(st[k], ROUNDS // 4 * 16)

        @block.tensor
        def _(pe):
            pe.wait_ge(w_in, 16)
            for n in range(ROUNDS):
                b, hh = divmod(n, PH // 2)
                if n >= 2:
                    pe.wait_ge(cp, n - 1)
                for c in range(3):
                    last = nc.tensor.matmul(ps[n % 2][:, c, 0:HALF], wq[:, hh * 128:(hh + 1) * 128],
                                            xT[0:DIM, b, c * HALF:(c + 1) * HALF], start=True, stop=True)
                last.then_inc(mm, 1)

        @block.scalar
        def _(act):
            for n in range(ROUNDS):
                act.wait_ge(mm, n + 1)
                if n >= 4:
                    act.wait_ge(st[n % 4], n // 4 * 16)
                nc.scalar.activation(qo[:, n % 4, :].rearrange("p (c n) -> p c n", c=3), ps[n % 2][:, :, 0:HALF], ACT.Copy,
                                     scale=DIM ** -0.5).then_inc(cp, 1)

    with ExitStack() as ctx:
        s = Space(nc, ctx, "rec")
        q = [s.sb(f"q{k}", [128, PAD]) for k in range(BATCH)]
        kb = [s.sb(f"k{k}", [128, PAD]) for k in range(BATCH)]
        V = [s.sb(f"v{k}", [TP, TILES, AUG]) for k in range(BATCH)]
        wo = s.sb("wo", [AUG, PH, AUG])
        mask, maskT, identb = (s.sb(n, [TP, TP], BF16) for n in ("causal", "causalT", "identity_bf16"))
        P = s.sb("probs", [TP, 3, HALF])
        nm3 = s.sb("chunk_max", [TP, TILES, 3])
        nm = s.sb("neg_max", [TP, TILES])
        mT = s.sb("neg_maxT", [TILES, TP])
        oT = s.sb("outT", [AUG, PAD])
        rs = s.sb("inv_sums", [TP, TILES])
        y = s.sb("scaled", [TP, 5, DIM])
        mD = nc.dram_tensor("scratch_mem_max", [BATCH, TILES, TP], F32).ap()
        psA = [s.ps(f"max_scores{k}", (128, 512)) for k in range(2)]
        psB = [s.ps(f"scores{k}", (128, 512)) for k in range(2)]
        ps_o, ps_m = s.ps("sums", (128, 3, 512)), s.ps("turned", (128, 512))
        ld = [s.sem(f"loaded{k}") for k in range(BATCH)]
        w_in, zeroed, init, m_made, m_st, m_in = (s.sem(n) for n in ("w_in", "zeroed", "init", "masks", "max_stored", "max_in"))
        a_mm, maxed, n_max, m_turned, m_cp, scored, exped, pv, o_cp, y_mm, yst, added = (
            s.sem(n) for n in ("a_scored", "maxed", "combined", "max_turned", "max_copied", "scored", "exped", "pv",
                               "sums_copied", "y_mm", "y_step", "added"))
        block = ctx.enter_context(nc.Block())
        CA = [(t, c, min(3, t + 1 - c)) for t in range(TILES) for c in range(0, t + 1, 3)]
        CB = [(t, max(t, c), c + 3 - max(t, c)) for t in range(TILES) for c in range(t // 3 * 3, TILES, 3)]
        NC = len(CA)
        assert NC == len(CB)
        PER = [2] * 4 + [1] * 10 + [0] * 4
        YT = [(0, 5), (5, 4)]

        def run(eng, one):
            with eng.Fori(0, PH - 1) as h:
                for b in range(BATCH):
                    one(h, h * BATCH + b, b, False)
            for b in range(BATCH):
                one(PH - 1, (PH - 1) * BATCH + b, b, b == BATCH - 1)

        @block.sync
        def _(sp):
            sp.dma_start(wo[0:DIM, :, 0:DIM], io["L0_ffn_Wo"].rearrange("(h d) c -> d h c", d=DIM)).then_inc(w_in, 16)

            def load(h, b):
                at = slice(h, h + 1) if isinstance(h, int) else bass.ds(h, 1)
                rows = slice(h * DIM, (h + 1) * DIM) if isinstance(h, int) else bass.ds(h * DIM, DIM)
                sp.dma_start(q[b][0:DIM, :], qD[rows, b, :]).then_inc(ld[b], 16)
                sp.dma_start(kb[b][0:DIM, :], kTD[at, :, b * PAD:(b + 1) * PAD].rearrange("a d n -> (a d) n")).then_inc(ld[b], 16)
                sp.dma_start(V[b][:, :, 0:DIM], vD[at, b * TILES:(b + 1) * TILES].rearrange("a t p d -> p (a t) d")).then_inc(ld[b], 16)

            def move_maxima(n, b):
                sp.wait_ge(m_cp, n + 1)
                sp.dma_start(mD[b], mT[:, :]).then_inc(m_st, 16)
                sp.wait_ge(m_st, n * 16 + 16)
                sp.dma_start(q[b][RECALL_MAX:RECALL_MAX + 1, :], mD[b:b + 1].rearrange("a t c -> a (t c)")).then_inc(m_in, 16)

            def one(h, n, b, last):
                if not last:
                    move_maxima(n + 1, (b + 1) % BATCH)
                if not isinstance(h, int):
                    sp.wait_ge(pv, (n + 1) * NC)
                    load(h + 1, b)

            for b in range(BATCH):
                load(0, b)
            sp.wait_ge(init, 11)
            move_maxima(0, 0)
            run(sp, one)

        @block.gpsimd
        def _(pool):
            nc.gpsimd.memset(mask[:, :], 0.0).then_inc(m_made, 1)
            nc.gpsimd.memset(maskT[:, :], 0.0).then_inc(m_made, 1)
            pool.wait_ge(m_made, 2)
            nc.gpsimd.affine_select(out=mask[:, :], in_=mask[:, :], compare_op=ALU.is_ge, fill=FAR, base=0,
                                    pattern=[[-1, TP]], channel_multiplier=1).then_inc(m_made, 1)
            nc.gpsimd.affine_select(out=maskT[:, :], in_=maskT[:, :], compare_op=ALU.is_ge, fill=FAR, base=0,
                                    pattern=[[1, TP]], channel_multiplier=-1).then_inc(m_made, 1)

        @block.tensor
        def _(pe):
            def search(n, b, x):
                t, c, w = CA[x]
                if not (isinstance(n, int) and n == 0 and x < 2):
                    pe.wait_ge(maxed, n * NC + x - 1)
                diag = c + w == t + 1
                last = nc.tensor.matmul(psA[x % 2][0:TP, 0:w * TP], q[b][0:RECALL_MAX, t * TP:(t + 1) * TP],
                                        kb[b][0:RECALL_MAX, c * TP:(c + w) * TP], start=True, stop=not diag)
                if diag:
                    last = nc.tensor.matmul(psA[x % 2][0:TP, (w - 1) * TP:w * TP], identb[:, :], mask[:, :], start=False, stop=True)
                last.then_inc(a_mm, 1)

            def turn_maxima(n):
                pe.wait_ge(n_max, n + 1)
                pe.wait_ge(m_cp, n)
                nc.tensor.transpose(ps_m[0:TILES, 384:384 + TP], nm[:, :], ident[0:TP, 0:TP]).then_inc(m_turned, 1)

            def score(n, b, x):
                t, c, w = CB[x]
                pe.wait_ge(exped, n * NC + max(x - 1, 0))
                diag = c == t
                last = nc.tensor.matmul(psB[x % 2][0:TP, 0:w * TP], kb[b][:, t * TP:(t + 1) * TP], q[b][:, c * TP:(c + w) * TP],
                                        start=True, stop=not diag)
                if diag:
                    last = nc.tensor.matmul(psB[x % 2][0:TP, 0:TP], identb[:, :], maskT[:, :], start=False, stop=True)
                last.then_inc(scored, 1)

            def attend(n, b, x):
                t, c, w = CB[x]
                pe.wait_ge(exped, n * NC + x + 1)
                nc.tensor.matmul(ps_o[0:AUG, c // 3, c % 3 * TP:(c % 3 + w) * TP], V[b][:, t, :], P[:, x % 3, 0:w * TP],
                                 start=(t == 0), stop=(t == c + w - 1)).then_inc(pv, 1)

            def project(h, n, g):
                pe.wait_ge(o_cp, n + 1)
                pe.wait_ge(added, n * 2 + g)
                first, count = YT[g]
                for t in range(count):
                    last = nc.tensor.matmul(ps_m[0:TP, t * AUG:(t + 1) * AUG], oT[:, (first + t) * TP:(first + t + 1) * TP],
                                            wo_now(h), start=True, stop=True)
                last.then_inc(y_mm, 1)

            def wo_now(h):
                if isinstance(h, int):
                    return wo[:, h, :]
                return wo[:, bass.ds(h, 1), :].rearrange("p a c -> p (a c)")

            pe.wait_ge(w_in, 16)
            pe.wait_ge(init, 11)
            pe.wait_ge(m_made, 4)
            pe.wait_ge(ld[0], 48)
            for x in range(NC):
                search(0, 0, x)
            turn_maxima(0)

            def one(h, n, b, last):
                nb = (b + 1) % BATCH
                late, own = b > 0, b == BATCH - 1
                if not last:
                    pe.wait_ge(ld[nb], (h + (nb == 0)) * 48 + 48)
                pe.wait_ge(m_in, n * 16 + 16)
                score(n, b, 0)
                at = 0
                for x in range(NC):
                    if not last and PER[x] > 0:
                        search(n + 1, nb, at)
                        at += 1
                    if x + 1 < NC:
                        score(n, b, x + 1)
                    if not last and PER[x] > 1:
                        search(n + 1, nb, at)
                        at += 1
                    if x == 0:
                        pe.wait_ge(o_cp, n)
                    attend(n, b, x)
                    if late and x == 2:
                        project(h, n - 1, 0)
                    if late and x == 5:
                        project(h, n - 1, 1)
                    if not last and x == 14:
                        pe.wait_ge(added, n * 2)
                        turn_maxima(n + 1)
                if own:
                    project(h, n, 0)
                    project(h, n, 1)
            run(pe, one)

        @block.scalar
        def _(act):
            nc.scalar.activation(identb[:, :], ident[0:TP, 0:TP], ACT.Copy).then_inc(init, 1)

            def copy_maxima(n):
                act.wait_ge(m_turned, n + 1)
                act.wait_ge(m_st, n * 16)
                nc.scalar.activation(mT[:, :], ps_m[0:TILES, 384:384 + TP], ACT.Copy).then_inc(m_cp, 1)

            def copy_sums(n):
                act.wait_ge(pv, (n + 1) * NC)
                act.wait_ge(y_mm, n * 2)
                nc.scalar.activation(oT[:, :].rearrange("p (c n) -> p c n", c=3), ps_o[0:AUG, :, 0:HALF], ACT.Copy).then_inc(o_cp, 1)

            copy_maxima(0)

            def one(h, n, b, last):
                for x in range(NC):
                    w = CB[x][2]
                    act.wait_ge(scored, n * NC + x + 1)
                    act.wait_ge(pv, n * NC + max(x - 2, 0))
                    nc.scalar.activation(P[:, x % 3, 0:w * TP], psB[x % 2][0:TP, 0:w * TP], ACT.Exp).then_inc(exped, 1)
                    if not last and x == 16:
                        copy_maxima(n + 1)
                copy_sums(n)
            run(act, one)

        @block.vector
        def _(dve):
            nc.vector.memset(nm3[:, :, :], FAR).then_inc(init, 1)
            nc.vector.memset(wo[:, :, DIM:AUG], 0.0).then_inc(zeroed, 1)
            nc.vector.memset(wo[DIM:AUG, :, 0:DIM], 0.0).then_inc(zeroed, 1)
            dve.wait_ge(zeroed, 2)
            nc.vector.memset(wo[DIM:AUG, :, DIM:AUG], 1.0).then_inc(init, 1)
            for b in range(BATCH):
                nc.vector.memset(q[b][DIM:128, :], 0.0).then_inc(zeroed, 1)
                nc.vector.memset(kb[b][DIM:128, :], 0.0).then_inc(zeroed, 1)
                dve.wait_ge(zeroed, 2 * b + 4)
                nc.vector.memset(kb[b][RECALL_MAX:RECALL_MAX + 1, :], 1.0).then_inc(init, 1)
                nc.vector.memset(V[b][:, :, DIM:AUG], 1.0).then_inc(init, 1)

            def maxima(n, x):
                t, c, w = CA[x]
                dve.wait_ge(a_mm, n * NC + x + 1)
                dve.wait_ge(n_max, n)
                nc.vector.tensor_reduce(nm3[:, t, c // 3:c // 3 + 1], psA[x % 2][0:TP, 0:w * TP], op=ALU.max, axis=AX.X).then_inc(maxed, 1)

            def combine(n):
                dve.wait_ge(maxed, (n + 1) * NC)
                dve.wait_ge(m_turned, n)
                nc.vector.tensor_reduce(nm[:, :], nm3[:, :, :], op=ALU.max, axis=AX.X, negate=True).then_inc(n_max, 1)

            def add(n, b, g):
                first, count = YT[g]
                st = Steps(dve, yst, (n * 2 + g) * 2)
                dve.wait_ge(y_mm, n * 2 + g + 1)
                dve.wait_ge(added, n * 2 + g)
                ys = ps_m[0:TP, 0:count * AUG].rearrange("p (t d) -> p t d", d=AUG)
                st.link(nc.vector.reciprocal(rs[:, 0:count], ys[:, :, DIM]))
                st.link(nc.vector.tensor_tensor(y[:, 0:count, :], ys[:, :, 0:DIM], bc_free(rs[:, 0:count], TP, DIM), ALU.mult))
                Hg = H[:, b * TILES + first:b * TILES + first + count, :]
                nc.vector.tensor_tensor(Hg, Hg, y[:, 0:count, :], ALU.add).then_inc(added, 1)

            dve.wait_ge(init, 11)
            for x in range(NC):
                maxima(0, x)
            combine(0)

            def one(h, n, b, last):
                late, own = b > 0, b == BATCH - 1
                at = 0
                for x in range(NC):
                    if not last:
                        for _ in range(PER[x]):
                            maxima(n + 1, at)
                            at += 1
                    if late and x in (2, 5):
                        add(n - 1, b - 1, (x - 2) // 3)
                if not last:
                    combine(n + 1)
                if own:
                    add(n, b, 0)
                    add(n, b, 1)
            run(dve, one)
            dve.wait_ge(added, PH * BATCH * 2)


MH, MHD = 8, 8
PARTS = 3
QK_ROWS = PARTS * PARTS * MHD
MROW = 96
CH = 8
XT = MH * TILES // CH
MA = 3


def heads_stage(nc, io, H, xT, ident):
    qD = nc.dram_tensor("scratch_mha_q", [UNITS + 1, PARTS, PARTS, DIM, TP], BF16).ap()
    kD = nc.dram_tensor("scratch_mha_k", [BATCH, PARTS, DIM, PAD], BF16).ap()
    with ExitStack() as outer:
        o = Space(nc, outer, "mha")
        V = o.sb("value", [TP, UNITS, MH, MHD + 1])
        wo = o.sb("wo", [AUG, DIM])
        keys = [o.sb(f"keys{k}", [128, MH, PAD], BF16) for k in range(2)]
        ahead = [o.sb(f"q_ahead{k}", [128, MH, TP], BF16) for k in range(2)]
        now = [o.sb(f"q_now{k}", [128, MH, TP], BF16) for k in range(2)]
        mparts = o.sb("max_parts", [TP, 128], BF16)
        identb = o.sb("identity_bf16", [128, 128], BF16)
        oT = o.sb("oT", [AUG, TP])
        with ExitStack() as ctx:
            s = Space(nc, ctx, "mhap")
            wqk, wv = s.sb("wqk", [AUG, 2 * DIM]), s.sb("wv", [AUG, DIM])
            xb = s.sb("tokens_batch", [AUG, PAD])
            qk = s.sb("qk", [128, PAD])
            rest = s.sb("rest", [128, 2, PAD])
            parts = s.sb("parts", [128, PARTS, PAD], BF16)
            sel = s.sb("selector", [128, MH])
            psq, psv = s.ps("psq", (128, 3, 512)), s.ps("psv", (128, 2, 512))
            w_in, init, scaled, x_cp, qk_mm, v_mm, qk_cp, v_cp, step, q_st, k_st, sel_done = (
                s.sem(n) for n in ("w_in", "init", "scaled", "x_copied", "qk_mm", "v_mm", "qk_copied", "v_copied",
                                   "step", "q_stored", "k_stored", "sel_done"))
            block = ctx.enter_context(nc.Block())

            @block.sync
            def _(sp):
                for n, (w, c) in {"q": (wqk, 0), "k": (wqk, DIM), "v": (wv, 0), "o": (wo, 0)}.items():
                    sp.dma_start(w[0:DIM, c:c + DIM], io[f"L1_attn_W{n}T"]).then_inc(w_in, 16)
                    sp.dma_start(w[DIM:AUG, c:c + DIM], io[f"L1_attn_b{n}"].unsqueeze(0)).then_inc(w_in, 16)
                with sp.Fori(0, BATCH) as b:
                    sp.wait_ge(step, (b + 1) * PROJ_STEPS)
                    for i in range(PARTS):
                        for j in range(PARTS):
                            sp.dma_start(qD[bass.ds(b * TILES, TILES), i, j].rearrange("t p c -> p t c"),
                                         parts[0:DIM, i, :].rearrange("p (t c) -> p t c", t=TILES)).then_inc(q_st, 16)
                    sp.dma_start(kD[bass.ds(b, 1)].rearrange("a i p n -> (a p) i n"), parts[DIM:128, :, :]).then_inc(k_st, 16)
                sp.dma_start(qD[UNITS].rearrange("i j p c -> p (i j) c"),
                             parts[0:DIM, 0, :].rearrange("p (t c) -> p t c", t=TILES)).then_inc(k_st, 16)
                sp.wait_ge(q_st, BATCH * PARTS * PARTS * 16)
                sp.wait_ge(k_st, (BATCH + 1) * 16)

            @block.gpsimd
            def _(pool):
                nc.gpsimd.memset(sel[:, :], 0.0).then_inc(sel_done, 1)
                for i in range(PARTS):
                    pool.wait_ge(sel_done, i + 1)
                    nc.gpsimd.affine_select(out=sel[:, :], in_=sel[:, :], compare_op=ALU.not_equal, fill=1.0,
                                            base=-(MROW + MH * i), pattern=[[-1, MH]], channel_multiplier=1).then_inc(sel_done, 1)

            @block.tensor
            def _(pe):
                pe.wait_ge(w_in, 16 * 8)
                pe.wait_ge(scaled, 1)
                with pe.Fori(0, BATCH) as b:
                    pe.wait_ge(x_cp, b + 1)
                    pe.wait_ge(qk_cp, b * 2)
                    pe.wait_ge(v_cp, b * 2)
                    for c in range(3):
                        last = nc.tensor.matmul(psq[:, c, 0:HALF], wqk[:, :], xb[:, c * HALF:(c + 1) * HALF], start=True, stop=True)
                    last.then_inc(qk_mm, 1)
                    for t in range(TILES):
                        last = nc.tensor.matmul(psv[0:TP, t // 8, t % 8 * DIM:(t % 8 + 1) * DIM], xb[:, t * TP:(t + 1) * TP],
                                                wv[:, :], start=True, stop=True)
                    last.then_inc(v_mm, 1)

            @block.scalar
            def _(act):
                nc.scalar.activation(identb[:, :], ident[:, :], ACT.Copy).then_inc(init, 1)
                act.wait_ge(sel_done, PARTS + 1)
                for k in range(2):
                    nc.scalar.activation(keys[k][MROW:128, :, :], bc_free(sel[MROW:128, :], 128 - MROW, PAD),
                                         ACT.Copy).then_inc(init, 1)
                with act.Fori(0, BATCH) as b:
                    act.wait_ge(v_mm, b)
                    nc.scalar.activation(xb[:, :], xT[:, bass.ds(b, 1), :].rearrange("p a n -> p (a n)"), ACT.Copy).then_inc(x_cp, 1)
                    act.wait_ge(qk_mm, b + 1)
                    act.wait_ge(step, b * PROJ_STEPS)
                    nc.scalar.activation(qk[:, :].rearrange("p (c n) -> p c n", c=3), psq[:, :, 0:HALF], ACT.Copy).then_inc(qk_cp, 1)
                    act.wait_ge(qk_cp, b * 2 + 1)
                    nc.scalar.activation(qk[:, PAD - 1:PAD], psq[:, 2, HALF - 2:HALF - 1], ACT.Copy).then_inc(qk_cp, 1)
                    act.wait_ge(v_mm, b + 1)
                    for t0, tn in ((0, 8), (8, 1)):
                        nc.scalar.activation(V[:, bass.ds(b * TILES + t0, tn), :, 0:MHD],
                                             psv[0:TP, t0 // 8, 0:tn * DIM].rearrange("p (t h d) -> p t h d", t=tn, h=MH),
                                             ACT.Copy).then_inc(v_cp, 1)
                act.wait_ge(v_cp, BATCH * 2)

            @block.vector
            def _(dve):
                nc.vector.memset(V[:, :, :, MHD:MHD + 1], 1.0).then_inc(init, 1)
                nc.vector.memset(oT[DIM:AUG, :], 1.0).then_inc(init, 1)
                dve.wait_ge(w_in, 16 * 8)
                nc.vector.tensor_scalar(wqk[:, 0:DIM], wqk[:, 0:DIM], MHD ** -0.5, None, ALU.mult).then_inc(scaled, 1)
                nc.vector.memset(mparts[:, :], 0.0).then_inc(init, 1)
                for k in range(2):
                    nc.vector.memset(now[k][64:128, :, :], 0.0).then_inc(init, 1)
                    nc.vector.memset(keys[k][64:96, :, :], 0.0).then_inc(init, 1)
                with dve.Fori(0, BATCH) as b:
                    st = Steps(dve, step, b * PROJ_STEPS)
                    dve.wait_ge(qk_cp, b * 2 + 2)
                    dve.wait_ge(q_st, b * PARTS * PARTS * 16)
                    dve.wait_ge(k_st, b * 16)
                    st.link(nc.vector.tensor_copy(parts[:, 0, :], qk[:, :]))
                    st.link(nc.vector.tensor_tensor(rest[:, 0, :], qk[:, :], parts[:, 0, :], ALU.subtract))
                    st.link(nc.vector.tensor_copy(parts[:, 1, :], rest[:, 0, :]))
                    st.mark(nc.vector.tensor_tensor(parts[:, 2, :], rest[:, 0, :], parts[:, 1, :], ALU.subtract))
                    assert st.n == PROJ_STEPS

        P = o.sb("probs", [TP, 3, CH * TP])
        Vw = o.sb("value_wide", [TP, 2, TILES, MH, VSTEP])
        nm3 = o.sb("chunk_max", [TP, MH, MA])
        nm = o.sb("neg_max", [TP, 2, MH])
        rs = o.sb("inv_sums", [TP, MH])
        sumsT = o.sb("sumsT", [VROWS, TP])
        out = o.sb("out", [TP, MH, MHD])
        psA = [o.ps(f"max_scores{k}", (128, 512)) for k in range(2)]
        psB = [o.ps(f"scores{k}", (128, 2, 512)) for k in range(2)]
        ps_o, ps_m = o.ps("sums", (128, 512)), o.ps("turned", (128, 512))
        k_in = [o.sem(f"keys_in{k}") for k in range(2)]
        a_in = [o.sem(f"ahead_in{k}") for k in range(2)]
        n_in = [o.sem(f"now_in{k}") for k in range(2)]
        a_mm, maxed, step, m_turned, m_ready, scored, exped, pv, zeroed, v_wide = (
            o.sem(n) for n in ("a_scored", "maxed", "max_step", "max_turned", "max_ready", "scored", "exped", "pv",
                               "zeroed", "v_wide"))
        s_copied, s_turned, inv, o_done, o_turned, oT_done, y_mm, added = (
            o.sem(n) for n in ("sums_copied", "sums_turned", "inv", "o_done", "o_turned", "oT_done", "y_mm", "added"))
        AN = MH * MA
        block = outer.enter_context(nc.Block())

        def run(eng, one):
            for b in range(BATCH):
                with eng.Fori(0, TILES // 2) as i:
                    for k in range(2):
                        one(b, b * TILES + i * 2 + k, (b * TILES + k) % 2, late=b > 0, own=b == 0, nxt=b,
                            loads=i + (b * TILES + k + 1) // 2 + 1)
                u = (b + 1) * TILES - 1
                one(b, u, u % 2, late=b > 0, own=b == BATCH - 1, nxt=b + 1 if b + 1 < BATCH else None, loads=(u + 1) // 2 + 1)

        @block.gpsimd
        def _(pool):
            nc.gpsimd.memset(Vw[:, :, :, :, :], 0.0).then_inc(zeroed, 1)
            pool.wait_ge(zeroed, 1)
            for b in range(BATCH):
                if b >= 2:
                    pool.wait_ge(scored, (b - 1) * TILES * XT)
                    pool.wait_ge(pv, (b - 1) * TILES * XT)
                for i in range(PARTS):
                    nc.gpsimd.dma_start(keys[b % 2][i * 24:(i + 1) * 24, :, :],
                                        kD[b].rearrange("j (d h) n -> (j d) h n", h=MH)).then_inc(k_in[b % 2], 16)
                nc.gpsimd.tensor_copy(Vw[:, b % 2, :, :, 0:MHD + 1], V[:, b * TILES:(b + 1) * TILES, :, :]).then_inc(v_wide, 1)

        @block.sync
        def _(sp):
            def load(u, buf, sem):
                sp.dma_start(buf[0:QK_ROWS, :, :],
                             qD[bass.ds(u, 1)].rearrange("a i j (d h) c -> (a i j d) h c", h=MH)).then_inc(sem, 16)

            load(0, ahead[0], a_in[0])
            load(0, now[0], n_in[0])
            load(1, ahead[1], a_in[1])

            def one(b, u, par, late, own, nxt, loads):
                if nxt is None:
                    return
                sp.wait_ge(scored, u * XT)
                load(u + 1, now[1 - par], n_in[1 - par])
                if not (isinstance(u, int) and u + 2 >= UNITS):
                    sp.wait_ge(a_mm, (u + 1) * AN)
                    load(u + 2, ahead[par], a_in[par])
            run(sp, one)
            sp.wait_ge(a_in[0], (UNITS // 2 + 1) * 16)

        @block.tensor
        def _(pe):
            def search(v, par, kb, n):
                j, c = divmod(n, MA)
                if not (isinstance(v, int) and v == 0 and n < 2):
                    pe.wait_ge(maxed, v * AN + n - 1)
                nc.tensor.matmul(psA[n % 2][0:TP, 0:HALF], ahead[par][0:QK_ROWS, j, :],
                                 keys[kb][0:QK_ROWS, j, c * HALF:(c + 1) * HALF], start=True, stop=True).then_inc(a_mm, 1)

            def turn_maxima(v):
                pe.wait_ge(step, (v + 1) * M_STEPS)
                nc.tensor.matmul(ps_m[:, 0:TP], mparts[:, :], identb[0:TP, 0:TP], start=True, stop=True).then_inc(m_turned, 1)

            def score(e0, par, kb, x):
                pe.wait_ge(exped, e0 + max(x - 1, 0))
                for y in range(CH):
                    j, kt = divmod(x * CH + y, TILES)
                    last = nc.tensor.matmul(psB[(x + par) % 2][0:TP, y // 4, y % 4 * TP:(y % 4 + 1) * TP],
                                            keys[kb][:, j, kt * TP:(kt + 1) * TP], now[par][:, j, :], start=True, stop=True)
                last.then_inc(scored, 1)

            def attend(e0, b, x, ns):
                for n in ns:
                    j, kt = divmod(n, TILES)
                    rows = TP - 1 if kt == TILES - 1 else TP
                    wide = Vw[0:rows, b % 2, kt, :, :].rearrange("p h v -> p (h v)")[:, j * VROWS:(j + 1) * VROWS]
                    last = nc.tensor.matmul(ps_o[0:VROWS, 0:TP], wide, P[0:rows, x % 3, (n - x * CH) * TP:(n - x * CH + 1) * TP],
                                            start=(n == 0), stop=(n == MH * TILES - 1))
                return last

            def turn_sums(v):
                pe.wait_ge(added, v)
                pe.wait_ge(s_copied, v + 1)
                nc.tensor.matmul(ps_m[0:TP, 384:384 + VROWS], sumsT[:, :], ident[0:VROWS, 0:VROWS], start=True, stop=True)\
                  .then_inc(s_turned, 1)

            def turn_out(v):
                pe.wait_ge(o_done, v + 1)
                turn(nc, ps_m[0:DIM, 128:128 + TP], out[:, :, :].rearrange("p h d -> p (h d)"), ident[0:TP, 0:TP],
                     after_wait=True).then_inc(o_turned, 1)

            def project(v):
                pe.wait_ge(oT_done, v + 1)
                nc.tensor.matmul(ps_m[0:TP, 256:256 + DIM], oT[:, :], wo[:, :], start=True, stop=True).then_inc(y_mm, 1)

            pe.wait_ge(k_in[0], 16 * PARTS)
            pe.wait_ge(a_in[0], 16)
            for n in range(AN):
                search(0, 0, 0, n)
            turn_maxima(0)
            pe.wait_ge(n_in[0], 16)

            def one(b, u, par, late, own, nxt, loads):
                e0 = u * XT
                other = 1 - par
                pe.wait_ge(m_ready, u + 1)
                score(e0, par, b % 2, 0)
                if nxt is not None:
                    if nxt != b:
                        pe.wait_ge(k_in[nxt % 2], 16 * PARTS * (nxt // 2 + 1))
                    pe.wait_ge(a_in[other], loads * 16)
                    pe.wait_ge(n_in[other], loads * 16)
                for x in range(XT):
                    tiles = range(x * CH, (x + 1) * CH)
                    search_now = nxt is not None and x < XT - 1
                    if search_now:
                        search(u + 1, other, nxt % 2, x * 3)
                    if x + 1 < XT:
                        score(e0, par, b % 2, x + 1)
                    if search_now:
                        search(u + 1, other, nxt % 2, x * 3 + 1)
                    if x == 0:
                        pe.wait_ge(v_wide, b + 1)
                        pe.wait_ge(s_copied, u)
                    pe.wait_ge(exped, e0 + x + 1)
                    attend(e0, b, x, tiles[0:CH // 2])
                    if search_now:
                        search(u + 1, other, nxt % 2, x * 3 + 2)
                    attend(e0, b, x, tiles[CH // 2:]).then_inc(pv, 1)
                    if late and x == 0:
                        turn_sums(u - 1)
                    if late and x == 2:
                        turn_out(u - 1)
                    if late and x == 4:
                        project(u - 1)
                    if nxt is not None and x == XT - 2:
                        pe.wait_ge(added, u)
                        turn_maxima(u + 1)
                if own:
                    turn_sums(u)
                    turn_out(u)
                    project(u)
            run(pe, one)

        @block.scalar
        def _(act):
            def copy_maxima(v, par):
                act.wait_ge(m_turned, v + 1)
                nc.scalar.activation(now[par][MROW:128, :, :], ps_m[MROW:128, 0:TP].unsqueeze(1).to_broadcast([128 - MROW, MH, TP]),
                                     ACT.Copy).then_inc(m_ready, 1)

            def copy_sums(v):
                act.wait_ge(pv, (v + 1) * XT)
                act.wait_ge(s_turned, v)
                nc.scalar.activation(sumsT[:, :], ps_o[0:VROWS, 0:TP], ACT.Copy).then_inc(s_copied, 1)

            def copy_out(v):
                act.wait_ge(o_turned, v + 1)
                act.wait_ge(y_mm, v)
                nc.scalar.activation(oT[0:DIM, :], ps_m[0:DIM, 128:128 + TP], ACT.Copy).then_inc(oT_done, 1)

            copy_maxima(0, 0)

            def one(b, u, par, late, own, nxt, loads):
                if late:
                    copy_sums(u - 1)
                for x in range(XT):
                    act.wait_ge(scored, u * XT + x + 1)
                    act.wait_ge(pv, u * XT + max(x - 2, 0))
                    nc.scalar.activation(P[:, x % 3, :].rearrange("p (c n) -> p c n", c=2), psB[(x + par) % 2][0:TP, :, 0:4 * TP],
                                         ACT.Exp).then_inc(exped, 1)
                    if late and x == 3:
                        copy_out(u - 1)
                if nxt is not None:
                    copy_maxima(u + 1, 1 - par)
                if own:
                    copy_sums(u)
                    copy_out(u)
            run(act, one)

        @block.vector
        def _(dve):
            def maxima(v, n):
                j, c = divmod(n, MA)
                dve.wait_ge(a_mm, v * AN + n + 1)
                if n == 0:
                    dve.wait_ge(step, v * M_STEPS)
                nc.vector.tensor_reduce(nm3[:, j, c:c + 1], psA[n % 2][0:TP, 0:HALF], op=ALU.max, axis=AX.X).then_inc(maxed, 1)

            def split_maxima(v):
                st = Steps(dve, step, v * M_STEPS)
                dve.wait_ge(maxed, (v + 1) * AN)
                st.link(nc.vector.tensor_reduce(nm[:, 0, :], nm3[:, :, :], op=ALU.max, axis=AX.X, negate=True))
                part = [mparts[:, MROW + i * MH:MROW + (i + 1) * MH] for i in range(PARTS)]
                dve.wait_ge(m_turned, v)
                st.link(nc.vector.tensor_copy(part[0], nm[:, 0, :]))
                st.link(nc.vector.tensor_tensor(nm[:, 1, :], nm[:, 0, :], part[0], ALU.subtract))
                st.link(nc.vector.tensor_copy(part[1], nm[:, 1, :]))
                st.mark(nc.vector.tensor_tensor(part[2], nm[:, 1, :], part[1], ALU.subtract))
                assert st.n == M_STEPS

            def normalise(v):
                dve.wait_ge(s_turned, v + 1)
                dve.wait_ge(o_done, v)
                sums = ps_m[0:TP, 384:384 + VROWS].rearrange("p (h d) -> p h d", h=MH)
                nc.vector.reciprocal(rs[:, :], sums[:, :, MHD]).then_inc(inv, 1)
                dve.wait_ge(inv, v + 1)
                dve.wait_ge(o_turned, v)
                nc.vector.tensor_tensor(out[:, :, :], sums[:, :, 0:MHD], bc_free(rs[:, :], TP, MHD), ALU.mult).then_inc(o_done, 1)

            def add(v):
                dve.wait_ge(y_mm, v + 1)
                Hu = H[:, bass.ds(v, 1), :].rearrange("p a d -> p (a d)")
                nc.vector.tensor_tensor(Hu, Hu, ps_m[0:TP, 256:256 + DIM], ALU.add).then_inc(added, 1)

            for n in range(AN):
                maxima(0, n)
            split_maxima(0)

            def one(b, u, par, late, own, nxt, loads):
                for x in range(XT - 1):
                    if nxt is not None:
                        for n in range(x * 3, (x + 1) * 3):
                            maxima(u + 1, n)
                    if late and x == 1:
                        normalise(u - 1)
                    if late and x == 4:
                        add(u - 1)
                if nxt is not None:
                    split_maxima(u + 1)
                if own:
                    normalise(u)
                    add(u)
            run(dve, one)
            dve.wait_ge(added, UNITS)


VROWS = MH * (MHD + 1)
VSTEP = VROWS + MHD + 1
M_STEPS = 5
PROJ_STEPS = 4


EDGES = 262144
ECOLS = EDGES // 128
LAST = BATCH * SEQ - 1
LAST_PAD = LAST + BATCH - 1
SENTINEL = -3.0e7
SHIFT = float(2 ** 23)
MAGIC = 12582912.0
SELCOL = 16
GH, GE = 4, 4
GF = GH * GE
MASK_STRIDE = NODES
JUNK = NODES * MASK_STRIDE
NODE_F = 20


def edge_stage(nc, io, ident, maskD, slots, n_rounds, hist):
    src_l, dst_l, u_l, p_l = slots
    with ExitStack() as ctx:
        s = Space(nc, ctx, "edge")
        raw = s.sb("raw", [128, ECOLS], I32)
        sp_ = s.sb("source", [128, ECOLS])
        dp = s.sb("destination", [128, ECOLS])
        a = s.sb("a", [128, ECOLS])
        c = s.sb("c", [128, ECOLS])
        vd = s.sb("valid", [128, ECOLS])
        hu = s.sb("hist_tile", [128, ECOLS])
        hp = s.sb("hist_row", [128, ECOLS])
        key = s.sb("key", [128, ECOLS])
        iota = s.sb("iota", [128, TP])
        iota_p = s.sb("iota_p", [128, 1])
        cnt = s.sb("count", [128, 1])
        cmax = s.sb("count_max", [1, 2])
        neg = s.sb("neg", [TP, MASK_STRIDE], BF16)
        zero = s.sb("zero", [128, 128], BF16)
        oh_p = s.sb("onehot_row", [128, 2, SELCOL, TP], BF16)
        oh_u = s.sb("onehot_tile", [128, 2, SELCOL, UNITS], BF16)
        gate = s.sb("gate", [128, 1])
        pgate = s.sb("gate_pool", [128, 2])
        pgated = s.sem("gated_pool")
        L = s.sb("largest", [128, 8])
        w = [s.sb(f"w{n}", [128, 8]) for n in range(10)]
        oi = s.sb("offset_i", [128, 2, 8], I32)
        off = s.sb("offset", [128, 8], I32)
        ps_h = s.ps("ps_h", (128, 512))
        ps_c = s.ps("ps_c", (128, 512))
        e_in, step, init, iota_done, counted, c_turned, rounds_done = (
            s.sem(n) for n in ("edges_in", "step", "init", "iota_done", "counted", "count_turned", "rounds_done"))
        filled, hot, h_mm, h_done, lstep, off_done, marked, raw_in2 = (
            s.sem(n) for n in ("filled", "onehot", "h_mm", "h_done", "loop_step", "off_done", "marked", "dst_in"))
        ready = s.sem("lists_ready")
        block = ctx.enter_context(nc.Block())
        edges = io["L1_ffn_edge_index"]

        @block.sync
        def _(sp):
            sp.dma_start(raw[:, :], edges[0].rearrange("(p c) -> p c", p=128)).then_inc(e_in, 16)
            sp.wait_ge(init, 1)
            with sp.Fori(0, UNITS) as u:
                sp.dma_start(maskD[bass.ds(u * TP * MASK_STRIDE, TP * MASK_STRIDE), :].rearrange("(p c) a -> p (c a)", p=TP),
                             neg[:, :]).then_inc(filled, 16)
            sp.wait_ge(ready, 1)
            sp.dma_start(raw[:, :], edges[1].rearrange("(p c) -> p c", p=128)).then_inc(raw_in2, 16)

        @block.gpsimd
        def _(pool):
            nc.gpsimd.iota(iota[:, :], pattern=[[1, TP]], base=0, channel_multiplier=0,
                           allow_small_or_imprecise_dtypes=True).then_inc(iota_done, 1)
            nc.gpsimd.iota(iota_p[:, :], pattern=[[1, 1]], base=0, channel_multiplier=1,
                           allow_small_or_imprecise_dtypes=True).then_inc(iota_done, 1)
            nc.gpsimd.memset(pgate[:, :], 0.0).then_inc(iota_done, 1)
            pool.wait_ge(iota_done, 3)
            pool.wait_ge(filled, 16 * UNITS)
            pool.wait_ge(rounds_done, 1)
            n = pool.value_load(n_rounds[0:1, 0:1], min_val=1, max_val=ECOLS // 8)
            with pool.Fori(0, n) as r:
                pool.wait_ge(off_done, r + 1)
                for j in range(8):
                    pool.wait_ge(pgated, r * 8 + j)
                    nc.gpsimd.tensor_tensor(pgate[:, 1:2], pgate[:, 0:1], pgate[:, 0:1], ALU.add).then_inc(pgated, 1)
                    nc.gpsimd.indirect_dma_start(
                        out=maskD, out_offset=bass.IndirectOffsetOnAxis(ap=off[:, j:j + 1], axis=0),
                        in_=zero[:, 0:1], in_offset=None).then_inc(marked, 16)
                    pool.wait_ge(marked, r * 128 + 16 * (j + 1))

        @block.tensor
        def _(pe):
            pe.wait_ge(counted, 1)
            nc.tensor.transpose(ps_c[0:1, 0:128], cnt[:, :], ident[:, :]).then_inc(c_turned, 1)
            pe.wait_ge(init, 2)
            nc.tensor.matmul(ps_h[0:TP, 0:UNITS], zero[:, 0:TP], zero[:, 0:UNITS], start=True, stop=False)
            with pe.Fori(0, ECOLS // SELCOL // 2) as i:
                for k in range(2):
                    pe.wait_ge(hot, i * 4 + 2 * k + 2)
                    for j in range(SELCOL):
                        last = nc.tensor.matmul(ps_h[0:TP, 0:UNITS], oh_p[:, k, j, :], oh_u[:, k, j, :], start=False, stop=False)
                    last.then_inc(h_mm, 1)
            nc.tensor.matmul(ps_h[0:TP, 0:UNITS], zero[:, 0:TP], zero[:, 0:UNITS], start=False, stop=True).then_inc(h_done, 1)

        @block.vector
        def _(dve):
            st = Steps(dve, step)
            V = nc.vector
            V.memset(neg[:, :], FAR).then_inc(init, 1)
            V.memset(zero[:, :], 0.0).then_inc(init, 1)

            def pad_number(dst, a):
                st.link(V.scalar_tensor_tensor(dst[:, :], a[:, :], float(SEQ), a[:, :], ALU.is_ge, ALU.add))
                for b in range(2, BATCH):
                    st.link(V.scalar_tensor_tensor(dst[:, :], a[:, :], float(SEQ * b), dst[:, :], ALU.is_ge, ALU.add))

            def tile_and_row(u, p, d):
                st.link(V.tensor_scalar(u, d, 1.0 / TP, 0.5 / TP - 0.5, ALU.mult, ALU.add))
                st.link(V.tensor_scalar(u, u, MAGIC, MAGIC, ALU.add, ALU.subtract))
                st.link(V.scalar_tensor_tensor(p, u, -float(TP), d, ALU.mult, ALU.add))

            dve.wait_ge(e_in, 16)
            st.link(V.tensor_copy(a[:, :], raw[:, :]))
            dve.wait_ge(step, st.n)
            V.tensor_scalar(a[:, :], a[:, :], float(LAST), None, ALU.min).then_inc(ready, 1)
            dve.wait_ge(ready, 1)
            pad_number(sp_, a)
            dve.wait_ge(raw_in2, 16)
            st.link(V.tensor_copy(c[:, :], raw[:, :]))
            st.link(V.tensor_scalar(vd[:, :], c[:, :], float(LAST + 1), None, ALU.is_lt))
            pad_number(dp, c)
            tile_and_row(hu[:, :], hp[:, :], dp[:, :])
            st.link(V.scalar_tensor_tensor(c[:, :], a[:, :], float(LAST), vd[:, :], ALU.is_equal, ALU.mult))
            st.link(V.scalar_tensor_tensor(hp[:, :], hp[:, :], 1.0, c[:, :], ALU.add, ALU.mult))
            st.link(V.tensor_scalar(hp[:, :], hp[:, :], -1.0, None, ALU.add))
            st.link(V.tensor_tensor(vd[:, :], vd[:, :], c[:, :], ALU.subtract))
            st.link(V.tensor_scalar(a[:, :], sp_[:, :], float(NODES), SHIFT, ALU.mult, ALU.subtract))
            st.link(V.tensor_tensor(a[:, :], a[:, :], dp[:, :], ALU.add))
            st.link(V.tensor_tensor(a[:, :], a[:, :], vd[:, :], ALU.mult))
            st.link(V.tensor_scalar(c[:, :], vd[:, :], -SENTINEL, SENTINEL, ALU.mult, ALU.add))
            st.link(V.tensor_tensor(key[:, :], a[:, :], c[:, :], ALU.add))
            V.tensor_reduce(cnt[:, :], vd[:, :], op=ALU.add, axis=AX.X).then_inc(counted, 1)
            dve.wait_ge(c_turned, 1)
            st.link(V.tensor_reduce(cmax[:, 0:1], ps_c[0:1, 0:128], op=ALU.max, axis=AX.X))
            st.link(V.tensor_scalar(cmax[:, 1:2], cmax[:, 0:1], 1.0 / 8, 7.0 / 8 - 7.0 / 16, ALU.mult, ALU.add))
            st.link(V.tensor_scalar(cmax[:, 1:2], cmax[:, 1:2], MAGIC, MAGIC, ALU.add, ALU.subtract))
            V.tensor_scalar(n_rounds[:, :], cmax[:, 1:2], 1.0, None, ALU.max).then_inc(rounds_done, 1)
            dve.wait_ge(rounds_done, 1)
            dve.wait_ge(iota_done, 2)
            n = dve.value_load(n_rounds[0:1, 0:1], min_val=1, max_val=ECOLS // 8)
            valid, q, rem, t, src, dst, u, p, fo, fs = (x[:, :] for x in w)
            with dve.Fori(0, n) as r:
                st = Steps(dve, lstep, r * LOOP_STEPS)
                col = bass.ds(r * 8, 8)
                st.mark(V.memset(gate[:, :], 0.0))
                st.link(V.max(L[:, :], key[:, :]))
                st.mark(V.memset(gate[:, :], 0.0))
                st.mark(V.match_replace(key[:, :], L[:, :], key[:, :], SENTINEL))
                st.link(V.tensor_scalar(valid, L[:, :], -SHIFT - 1.0, None, ALU.is_gt))
                st.link(V.tensor_scalar(L[:, :], L[:, :], -SHIFT, None, ALU.max))
                st.link(V.tensor_scalar(q, L[:, :], 1.0 / NODES, SHIFT / NODES - 0.5, ALU.mult, ALU.add))
                st.link(V.tensor_scalar(q, q, MAGIC, MAGIC, ALU.add, ALU.subtract))
                st.link(V.tensor_scalar(rem, q, float(NODES), SHIFT, ALU.mult, ALU.subtract))
                st.link(V.tensor_tensor(rem, L[:, :], rem, ALU.subtract))
                st.link(V.tensor_scalar(t, rem, 0.0, None, ALU.is_lt))
                st.link(V.tensor_tensor(q, q, t, ALU.subtract))
                st.link(V.scalar_tensor_tensor(rem, t, float(NODES), rem, ALU.mult, ALU.add))
                st.link(V.tensor_scalar(t, rem, float(NODES), None, ALU.is_ge))
                st.link(V.tensor_tensor(src, q, t, ALU.add))
                st.link(V.scalar_tensor_tensor(dst, t, -float(NODES), rem, ALU.mult, ALU.add))
                st.link(V.tensor_scalar(u, dst, 1.0 / TP, 0.5 / TP - 0.5, ALU.mult, ALU.add))
                st.link(V.tensor_scalar(u, u, MAGIC, MAGIC, ALU.add, ALU.subtract))
                st.link(V.scalar_tensor_tensor(p, u, -float(TP), dst, ALU.mult, ALU.add))
                st.link(V.scalar_tensor_tensor(p, p, 1.0, valid, ALU.add, ALU.mult))
                st.link(V.tensor_scalar(p, p, -1.0, None, ALU.add))
                st.mark(V.tensor_copy(src_l[:, col], src))
                st.mark(V.tensor_copy(dst_l[:, col], dst))
                st.mark(V.tensor_copy(u_l[:, col], u))
                st.mark(V.tensor_copy(p_l[:, col], p))
                st.mark(V.tensor_scalar(fo, dst, float(MASK_STRIDE), -float(JUNK), ALU.mult, ALU.add))
                st.link(V.tensor_scalar(fs, src, iota_p[:, 0:1], None, ALU.subtract))
                st.mark(V.tensor_tensor(fo, fo, valid, ALU.mult))
                st.link(V.tensor_tensor(fs, fs, valid, ALU.mult))
                st.mark(V.tensor_scalar(oi[:, 0, :], fo, float(JUNK), None, ALU.add))
                st.link(V.tensor_scalar(oi[:, 1, :], fs, iota_p[:, 0:1], None, ALU.add))
                dve.wait_ge(marked, r * 128)
                st.mark(V.memset(gate[:, :], 0.0))
                V.tensor_tensor(off[:, :], oi[:, 0, :], oi[:, 1, :], ALU.add).then_inc(off_done, 1)
                dve.wait_ge(off_done, r + 1)
                assert st.n == LOOP_STEPS, st.n
            with dve.Fori(0, ECOLS // SELCOL // 2) as i:
                for k in range(2):
                    dve.wait_ge(h_mm, i * 2)
                    cc = bass.ds((i * 2 + k) * SELCOL, SELCOL)
                    V.tensor_tensor(oh_p[:, k, :, :], hp[:, cc].unsqueeze(2).to_broadcast([128, SELCOL, TP]),
                                    iota[:, :].unsqueeze(1).to_broadcast([128, SELCOL, TP]), ALU.is_equal).then_inc(hot, 1)
                    V.tensor_tensor(oh_u[:, k, :, :], hu[:, cc].unsqueeze(2).to_broadcast([128, SELCOL, UNITS]),
                                    iota[:, 0:UNITS].unsqueeze(1).to_broadcast([128, SELCOL, UNITS]), ALU.is_equal).then_inc(hot, 1)
            dve.wait_ge(h_done, 1)
            V.tensor_copy(hist[:, :], ps_h[0:TP, 0:UNITS]).then_inc(counted, 1)
            dve.wait_ge(counted, 2)


LOOP_STEPS = 32


def graph_stage(nc, io, H, xT, maskD, slots, n_rounds, hist, gates):
    src_l, dst_l, u_l, p_l = slots
    srcD = nc.dram_tensor("scratch_nodes", [NODES, NODE_F], F32).ap()
    dstD = nc.dram_tensor("scratch_dst", [NODES, 2 * GH], F32).ap()
    with ExitStack() as ctx:
        s = Space(nc, ctx, "gat")
        wg = s.sb("w_gat", [DIM, GF])
        was = s.sb("w_src", [DIM, GH])
        wab = s.sb("w_src_wide", [DIM, GH, TP])
        prod = s.sb("prod", [DIM, GF])
        att = [s.sb(f"att{n}", [TP, GF]) for n in ("s", "d")]
        rows = {n: s.sb(n, [TP, GF]) for n in ("b_gat", "ln_gamma", "ln_beta")}
        xb = s.sb("tokens_batch", [AUG, PAD])
        TS = s.sb("node_rows", [TP, UNITS, NODE_F])
        TD = s.sb("dst_rows", [TP, UNITS, 2 * GH])
        big = s.sb("big", [TP, UNITS, GF])
        asb = s.sb("src_score", [TP, GH, NODES])
        mk = s.sb("mask", [TP, 2, NODES], BF16)
        junk = s.sb("junk", [TP, NODES], BF16)
        mx = s.sb("mx", [TP, 2, GH])
        M = s.sb("src_max", [TP, UNITS, GH])
        lastr = s.sb("last_row", [TP, NODE_F])
        lm = s.sb("last_mask", [TP, UNITS])
        z = [s.sb(f"z{n}", [TP, UNITS, GH]) for n in range(3)]
        gate = s.sb("gate", [TP, 1])
        sem = s.sem
        w_in, step, xcp, h_mm, h_cp, as_mm, as_cp, ts_st, last_in, td_st = (
            sem(n) for n in ("w_in", "step", "x_copied", "h_mm", "h_copied", "as_mm", "as_copied", "rows_stored",
                             "last_in", "dst_stored"))
        m_in = [sem(f"mask_in{k}") for k in range(2)]
        mstep, was_done, ts_done, td_done = sem("max_step"), sem("was_done"), sem("rows_done"), sem("dst_done")
        with ExitStack() as inner:
            ps = [inner.enter_context(nc.psum_tensor(f"gat_ps{k}", [128, 512], F32)) for k in range(4)]
            block = inner.enter_context(nc.Block())

            @block.sync
            def _(sp):
                sp.dma_start(wg[:, :], io["L1_ffn_W_gat"]).then_inc(w_in, 16)
                for n, d in (("L1_ffn_att_src", att[0]), ("L1_ffn_att_dst", att[1])):
                    sp.dma_start(d[:, :], io[n].rearrange("h e -> (h e)").unsqueeze(0).to_broadcast([TP, GF])).then_inc(w_in, 16)
                for n, d in rows.items():
                    sp.dma_start(d[:, :], io["L1_ffn_" + n].unsqueeze(0).to_broadcast([TP, GF])).then_inc(w_in, 16)
                sp.wait_ge(ts_done, 1)
                sp.dma_start(srcD.rearrange("(u p) f -> p u f", p=TP), TS[:, :, :]).then_inc(ts_st, 16)
                sp.wait_ge(ts_st, 16)
                sp.dma_start(lastr[:, :], srcD[LAST_PAD:LAST_PAD + 1, :].to_broadcast([TP, NODE_F])).then_inc(last_in, 16)
                for k in range(2):
                    sp.dma_start(mk[:, k, :], maskD[k * TP * MASK_STRIDE:(k + 1) * TP * MASK_STRIDE, :]
                                 .rearrange("(p c) a -> p (c a)", p=TP)).then_inc(m_in[k], 16)
                pairs = maskD[0:JUNK, :].rearrange("(i k p c) a -> i k p (c a)", k=2, p=TP, c=MASK_STRIDE)
                with sp.Fori(1, UNITS // 2) as i:
                    for k in range(2):
                        sp.wait_ge(mstep, (i - 1) * MAX_STEPS + (k + 1) * MAX_STEPS // 2)
                        sp.dma_start(mk[:, k, :], pairs[bass.ds(i, 1), k].rearrange("i p c -> (i p) c")).then_inc(m_in[k], 16)
                sp.wait_ge(td_done, 1)
                sp.dma_start(dstD.rearrange("(u p) f -> p u f", p=TP), TD[:, :, :]).then_inc(td_st, 16)
                sp.wait_ge(td_st, 16)

            @block.gpsimd
            def _(pool):
                with pool.Fori(0, BATCH) as b:
                    pool.wait_ge(as_mm, b * 12)
                    nc.gpsimd.tensor_copy(xb[:, :], xT[:, bass.ds(b, 1), :].rearrange("p a n -> p (a n)")).then_inc(xcp, 1)

            @block.tensor
            def _(pe):
                pe.wait_ge(w_in, 16 * 6)
                with pe.Fori(0, BATCH) as b:
                    pe.wait_ge(h_cp, b)
                    pe.wait_ge(xcp, b + 1)
                    for t in range(TILES):
                        last = nc.tensor.matmul(ps[0][0:TP, t * GF:(t + 1) * GF], xb[0:DIM, t * TP:(t + 1) * TP], wg[:, :],
                                                start=True, stop=True)
                    last.then_inc(h_mm, 1)
                    pe.wait_ge(was_done, 1)
                    for h in range(GH):
                        for c in range(3):
                            n = h * 3 + c
                            pe.wait_ge(as_cp, b * 12 + max(n - 1, 0))
                            nc.tensor.matmul(ps[2 + n % 2][0:TP, 0:HALF], wab[:, h, :], xb[0:DIM, c * HALF:(c + 1) * HALF],
                                             start=True, stop=True).then_inc(as_mm, 1)

            @block.scalar
            def _(act):
                with act.Fori(0, BATCH) as b:
                    act.wait_ge(h_mm, b + 1)
                    nc.scalar.activation(TS[:, bass.ds(b * TILES, TILES), 0:GF],
                                         ps[0][0:TP, 0:TILES * GF].rearrange("p (t f) -> p t f", t=TILES), ACT.Copy).then_inc(h_cp, 1)
                    for n in range(12):
                        act.wait_ge(as_mm, b * 12 + n + 1)
                        nc.scalar.activation(asb[:, n // 3, bass.ds(b * PAD + n % 3 * HALF, HALF)], ps[2 + n % 2][0:TP, 0:HALF],
                                             ACT.Copy).then_inc(as_cp, 1)

            @block.vector
            def _(dve):
                st = Steps(dve, step)
                V = nc.vector
                dve.wait_ge(w_in, 16 * 6)
                st.link(V.tensor_tensor(prod[:, :], wg[:, :], att[0][0:DIM, :], ALU.mult))
                st.link(V.tensor_reduce(was[:, :], prod[:, :].rearrange("p (h e) -> p h e", h=GH), op=ALU.add, axis=AX.X))
                V.tensor_copy(wab[:, :, :], bc_free(was[:, :], DIM, TP)).then_inc(was_done, 1)
                dve.wait_ge(h_cp, BATCH)
                hview = TS[:, :, 0:GF]
                for n, dst in ((0, TS[:, :, GF:NODE_F]), (1, TD[:, :, 0:GH])):
                    st.link(V.tensor_tensor(big[:, :, :], hview, att[n][:, :].unsqueeze(1).to_broadcast([TP, UNITS, GF]), ALU.mult))
                    ins = V.tensor_reduce(dst, big[:, :, :].rearrange("p u (h e) -> p u h e", h=GH), op=ALU.add, axis=AX.X)
                    st.link(ins) if n else ins.then_inc(ts_done, 1)
                    dve.wait_ge(ts_done, 1)
                dve.wait_ge(as_cp, BATCH * 12)
                with dve.Fori(0, UNITS // 2) as i:
                    mt = Steps(dve, mstep, i * MAX_STEPS)
                    for k in range(2):
                        dve.wait_ge(m_in[k], i * 16 + 16)
                        mt.mark(V.memset(gate[:, :], 0.0))
                        for h in range(GH):
                            mt.mark(V.tensor_tensor_reduce(out=junk[:, :], in0=mk[:, k, :], in1=asb[:, h, :], scale=1.0,
                                                           scalar=FAR, op0=ALU.add, op1=ALU.max, accum_out=mx[:, k, h:h + 1]))
                            if h < GH - 1:
                                mt.settle()
                                mt.mark(V.memset(gate[:, :], 0.0))
                        mt.settle()
                        mt.mark(V.tensor_copy(M[:, bass.ds(i * 2 + k, 1), :].rearrange("p a h -> p (a h)"), mx[:, k, :]))
                    assert mt.n == MAX_STEPS, mt.n
                dve.wait_ge(mstep, (UNITS // 2) * MAX_STEPS)
                dve.wait_ge(last_in, 16)
                asrc, adst = TS[:, :, GF:NODE_F], TD[:, :, 0:GH]
                st.link(V.tensor_tensor(M[:, :, :], M[:, :, :], asrc, ALU.max))
                st.link(V.tensor_scalar(lm[:, :], hist[:, :], 0.0, None, ALU.is_gt))
                st.link(V.tensor_scalar(lm[:, :], lm[:, :], -FAR, FAR, ALU.mult, ALU.add))
                for h in range(GH):
                    st.link(V.scalar_tensor_tensor(M[:, :, h], lm[:, :], lastr[:, GF + h:GF + h + 1], M[:, :, h], ALU.add, ALU.max))
                st.link(V.tensor_tensor(z[0][:, :, :], M[:, :, :], adst, ALU.add))
                V.scalar_tensor_tensor(TD[:, :, GH:2 * GH], z[0][:, :, :], 0.2, z[0][:, :, :], ALU.mult, ALU.max).then_inc(td_done, 1)
                dve.wait_ge(td_done, 1)

        pgate = s.sb("gate_pool", [128, 2])
        pgated = s.sem("gated_pool")
        gs = s.sb("src_gathered", [128, 2, 8, NODE_F])
        gd = s.sb("dst_gathered", [128, 2, 8, 2 * GH])
        ix = s.sb("indices", [128, 2, 8], I32)
        iota = s.sb("iota", [128, TP])
        zf = s.sb("zeros", [128, 512])
        sc = s.sb("edge_score", [128, 8, GH])
        sl = s.sb("edge_leaky", [128, 8, GH])
        we = s.sb("edge_weight", [128, 8, GH])
        msg = s.sb("message", [128, 8, NODE_F])
        up = s.sb("tile_row", [128, 2, 8])
        oh_p = s.sb("onehot_row", [128, 8, TP])
        oh_u = s.sb("onehot_tile", [128, 8, UNITS])
        om = s.sb("tile_message", [128, 8, UNITS * NODE_F])
        acc = s.sb("sums", [TP, UNITS, NODE_F])
        estep, init, iota_done, idx_done, gathered, shifted, exped, spread, sc_mm, opened, fin = (
            sem(n) for n in ("edge_step", "init2", "iota_done", "idx_done", "gathered", "shifted", "exped", "spread",
                             "sc_mm", "opened", "finished"))
        g_s = [sem(f"g_src{j}") for j in range(8)]
        g_d = [sem(f"g_dst{j}") for j in range(8)]
        w_e, w_ed, fstep, f_sqrt, f_root = sem("w_arg"), sem("w_exped"), sem("fstep"), sem("f_var"), sem("f_root")
        g_arg, g_exp = sem("g_arg"), sem("g_exp")
        ps_a, ps_b = s.ps("acc_a", (128, 512)), s.ps("acc_b", (128, 512))
        HU = UNITS // 2 * NODE_F
        ws, wl = s.sb("w_self", [TP, UNITS, GH]), s.sb("w_last", [TP, UNITS, GH])
        stat, root = s.sb("stat", [TP, UNITS]), s.sb("root", [TP, UNITS])
        scr = s.sb("scores", [TP, GE, UNITS])
        ge = s.sb("gate_exp", [TP, GE, UNITS])
        rank, cmp_ = s.sb("rank", [TP, GE, UNITS]), s.sb("cmp", [TP, UNITS])
        top = s.sb("top_score", [TP, UNITS])
        block = ctx.enter_context(nc.Block())

        @block.gpsimd
        def _(pool):
            nc.gpsimd.iota(iota[:, :], pattern=[[1, TP]], base=0, channel_multiplier=0,
                           allow_small_or_imprecise_dtypes=True).then_inc(iota_done, 1)
            nc.gpsimd.memset(pgate[:, :], 0.0).then_inc(iota_done, 1)
            pool.wait_ge(iota_done, 2)
            n = pool.value_load(n_rounds[0:1, 0:1], min_val=1, max_val=ECOLS // 8)
            with pool.Fori(0, n) as r:
                pool.wait_ge(idx_done, r * 4 + 2)
                pool.wait_ge(pgated, r)
                nc.gpsimd.tensor_tensor(pgate[:, 1:2], pgate[:, 0:1], pgate[:, 0:1], ALU.add).then_inc(pgated, 1)
                for j in range(8):
                    nc.gpsimd.indirect_dma_start(out=gs[:, 0, j, :], out_offset=None, in_=srcD,
                                                 in_offset=bass.IndirectOffsetOnAxis(ap=ix[:, 0, j:j + 1], axis=0)).then_inc(g_s[j], 16)
                    nc.gpsimd.indirect_dma_start(out=gd[:, 0, j, :], out_offset=None, in_=dstD,
                                                 in_offset=bass.IndirectOffsetOnAxis(ap=ix[:, 1, j:j + 1], axis=0)).then_inc(g_d[j], 16)

        @block.scalar
        def _(act):
            n = act.value_load(n_rounds[0:1, 0:1], min_val=1, max_val=ECOLS // 8)
            with act.Fori(0, n) as r:
                act.wait_ge(shifted, r + 1)
                act.wait_ge(spread, r)
                nc.scalar.activation(we[:, :, :], sl[:, :, :], ACT.Exp).then_inc(exped, 1)
            act.wait_ge(w_e, 2)
            nc.scalar.activation(ws[:, :, :], z[1][:, :, :], ACT.Exp).then_inc(w_ed, 1)
            nc.scalar.activation(wl[:, :, :], z[2][:, :, :], ACT.Exp).then_inc(w_ed, 1)
            act.wait_ge(f_sqrt, 1)
            nc.scalar.activation(root[:, :], stat[:, :], ACT.Sqrt).then_inc(f_root, 1)
            act.wait_ge(g_arg, 1)
            nc.scalar.activation(ge[:, :, :], scr[:, :, :], ACT.Exp).then_inc(g_exp, 1)

        @block.tensor
        def _(pe):
            pe.wait_ge(init, 1)
            nc.tensor.matmul(ps_a[0:TP, 0:HU], zf[:, 0:TP], zf[:, 0:HU], start=True, stop=False)
            nc.tensor.matmul(ps_b[0:TP, 0:HU], zf[:, 0:TP], zf[:, 0:HU], start=True, stop=False)
            n = pe.value_load(n_rounds[0:1, 0:1], min_val=1, max_val=ECOLS // 8)
            with pe.Fori(0, n) as r:
                pe.wait_ge(spread, r + 1)
                for j in range(8):
                    nc.tensor.matmul(ps_a[0:TP, 0:HU], oh_p[:, j, :], om[:, j, 0:HU], start=False, stop=False)
                    last = nc.tensor.matmul(ps_b[0:TP, 0:HU], oh_p[:, j, :], om[:, j, HU:2 * HU], start=False, stop=False)
                last.then_inc(sc_mm, 1)
            nc.tensor.matmul(ps_a[0:TP, 0:HU], zf[:, 0:TP], zf[:, 0:HU], start=False, stop=True)
            nc.tensor.matmul(ps_b[0:TP, 0:HU], zf[:, 0:TP], zf[:, 0:HU], start=False, stop=True).then_inc(opened, 1)

        @block.vector
        def _(dve):
            V = nc.vector
            V.memset(zf[:, :], 0.0).then_inc(init, 1)
            dve.wait_ge(iota_done, 1)
            n = dve.value_load(n_rounds[0:1, 0:1], min_val=1, max_val=ECOLS // 8)
            with dve.Fori(0, n) as r:
                col = bass.ds(r * 8, 8)
                st = Steps(dve, estep, r * EDGE_STEPS)
                V.tensor_copy(ix[:, 0, :], src_l[:, col]).then_inc(idx_done, 1)
                V.tensor_copy(ix[:, 1, :], dst_l[:, col]).then_inc(idx_done, 1)
                V.tensor_copy(up[:, 0, :], u_l[:, col]).then_inc(idx_done, 1)
                V.tensor_copy(up[:, 1, :], p_l[:, col]).then_inc(idx_done, 1)
                dve.wait_ge(idx_done, r * 4 + 4)
                dve.wait_ge(sc_mm, r)
                st.mark(V.tensor_tensor(oh_p[:, :, :], up[:, 1, :].unsqueeze(2).to_broadcast([128, 8, TP]),
                                        iota[:, :].unsqueeze(1).to_broadcast([128, 8, TP]), ALU.is_equal))
                st.link(V.tensor_tensor(oh_u[:, :, :], up[:, 0, :].unsqueeze(2).to_broadcast([128, 8, UNITS]),
                                        iota[:, 0:UNITS].unsqueeze(1).to_broadcast([128, 8, UNITS]), ALU.is_equal))
                for j in range(8):
                    dve.wait_ge(g_s[j], r * 16 + 16)
                    dve.wait_ge(g_d[j], r * 16 + 16)
                st.link(V.tensor_tensor(sc[:, :, :], gs[:, 0, :, GF:NODE_F], gd[:, 0, :, 0:GH], ALU.add))
                st.link(V.scalar_tensor_tensor(sl[:, :, :], sc[:, :, :], 0.2, sc[:, :, :], ALU.mult, ALU.max))
                V.tensor_tensor(sl[:, :, :], sl[:, :, :], gd[:, 0, :, GH:2 * GH], ALU.subtract).then_inc(shifted, 1)
                dve.wait_ge(exped, r + 1)
                st.mark(V.tensor_tensor(msg[:, :, 0:GF].rearrange("p j (h e) -> p j h e", h=GH),
                                        gs[:, 0, :, 0:GF].rearrange("p j (h e) -> p j h e", h=GH),
                                        we[:, :, :].unsqueeze(3).to_broadcast([128, 8, GH, GE]), ALU.mult))
                st.link(V.tensor_copy(msg[:, :, GF:NODE_F], we[:, :, :]))
                for j in range(8):
                    ins = V.tensor_tensor(om[:, j, :].rearrange("p (u f) -> p u f", u=UNITS), bc_free(oh_u[:, j, :], 128, NODE_F),
                                          msg[:, j, :].unsqueeze(1).to_broadcast([128, UNITS, NODE_F]), ALU.mult)
                    st.mark(ins) if j < 7 else ins.then_inc(spread, 1)
                dve.wait_ge(spread, r + 1)
                st.settle()
                assert st.n == EDGE_STEPS, st.n
            st = Steps(dve, fstep)
            asrc, adst, m = TS[:, :, GF:NODE_F], TD[:, :, 0:GH], TD[:, :, GH:2 * GH]
            st.link(V.tensor_tensor(z[0][:, :, :], asrc, adst, ALU.add))
            st.link(V.scalar_tensor_tensor(z[1][:, :, :], z[0][:, :, :], 0.2, z[0][:, :, :], ALU.mult, ALU.max))
            V.tensor_tensor(z[1][:, :, :], z[1][:, :, :], m, ALU.subtract).then_inc(w_e, 1)
            st.link(V.tensor_tensor(z[0][:, :, :], adst, lastr[:, GF:NODE_F].unsqueeze(1).to_broadcast([TP, UNITS, GH]), ALU.add))
            st.link(V.scalar_tensor_tensor(z[2][:, :, :], z[0][:, :, :], 0.2, z[0][:, :, :], ALU.mult, ALU.max))
            st.link(V.tensor_tensor(z[2][:, :, :], z[2][:, :, :], m, ALU.subtract))
            V.tensor_scalar(z[2][:, :, :], z[2][:, :, :], 0.0, None, ALU.min).then_inc(w_e, 1)
            dve.wait_ge(w_ed, 2)
            st.link(V.tensor_tensor(wl[:, :, :], wl[:, :, :], bc_free(hist[:, :], TP, GH), ALU.mult))
            dve.wait_ge(opened, 1)
            st.mark(V.tensor_copy(acc[:, 0:UNITS // 2, :].rearrange("p u f -> p (u f)"), ps_a[0:TP, 0:HU]))
            st.link(V.tensor_copy(acc[:, UNITS // 2:UNITS, :].rearrange("p u f -> p (u f)"), ps_b[0:TP, 0:HU]))
            num, den = acc[:, :, 0:GF], acc[:, :, GF:NODE_F]
            four = lambda ap: ap.rearrange("p u (h e) -> p u h e", h=GH)
            hrow = lastr[:, 0:GF].unsqueeze(1).to_broadcast([TP, UNITS, GF])
            st.link(V.tensor_tensor(den, den, ws[:, :, :], ALU.add))
            st.link(V.tensor_tensor(den, den, wl[:, :, :], ALU.add))
            for h in range(GH):
                hs = slice(h * GE, (h + 1) * GE)
                st.link(V.tensor_tensor(big[:, :, hs], TS[:, :, hs], bc_free(ws[:, :, h], TP, GE), ALU.mult))
            st.link(V.tensor_tensor(num, num, big[:, :, :], ALU.add))
            for h in range(GH):
                hs = slice(h * GE, (h + 1) * GE)
                st.link(V.tensor_tensor(big[:, :, hs], hrow[:, :, hs], bc_free(wl[:, :, h], TP, GE), ALU.mult))
            st.link(V.tensor_tensor(num, num, big[:, :, :], ALU.add))
            st.link(V.tensor_scalar(z[0][:, :, :], den, 1e-16, None, ALU.add))
            st.link(V.reciprocal(z[1][:, :, :], z[0][:, :, :]))
            for h in range(GH):
                hs = slice(h * GE, (h + 1) * GE)
                st.link(V.tensor_tensor(big[:, :, hs], acc[:, :, hs], bc_free(z[1][:, :, h], TP, GE), ALU.mult))

            def row(n):
                return rows[n][:, :].unsqueeze(1).to_broadcast([TP, UNITS, GF])

            st.link(V.tensor_tensor(big[:, :, :], big[:, :, :], row("b_gat"), ALU.add))
            st.link(V.tensor_reduce(stat[:, :], big[:, :, :], op=ALU.add, axis=AX.X))
            st.link(V.tensor_scalar(stat[:, :], stat[:, :], 1.0 / GF, None, ALU.mult))
            st.link(V.tensor_tensor(big[:, :, :], big[:, :, :], bc_free(stat[:, :], TP, GF), ALU.subtract))
            st.link(V.tensor_tensor(num, big[:, :, :], big[:, :, :], ALU.mult))
            st.link(V.tensor_reduce(stat[:, :], num, op=ALU.add, axis=AX.X))
            V.tensor_scalar(stat[:, :], stat[:, :], 1.0 / GF, EPS, ALU.mult, ALU.add).then_inc(f_sqrt, 1)
            dve.wait_ge(f_root, 1)
            st.link(V.reciprocal(stat[:, :], root[:, :]))
            st.link(V.tensor_tensor(big[:, :, :], big[:, :, :], bc_free(stat[:, :], TP, GF), ALU.mult))
            st.link(V.tensor_tensor(big[:, :, :], big[:, :, :], row("ln_gamma"), ALU.mult))
            st.link(V.tensor_tensor(big[:, :, :], big[:, :, :], row("ln_beta"), ALU.add))
            for e in range(GE):
                st.mark(V.tensor_reduce(scr[:, e, :], big[:, :, e:GF:GE], op=ALU.add, axis=AX.X))
            st.settle()
            st.link(V.tensor_scalar(scr[:, :, :], scr[:, :, :], 1.0 / GH, None, ALU.mult))
            st.link(V.memset(rank[:, :, :], 0.0))
            for e in range(GE):
                for o in range(GE):
                    if o != e:
                        st.link(V.tensor_tensor(cmp_[:, :], scr[:, o, :], scr[:, e, :], ALU.is_ge if o < e else ALU.is_gt))
                        st.link(V.tensor_tensor(rank[:, e, :], rank[:, e, :], cmp_[:, :], ALU.add))
            st.link(V.tensor_tensor(top[:, :], scr[:, 0, :], scr[:, 1, :], ALU.max))
            for e in (2, 3):
                st.link(V.tensor_tensor(top[:, :], top[:, :], scr[:, e, :], ALU.max))
            V.tensor_tensor(scr[:, :, :], scr[:, :, :], top[:, :].unsqueeze(1).to_broadcast([TP, GE, UNITS]),
                            ALU.subtract).then_inc(g_arg, 1)
            dve.wait_ge(g_exp, 1)
            st.link(V.scalar_tensor_tensor(ge[:, :, :], rank[:, :, :], 2.0, ge[:, :, :], ALU.is_lt, ALU.mult))
            st.link(V.tensor_tensor(top[:, :], ge[:, 0, :], ge[:, 1, :], ALU.add))
            for e in (2, 3):
                st.link(V.tensor_tensor(top[:, :], top[:, :], ge[:, e, :], ALU.add))
            st.link(V.reciprocal(cmp_[:, :], top[:, :]))
            st.link(V.tensor_tensor(gates[:, :, :], ge[:, :, :], cmp_[:, :].unsqueeze(1).to_broadcast([TP, GE, UNITS]), ALU.mult))


MAX_STEPS = 2 * (1 + GH + GH - 1 + 1)
EDGE_STEPS = 2 + 2 + 2 + 7


def expert_stage(nc, io, H, xT, gates, out):
    HID = 2 * DIM
    with ExitStack() as ctx:
        s = Space(nc, ctx, "ffn")
        w1 = s.sb("w1", [AUG, GE, HID])
        w2 = s.sb("w2", [HID, GE, DIM])
        b2 = s.sb("b2", [1, GE, DIM])
        one = s.sb("one", [1, TP])
        xb = s.sb("tokens_batch", [AUG, PAD])
        hh = s.sb("hidden", [HID, 2, PAD])
        acc = s.sb("sum", [TP, TILES, DIM])
        tmp = s.sb("gated", [TP, TILES, DIM])
        ps_u = s.ps("up", (128, 3, 512))
        ps_d = [s.ps(f"down{k}", (128, 1024)) for k in range(2)]
        w_in, init, xcp, up, act_done, down, gated, summed, st_a, started = (
            s.sem(n) for n in ("w_in", "init", "x_copied", "up", "act_done", "down", "gated", "summed", "stored", "started"))
        block = ctx.enter_context(nc.Block())

        @block.sync
        def _(sp):
            sp.dma_start(w1[0:DIM, :, :], io["L1_ffn_W1"].rearrange("e c f -> c e f")).then_inc(w_in, 16)
            sp.dma_start(w1[DIM:AUG, :, :], io["L1_ffn_b1"].unsqueeze(0)).then_inc(w_in, 16)
            sp.dma_start(w2[:, :, :], io["L1_ffn_W2"].rearrange("e c f -> c e f")).then_inc(w_in, 16)
            sp.dma_start(b2[:, :, :], io["L1_ffn_b2"].unsqueeze(0)).then_inc(w_in, 16)
            with sp.Fori(0, BATCH) as b:
                sp.wait_ge(st_a, b * 16)
                sp.wait_ge(started, b * 16)
                sp.wait_ge(summed, (b + 1) * (GE + 1))
                ob = out[bass.ds(b, 1)].rearrange("a n d -> (a n) d")
                sp.dma_start(ob[0:8 * TP, :].rearrange("(t p) d -> p t d", p=TP), acc[:, 0:8, :]).then_inc(st_a, 16)
                sp.dma_start(ob[8 * TP:SEQ, :], acc[0:TP - 1, 8, :]).then_inc(started, 16)
            sp.wait_ge(st_a, BATCH * 16)
            sp.wait_ge(started, BATCH * 16)

        @block.gpsimd
        def _(pool):
            with pool.Fori(0, BATCH) as b:
                pool.wait_ge(up, b * GE)
                nc.gpsimd.tensor_copy(xb[:, :], xT[:, bass.ds(b, 1), :].rearrange("p a n -> p (a n)")).then_inc(xcp, 1)

        @block.tensor
        def _(pe):
            pe.wait_ge(w_in, 64)
            pe.wait_ge(init, 1)
            with pe.Fori(0, BATCH) as b:
                pe.wait_ge(xcp, b + 1)

                def go_up(e):
                    n = b * GE + e
                    pe.wait_ge(act_done, n)
                    for c in range(3):
                        last = nc.tensor.matmul(ps_u[:, c, 0:HALF], w1[:, e, :], xb[:, c * HALF:(c + 1) * HALF], start=True, stop=True)
                    last.then_inc(up, 1)

                def go_down(e):
                    n = b * GE + e
                    pe.wait_ge(act_done, n + 1)
                    if e >= 2:
                        pe.wait_ge(gated, n - 1)
                    else:
                        pe.wait_ge(gated, b * GE)
                    for t in range(TILES):
                        dst = ps_d[e % 2][0:TP, t * DIM:(t + 1) * DIM]
                        nc.tensor.matmul(dst, hh[:, e % 2, t * TP:(t + 1) * TP], w2[:, e, :], start=True, stop=False)
                        last = nc.tensor.matmul(dst, one[:, :], b2[:, e, :], start=False, stop=True)
                    last.then_inc(down, 1)

                go_up(0)
                for e in range(GE):
                    if e + 1 < GE:
                        go_up(e + 1)
                    go_down(e)

        @block.scalar
        def _(act):
            with act.Fori(0, BATCH) as b:
                for e in range(GE):
                    n = b * GE + e
                    act.wait_ge(up, n + 1)
                    act.wait_ge(down, n - 1 if e >= 2 else b * GE)
                    nc.scalar.activation(hh[:, e % 2, :].rearrange("p (c n) -> p c n", c=3), ps_u[:, :, 0:HALF],
                                         ACT.Gelu).then_inc(act_done, 1)

        @block.vector
        def _(dve):
            nc.vector.memset(one[:, :], 1.0).then_inc(init, 1)
            with dve.Fori(0, BATCH) as b:
                s0 = b * (GE + 1)
                dve.wait_ge(st_a, b * 16)
                dve.wait_ge(started, b * 16)
                nc.vector.tensor_copy(acc[:, :, :], H[:, bass.ds(b * TILES, TILES), :]).then_inc(summed, 1)
                for e in range(GE):
                    n = b * GE + e
                    dve.wait_ge(down, n + 1)
                    dve.wait_ge(summed, s0 + e + 1)
                    nc.vector.tensor_tensor(tmp[:, :, :], ps_d[e % 2][0:TP, 0:TILES * DIM].rearrange("p (t d) -> p t d", t=TILES),
                                            gates[:, e, bass.ds(b * TILES, TILES)].unsqueeze(2).to_broadcast([TP, TILES, DIM]),
                                            ALU.mult).then_inc(gated, 1)
                    dve.wait_ge(gated, n + 1)
                    nc.vector.tensor_tensor(acc[:, :, :], acc[:, :, :], tmp[:, :, :], ALU.add).then_inc(summed, 1)


def lay_out(inputs):
    arrays = {n: np.ascontiguousarray(a) for n, a in inputs.items()}
    arrays["L0_tok_gammaT"] = np.ascontiguousarray(arrays.pop("L0_tok_d_gamma_batched").T)
    arrays["L0_ffn_Wq_pkT"] = np.ascontiguousarray(arrays.pop("L0_ffn_Wq_pk").T)
    arrays["L0_ffn_pk_keysT"] = np.ascontiguousarray(arrays.pop("L0_ffn_pk_keys").transpose(0, 2, 3, 1))
    arrays["L0_ffn_tables"] = np.concatenate([arrays.pop("L0_ffn_keys_table"), arrays.pop("L0_ffn_values_table")], axis=1)
    for n in "qkvo":
        arrays[f"L1_attn_W{n}T"] = np.ascontiguousarray(arrays.pop(f"L1_attn_W{n}").T)
    for n in "qk":
        w, b = arrays[f"L1_attn_W{n}T"], arrays[f"L1_attn_b{n}"]
        arrays[f"L1_attn_W{n}T"] = np.ascontiguousarray(w.reshape(DIM, MH, MHD).transpose(0, 2, 1).reshape(DIM, DIM))
        arrays[f"L1_attn_b{n}"] = np.ascontiguousarray(b.reshape(MH, MHD).T.reshape(DIM))
    arrays["L0_tok_prelu_a"] = arrays["L0_tok_prelu_a"].reshape(1, 1)
    return arrays


def window_layer(nc, io, H, xT, ident):
    norm_stage(nc, "norm_win", H, xT, ident)
    window_stage(nc, io, H, xT, ident)


def memory_layer(nc, io, H, xT, ident):
    norm_stage(nc, "norm_mem", H, xT, ident)
    kTD = nc.dram_tensor("scratch_mem_keys", [PH, DIM, NODES], F32).ap()
    vD = nc.dram_tensor("scratch_mem_values", [PH, UNITS, TP, DIM], F32).ap()
    e01D = nc.dram_tensor("scratch_e01", [UNITS, TP, GROUPS * PK], F32).ap()
    with nc.sbuf_tensor("theta", [TP, UNITS, PH], F32) as theta, nc.sbuf_tensor("inv_z", [TP, UNITS, PH], F32) as inv_z:
        select_stage(nc, io, xT, e01D, theta, inv_z)
        memory_stage(nc, io, e01D, theta, inv_z, ident, kTD, vD)
    recall_stage(nc, io, H, xT, ident, kTD, vD)


def heads_layer(nc, io, H, xT, ident):
    norm_stage(nc, "norm_mha", H, xT, ident)
    heads_stage(nc, io, H, xT, ident)


def expert_layer(nc, io, H, xT, ident, out):
    norm_stage(nc, "norm_gat", H, xT, ident)
    maskD = nc.dram_tensor("scratch_mask", [JUNK + 128, 1], BF16).ap()
    with ExitStack() as ctx:
        s = Space(nc, ctx, "moe")
        slots = (s.sb("slot_src", [128, ECOLS], I32), s.sb("slot_dst", [128, ECOLS], I32),
                 s.sb("slot_tile", [128, ECOLS]), s.sb("slot_row", [128, ECOLS]))
        n_rounds, clipped = s.sb("n_rounds", [1, 1], I32), s.sb("clipped_count", [TP, UNITS])
        gates = s.sb("gates", [TP, GE, UNITS])
        edge_stage(nc, io, ident, maskD, slots, n_rounds, clipped)
        graph_stage(nc, io, H, xT, maskD, slots, n_rounds, clipped, gates)
        expert_stage(nc, io, H, xT, gates, out)


def program(nc, io, out):
    with ExitStack() as ctx:
        H = ctx.enter_context(nc.sbuf_tensor("hidden", [TP, UNITS, DIM], F32))
        ident = ctx.enter_context(nc.sbuf_tensor("identity", [128, 128], F32))
        ones = ctx.enter_context(nc.sbuf_tensor("ones", [1, 128], F32))
        constants_stage(nc, ident, ones)
        tok_stage(nc, io, H, ident)
        xT = ctx.enter_context(nc.sbuf_tensor("normedT", [AUG, BATCH, PAD], F32))
        window_layer(nc, io, H, xT, ident)
        memory_layer(nc, io, H, xT, ident)
        heads_layer(nc, io, H, xT, ident)
        expert_layer(nc, io, H, xT, ident, out)


def kernel(**inputs):
    import concourse.bacc as bacc
    from concourse.bass_utils import run_bass_kernel_spmd

    nc = bacc.Bacc("TRN2", target_bir_lowering=False, num_devices=1)
    arrays, io = {}, {}
    for name, a in lay_out(inputs).items():
        arrays[f"in_{name}_dram"] = a
        io[name] = nc.dram_tensor(f"in_{name}_dram", a.shape, mybir.dt.from_np(a.dtype), kind="ExternalInput").ap()
    out = nc.dram_tensor("out_0_dram", (BATCH, SEQ, DIM), F32, kind="ExternalOutput").ap()
    program(nc, io, out)
    r = run_bass_kernel_spmd(nc, [arrays], core_ids=[0])
    return r.results[0]["out_0_dram"]
```
